# Optimizing a Trainium2 kernel written in Bass

```python
import numpy as np
import jax
import jax.numpy as jnp

def _softmax(x, axis=-1):
    return jax.nn.softmax(x, axis=axis)

def _gelu(x):
    return jax.nn.gelu(x, approximate=True)

def _silu(x):
    return jax.nn.silu(x)

def _sigmoid(x):
    return jax.nn.sigmoid(x)

def _layernorm(x, axis=-1, eps=1e-05):
    m = jnp.mean(x, axis=axis, keepdims=True)
    v = jnp.var(x, axis=axis, keepdims=True)
    return (x - m) / jnp.sqrt(v + eps)

def _scatter_add(tgt, idx, src, axis=0):
    return tgt.at[idx].add(src)

def _segment_sum(src, seg, n):
    return jax.ops.segment_sum(src, seg, n)
kernel_name = 'mk_flamingo_gated_d4_seqx_r8_c00205'

def setup_inputs(seed: int=0):
    np.random.seed(seed)
    _w = jnp.asarray

    def _rec_inputs():
        import jax
        import jax.numpy as jnp
        _rk = jax.random.key(seed)
        x = -0.0003929 + 0.9999 * jax.random.normal(jax.random.fold_in(_rk, 1), (16, 128, 128), jnp.float32)
        _lenS = 128 - jax.random.randint(jax.random.fold_in(_rk, 7), (16,), 0, max(1, 128 // 4) + 1, jnp.int32)
        _lenS2 = 128 - jax.random.randint(jax.random.fold_in(_rk, 8), (16,), 0, max(1, 128 // 4) + 1, jnp.int32)
        _ctx_1024P = jax.random.normal(jax.random.fold_in(_rk, 11), (16, 16, 128), jnp.float32)
        _ctx_1024c = jax.random.dirichlet(jax.random.fold_in(_rk, 511), 0.3 * jnp.ones((16,), jnp.float32), (16, 128))
        _ctx_1024t = jnp.einsum('bsk,bkd->bsd', _ctx_1024c, _ctx_1024P)
        _ctx_1024t = _ctx_1024t * jax.lax.rsqrt(jnp.mean(jnp.square(_ctx_1024t)) + 1e-12) * 0.953939
        ctx_1024 = 2.81802e-05 + 1.00001 * (_ctx_1024t + 0.3 * jax.random.normal(jax.random.fold_in(_rk, 611), (16, 128, 128), jnp.float32))
        _validS = jnp.arange(128)[None, :] < _lenS[:, None]
        _validS2 = jnp.arange(128)[None, :] < _lenS2[:, None]
        _causal = jnp.tril(jnp.ones((128, 128), dtype=bool))
        mask_BxSxS2_ff1 = jnp.where(jnp.ones((16, 128, 128), dtype=bool), 1.0, 0.0).astype(jnp.float32)
        mask_BxS2_ff1 = jnp.where(jnp.ones((16, 128), dtype=bool), 1.0, 0.0).astype(jnp.float32)
        mask_1x1xSxS2_if1 = jnp.where(jnp.ones((1, 1, 128, 128), dtype=bool), 1, 0).astype(jnp.int32)
        _g = jax.random.normal(jax.random.fold_in(_rk, 9001), (2, 4), jnp.float32)
        _g = jnp.sign(_g) * jnp.maximum(jnp.abs(_g), 1.0) + (_g == 0) * 1.0
        g_xattn = _g[0]
        g_ffn = _g[1]
        return (x, ctx_1024, mask_BxSxS2_ff1, mask_BxS2_ff1, mask_1x1xSxS2_if1, g_xattn, g_ffn)
    x, ctx_1024, mask_BxSxS2_ff1, mask_BxS2_ff1, mask_1x1xSxS2_if1, g_xattn, g_ffn = _rec_inputs()

    def _L0_xattn_setup():
        import jax, jax.numpy as jnp
        import numpy as np
        key = jax.random.key(seed)
        ks = jax.random.split(key, 5)
        B, S, D = (8, 256, 128)
        return {'query': jax.random.normal(ks[0], (B, S, D), dtype=jnp.float32), 'key': jax.random.normal(ks[1], (B, S, D), dtype=jnp.float32), 'value': jax.random.normal(ks[2], (B, S, D), dtype=jnp.float32), 'cell_mask': jnp.ones((B, S, S), dtype=jnp.float32), 'seq_mask': jnp.ones((B, S), dtype=jnp.float32), 'W_k': jax.random.normal(ks[3], (D, D), dtype=jnp.float32) * (1.0 / np.sqrt(D)), 'b_k': jnp.zeros((D,), dtype=jnp.float32), 'W_o': jax.random.normal(ks[4], (D, D), dtype=jnp.float32) * (1.0 / np.sqrt(D)), 'b_o': jnp.zeros((D,), dtype=jnp.float32)}
    _L0_xattn_all = _L0_xattn_setup()
    _L0_xattn_in = {k: v for k, v in _L0_xattn_all.items() if k in ('W_k', 'b_k', 'W_o', 'b_o')}
    del _L0_xattn_all

    def _L0_ffn_setup():
        import jax, jax.numpy as jnp
        import numpy as np
        BLOCK = 32
        W_BITS = 4
        ACT_BITS = 16

        def act_qdq(x):
            qmax = 2.0 ** (ACT_BITS - 1) - 1.0
            scale = jnp.maximum(jnp.max(jnp.abs(x)) / qmax, 1e-12)
            return jnp.clip(jnp.round(x / scale), -qmax - 1.0, qmax) * scale

        def fixed_qdq_u16(x):
            scale = 1.0 / 65536.0
            return jnp.clip(jnp.round(x / scale), 0.0, 65535.0) * scale

        def lpbq_dequant(w):
            O, I = w.shape
            qmax = 2.0 ** (W_BITS - 1) - 1.0
            wb = w.reshape(O, I // BLOCK, BLOCK)
            s = jnp.maximum(jnp.max(jnp.abs(wb), axis=-1, keepdims=True) / qmax, 1e-12)
            wq = jnp.clip(jnp.round(wb / s), -qmax - 1.0, qmax) * s
            return wq.reshape(O, I)
        key = jax.random.key(seed)
        k1, k2, k3, k4 = jax.random.split(key, 4)
        B, S, H, I = (2, 512, 128, 384)
        x = jax.random.normal(k1, (B, S, H), jnp.float32)
        w_gate = jax.random.normal(k2, (I, H), jnp.float32) * 0.02
        w_up = jax.random.normal(k3, (I, H), jnp.float32) * 0.02
        w_down = jax.random.normal(k4, (H, I), jnp.float32) * 0.02
        return {'x': x, 'w_gate': w_gate, 'w_up': w_up, 'w_down': w_down}
    _L0_ffn_all = _L0_ffn_setup()
    _L0_ffn_in = {k: v for k, v in _L0_ffn_all.items() if k in ('w_gate', 'w_up', 'w_down')}
    del _L0_ffn_all

    def _L1_xattn_setup():
        import jax, jax.numpy as jnp
        import numpy as np
        import math
        HIDDEN = 128
        HEADS = 16
        HEAD = HIDDEN // HEADS
        SCALE_BASE = 512.0

        def _gammas(heads):
            return 1.0 - jnp.exp(jnp.linspace(math.log(1.0 / 32.0), math.log(1.0 / 512.0), heads))

        def _xpos(x, downscale):
            S, d = (x.shape[2], x.shape[3])
            half = d // 2
            base_scale = (jnp.arange(0, d, 2, dtype=jnp.float32) + 0.4 * d) / (1.4 * d)
            pos = jnp.arange(S, dtype=jnp.float32)
            scale = base_scale[None, :] ** (pos / SCALE_BASE)[:, None]
            if downscale:
                scale = 1.0 / scale
            inv_freq = 1.0 / 10000.0 ** (jnp.arange(half, dtype=jnp.float32) / half)
            sinusoid = pos[:, None] * inv_freq[None, :]
            sin = jnp.repeat(jnp.sin(sinusoid) * scale, 2, axis=-1)
            cos = jnp.repeat(jnp.cos(sinusoid) * scale, 2, axis=-1)
            x1 = x[..., ::2]
            x2 = x[..., 1::2]
            rot = jnp.stack([-x2, x1], axis=-1).reshape(x.shape)
            return x * cos + rot * sin

        def _decay_mask(S, gammas):
            n = jnp.arange(S)[:, None]
            m = jnp.arange(S)[None, :]
            diff = (n - m).astype(jnp.float32)
            mask = n >= m
            pw = jnp.maximum(diff, 0.0)[None, :, :]
            return jnp.where(mask[None, :, :], gammas[:, None, None] ** pw, 0.0)

        def retention_forward(Q, K, V):
            B, S, _ = Q.shape

            def split(x, hd):
                return x.reshape(B, S, HEADS, hd).transpose(0, 2, 1, 3)
            q = _xpos(split(Q, HEAD), downscale=False)
            k = _xpos(split(K, HEAD), downscale=True)
            v = split(V, HEAD)
            D = _decay_mask(S, _gammas(HEADS).astype(Q.dtype))
            scores = jnp.einsum('bhsd,bhtd->bhst', q, k) * D[None]
            out = jnp.einsum('bhst,bhtd->bhsd', scores, v)
            return out.transpose(0, 2, 1, 3).reshape(B, S, HEADS * HEAD)
        key = jax.random.key(seed)
        kq, kk, kv = jax.random.split(key, 3)
        B, S = (2, 256)
        return {'Q': jax.random.normal(kq, (B, S, HIDDEN), dtype=jnp.float32), 'K': jax.random.normal(kk, (B, S, HIDDEN), dtype=jnp.float32), 'V': jax.random.normal(kv, (B, S, HIDDEN), dtype=jnp.float32)}
    _L1_xattn_all = _L1_xattn_setup()
    _L1_xattn_in = {k: v for k, v in _L1_xattn_all.items() if k in ()}
    del _L1_xattn_all

    def _L1_ffn_setup():
        import jax, jax.numpy as jnp
        import numpy as np
        from jax import lax
        B, L, D = (4, 256, 128)
        E, TOPK = (8, 2)
        K, DIL = (3, 1)
        HID = D // 4
        EPS = 1e-06

        def _rmsnorm(h, w):
            rms = jnp.sqrt(jnp.mean(h * h, axis=-1, keepdims=True) + EPS)
            return w * (h / rms)

        def _forward(x, dw_kernel, dw_bias, pw_w, pw_b, router_w, router_b, expert_w, expert_b, out_w, out_b, norm_w, ff_down_w, ff_down_b, ff_up_w, ff_up_b):
            pad = (K - 1) * DIL
            xc = jnp.transpose(x, (0, 2, 1))
            xc = lax.conv_general_dilated(xc, dw_kernel, window_strides=(1,), padding=((pad, 0),), rhs_dilation=(DIL,), dimension_numbers=('NCH', 'OIH', 'NCH'), feature_group_count=D) + dw_bias[None, :, None]
            xc = jax.nn.silu(jnp.einsum('bdl,ed->bel', xc, pw_w) + pw_b[None, :, None])
            x1 = x + jnp.transpose(xc, (0, 2, 1))
            logits = jnp.einsum('bsd,ed->bse', x1, router_w) + router_b
            top_v, top_i = lax.top_k(logits, TOPK)
            top_w = jax.nn.softmax(top_v, axis=-1)
            rw = jnp.sum(jax.nn.one_hot(top_i, E, dtype=x1.dtype) * top_w[..., None], axis=-2)
            ye = jax.nn.silu(jnp.einsum('bsd,eod->bseo', x1, expert_w) + expert_b)
            combined = jnp.einsum('bse,bseo->bso', rw, ye)
            moe_out = jnp.einsum('bsd,od->bso', combined, out_w) + out_b
            h = _rmsnorm(x1 + moe_out, norm_w)
            ff = jax.nn.gelu(jnp.einsum('bsd,hd->bsh', h, ff_down_w) + ff_down_b, approximate=False)
            ff = jnp.einsum('bsh,dh->bsd', ff, ff_up_w) + ff_up_b
            return h + ff
        key = jax.random.key(seed)
        ks = jax.random.split(key, 16)
        s = 0.02
        return {'x': jax.random.normal(ks[0], (B, L, D), dtype=jnp.float32), 'dw_kernel': jax.random.normal(ks[1], (D, 1, K), dtype=jnp.float32) * s, 'dw_bias': jnp.zeros((D,), dtype=jnp.float32), 'pw_w': jax.random.normal(ks[2], (D, D), dtype=jnp.float32) * s, 'pw_b': jnp.zeros((D,), dtype=jnp.float32), 'router_w': jax.random.normal(ks[3], (E, D), dtype=jnp.float32) * s, 'router_b': jnp.zeros((E,), dtype=jnp.float32), 'expert_w': jax.random.normal(ks[4], (E, D, D), dtype=jnp.float32) * s, 'expert_b': jnp.zeros((E, D), dtype=jnp.float32), 'out_w': jax.random.normal(ks[5], (D, D), dtype=jnp.float32) * s, 'out_b': jnp.zeros((D,), dtype=jnp.float32), 'norm_w': jnp.ones((D,), dtype=jnp.float32), 'ff_down_w': jax.random.normal(ks[6], (HID, D), dtype=jnp.float32) * s, 'ff_down_b': jnp.zeros((HID,), dtype=jnp.float32), 'ff_up_w': jax.random.normal(ks[7], (D, HID), dtype=jnp.float32) * s, 'ff_up_b': jnp.zeros((D,), dtype=jnp.float32)}
    _L1_ffn_all = _L1_ffn_setup()
    _L1_ffn_in = {k: v for k, v in _L1_ffn_all.items() if k in ('dw_kernel', 'dw_bias', 'pw_w', 'pw_b', 'router_w', 'router_b', 'expert_w', 'expert_b', 'out_w', 'out_b', 'norm_w', 'ff_down_w', 'ff_down_b', 'ff_up_w', 'ff_up_b')}
    del _L1_ffn_all

    def _L2_xattn_setup():
        import jax, jax.numpy as jnp
        import numpy as np
        import math
        EPS = 1e-08
        LN_EPS = 1e-05
        B, S, E, NH = (2, 256, 128, 4)
        DH = E // NH

        def _mlstm_cell(q, k, v, igate_w, igate_b, fgate_w, fgate_b, out_w):
            Bq, Sq, Eq = q.shape
            if_in = jnp.concatenate([q, k, v], axis=-1)
            ig = jnp.einsum('bsf,hf->bsh', if_in, igate_w) + igate_b
            fg = jnp.einsum('bsf,hf->bsh', if_in, fgate_w) + fgate_b
            ig = jnp.transpose(ig, (0, 2, 1))[..., None]
            fg = jnp.transpose(fg, (0, 2, 1))[..., None]
            qh = q.reshape(Bq, Sq, NH, DH).transpose(0, 2, 1, 3)
            kh = k.reshape(Bq, Sq, NH, DH).transpose(0, 2, 1, 3)
            vh = v.reshape(Bq, Sq, NH, DH).transpose(0, 2, 1, 3)
            log_fg = jax.nn.log_sigmoid(fg)
            cs = jnp.cumsum(log_fg, axis=2)
            cs_shift = jnp.concatenate([jnp.zeros_like(cs[:, :, :1]), cs[:, :, :-1]], axis=2)
            logfg_mat = cs - jnp.swapaxes(cs_shift, -2, -1)
            ltr = jnp.tril(jnp.ones((Sq, Sq), dtype=bool))
            logfg_mat = jnp.where(ltr, logfg_mat, -jnp.inf)
            log_D = logfg_mat + jnp.swapaxes(ig, -2, -1)
            max_log_D = jnp.max(log_D, axis=-1, keepdims=True)
            D = jnp.exp(log_D - max_log_D)
            qk = jnp.einsum('bhsd,bhtd->bhst', qh, kh / math.sqrt(DH))
            C = qk * D
            sum_C_abs = jnp.abs(jnp.sum(C, axis=-1, keepdims=True))
            normaliser = jnp.maximum(sum_C_abs, jnp.exp(-max_log_D))
            C_norm = C / (normaliser + EPS)
            h = jnp.einsum('bhst,bhtd->bhsd', C_norm, vh)
            mean = jnp.mean(h, axis=-1, keepdims=True)
            var = jnp.mean((h - mean) ** 2, axis=-1, keepdims=True)
            h_norm = (h - mean) / jnp.sqrt(var + LN_EPS)
            scale = (1.0 + out_w).reshape(1, NH, 1, DH)
            h_norm = h_norm * scale
            return h_norm.transpose(0, 2, 1, 3).reshape(Bq, Sq, Eq)
        key = jax.random.key(seed)
        ks = jax.random.split(key, 7)
        std_g = math.sqrt(2.0 / (5.0 * 3 * E))
        return {'q': jax.random.normal(ks[0], (B, S, E), dtype=jnp.float32), 'k': jax.random.normal(ks[1], (B, S, E), dtype=jnp.float32), 'v': jax.random.normal(ks[2], (B, S, E), dtype=jnp.float32), 'igate_w': jax.random.normal(ks[3], (NH, 3 * E), dtype=jnp.float32) * std_g, 'igate_b': jax.random.normal(ks[4], (NH,), dtype=jnp.float32) * 0.1, 'fgate_w': jax.random.normal(ks[5], (NH, 3 * E), dtype=jnp.float32) * std_g, 'fgate_b': jnp.linspace(3.4, 6.0, NH, dtype=jnp.float32), 'out_w': jnp.zeros((E,), dtype=jnp.float32)}
    _L2_xattn_all = _L2_xattn_setup()
    _L2_xattn_in = {k: v for k, v in _L2_xattn_all.items() if k in ('igate_w', 'igate_b', 'fgate_w', 'fgate_b', 'out_w')}
    del _L2_xattn_all

    def _L2_ffn_setup():
        import jax, jax.numpy as jnp
        import numpy as np
        B, T, DIM, H, DH, TOPK = (4, 256, 128, 8, 64, 3)
        key = jax.random.key(seed)
        ks = jax.random.split(key, 6)
        x = jax.random.normal(ks[0], (B, T, DIM), dtype=jnp.float32)
        sc = 1.0 / np.sqrt(DIM)
        Wq = jax.random.normal(ks[1], (DIM, H * DH), dtype=jnp.float32) * sc
        Wkv = jax.random.normal(ks[2], (DIM, 2 * H * DH), dtype=jnp.float32) * sc
        Ws = jax.random.normal(ks[3], (DIM, H), dtype=jnp.float32) * sc
        Wo = jax.random.normal(ks[4], (H, DH, DIM), dtype=jnp.float32) * (1.0 / np.sqrt(DH))
        bo = jax.random.normal(ks[5], (H, DIM), dtype=jnp.float32) * 0.01
        return {'x': x, 'Wq': Wq, 'Wkv': Wkv, 'Ws': Ws, 'Wo': Wo, 'bo': bo}
    _L2_ffn_all = _L2_ffn_setup()
    _L2_ffn_in = {k: v for k, v in _L2_ffn_all.items() if k in ('Wq', 'Wkv', 'Ws', 'Wo', 'bo')}
    del _L2_ffn_all

    def _L3_xattn_setup():
        import jax, jax.numpy as jnp
        import numpy as np
        D_MODEL = 128
        NUM_HEADS = 16
        D_K = D_MODEL // NUM_HEADS
        R = 8
        ALPHA = 16
        SCALING = ALPHA / R

        def _lora_linear(x, W, b, A, Bm):
            base = jnp.einsum('btd,od->bto', x, W) + b
            lora = jnp.einsum('btr,or->bto', jnp.einsum('btd,rd->btr', x, A), Bm) * SCALING
            return base + lora
        key = jax.random.key(seed)
        ks = jax.random.split(key, 20)
        B, T = (2, 256)
        inp = {'q': jax.random.normal(ks[0], (B, T, D_MODEL), jnp.float32), 'k': jax.random.normal(ks[1], (B, T, D_MODEL), jnp.float32), 'v': jax.random.normal(ks[2], (B, T, D_MODEL), jnp.float32), 'mask': jnp.ones((1, 1, T, T), jnp.int32)}
        i = 3
        for name in ('q', 'k', 'v'):
            inp[f'W{name}'] = jax.random.normal(ks[i], (D_MODEL, D_MODEL), jnp.float32) * 0.02
            i += 1
            inp[f'b{name}'] = jnp.zeros((D_MODEL,), jnp.float32)
            inp[f'A{name}'] = jax.random.normal(ks[i], (R, D_MODEL), jnp.float32) * 0.01
            i += 1
            inp[f'B{name}'] = jax.random.normal(ks[i], (D_MODEL, R), jnp.float32) * 0.01
            i += 1
        inp['Wo'] = jax.random.normal(ks[i], (D_MODEL, D_MODEL), jnp.float32) * 0.02
        inp['bo'] = jnp.zeros((D_MODEL,), jnp.float32)
        return inp
    _L3_xattn_all = _L3_xattn_setup()
    _L3_xattn_in = {k: v for k, v in _L3_xattn_all.items() if k in ('Wq', 'bq', 'Aq', 'Bq', 'Wk', 'bk', 'Ak', 'Bk', 'Wv', 'bv', 'Av', 'Bv', 'Wo', 'bo')}
    del _L3_xattn_all

    def _L3_ffn_setup():
        import jax, jax.numpy as jnp
        import numpy as np
        EPS = 1e-05

        def _quantize(W):
            gamma = jnp.mean(jnp.abs(W))
            return jnp.clip(jnp.round(W / (gamma + EPS)), -1.0, 1.0)
        key = jax.random.key(seed)
        k_x, k_w1, k_b1, k_w2, k_b2 = jax.random.split(key, 5)
        n_embd = 128
        d_ff = 4 * n_embd
        B, S = (4, 512)
        bound1 = 1.0 / np.sqrt(n_embd)
        bound2 = 1.0 / np.sqrt(d_ff)
        x = jax.random.normal(k_x, (B, S, n_embd), dtype=jnp.float32)
        W1 = jax.random.uniform(k_w1, (d_ff, n_embd), jnp.float32, -bound1, bound1)
        b1 = jax.random.uniform(k_b1, (d_ff,), jnp.float32, -bound1, bound1)
        W2 = jax.random.uniform(k_w2, (n_embd, d_ff), jnp.float32, -bound2, bound2)
        b2 = jax.random.uniform(k_b2, (n_embd,), jnp.float32, -bound2, bound2)
        return {'x': x, 'W1': W1, 'b1': b1, 'W2': W2, 'b2': b2}
    _L3_ffn_all = _L3_ffn_setup()
    _L3_ffn_in = {k: v for k, v in _L3_ffn_all.items() if k in ('W1', 'b1', 'W2', 'b2')}
    del _L3_ffn_all
    return {'x': x, 'ctx_1024': ctx_1024, 'mask_BxSxS2_ff1': mask_BxSxS2_ff1, 'mask_BxS2_ff1': mask_BxS2_ff1, 'mask_1x1xSxS2_if1': mask_1x1xSxS2_if1, 'g_xattn': g_xattn, 'g_ffn': g_ffn, 'L0_xattn_W_k': _L0_xattn_in['W_k'], 'L0_xattn_b_k': _L0_xattn_in['b_k'], 'L0_xattn_W_o': _L0_xattn_in['W_o'], 'L0_xattn_b_o': _L0_xattn_in['b_o'], 'L0_ffn_w_gate': _L0_ffn_in['w_gate'], 'L0_ffn_w_up': _L0_ffn_in['w_up'], 'L0_ffn_w_down': _L0_ffn_in['w_down'], 'L1_ffn_dw_kernel': _L1_ffn_in['dw_kernel'], 'L1_ffn_dw_bias': _L1_ffn_in['dw_bias'], 'L1_ffn_pw_w': _L1_ffn_in['pw_w'], 'L1_ffn_pw_b': _L1_ffn_in['pw_b'], 'L1_ffn_router_w': _L1_ffn_in['router_w'], 'L1_ffn_router_b': _L1_ffn_in['router_b'], 'L1_ffn_expert_w': _L1_ffn_in['expert_w'], 'L1_ffn_expert_b': _L1_ffn_in['expert_b'], 'L1_ffn_out_w': _L1_ffn_in['out_w'], 'L1_ffn_out_b': _L1_ffn_in['out_b'], 'L1_ffn_norm_w': _L1_ffn_in['norm_w'], 'L1_ffn_ff_down_w': _L1_ffn_in['ff_down_w'], 'L1_ffn_ff_down_b': _L1_ffn_in['ff_down_b'], 'L1_ffn_ff_up_w': _L1_ffn_in['ff_up_w'], 'L1_ffn_ff_up_b': _L1_ffn_in['ff_up_b'], 'L2_xattn_igate_w': _L2_xattn_in['igate_w'], 'L2_xattn_igate_b': _L2_xattn_in['igate_b'], 'L2_xattn_fgate_w': _L2_xattn_in['fgate_w'], 'L2_xattn_fgate_b': _L2_xattn_in['fgate_b'], 'L2_xattn_out_w': _L2_xattn_in['out_w'], 'L2_ffn_Wq': _L2_ffn_in['Wq'], 'L2_ffn_Wkv': _L2_ffn_in['Wkv'], 'L2_ffn_Ws': _L2_ffn_in['Ws'], 'L2_ffn_Wo': _L2_ffn_in['Wo'], 'L2_ffn_bo': _L2_ffn_in['bo'], 'L3_xattn_Wq': _L3_xattn_in['Wq'], 'L3_xattn_bq': _L3_xattn_in['bq'], 'L3_xattn_Aq': _L3_xattn_in['Aq'], 'L3_xattn_Bq': _L3_xattn_in['Bq'], 'L3_xattn_Wk': _L3_xattn_in['Wk'], 'L3_xattn_bk': _L3_xattn_in['bk'], 'L3_xattn_Ak': _L3_xattn_in['Ak'], 'L3_xattn_Bk': _L3_xattn_in['Bk'], 'L3_xattn_Wv': _L3_xattn_in['Wv'], 'L3_xattn_bv': _L3_xattn_in['bv'], 'L3_xattn_Av': _L3_xattn_in['Av'], 'L3_xattn_Bv': _L3_xattn_in['Bv'], 'L3_xattn_Wo': _L3_xattn_in['Wo'], 'L3_xattn_bo': _L3_xattn_in['bo'], 'L3_ffn_W1': _L3_ffn_in['W1'], 'L3_ffn_b1': _L3_ffn_in['b1'], 'L3_ffn_W2': _L3_ffn_in['W2'], 'L3_ffn_b2': _L3_ffn_in['b2']}

def reference(x, ctx_1024, mask_BxSxS2_ff1, mask_BxS2_ff1, mask_1x1xSxS2_if1, g_xattn, g_ffn, L0_xattn_W_k, L0_xattn_b_k, L0_xattn_W_o, L0_xattn_b_o, L0_ffn_w_gate, L0_ffn_w_up, L0_ffn_w_down, L1_ffn_dw_kernel, L1_ffn_dw_bias, L1_ffn_pw_w, L1_ffn_pw_b, L1_ffn_router_w, L1_ffn_router_b, L1_ffn_expert_w, L1_ffn_expert_b, L1_ffn_out_w, L1_ffn_out_b, L1_ffn_norm_w, L1_ffn_ff_down_w, L1_ffn_ff_down_b, L1_ffn_ff_up_w, L1_ffn_ff_up_b, L2_xattn_igate_w, L2_xattn_igate_b, L2_xattn_fgate_w, L2_xattn_fgate_b, L2_xattn_out_w, L2_ffn_Wq, L2_ffn_Wkv, L2_ffn_Ws, L2_ffn_Wo, L2_ffn_bo, L3_xattn_Wq, L3_xattn_bq, L3_xattn_Aq, L3_xattn_Bq, L3_xattn_Wk, L3_xattn_bk, L3_xattn_Ak, L3_xattn_Bk, L3_xattn_Wv, L3_xattn_bv, L3_xattn_Av, L3_xattn_Bv, L3_xattn_Wo, L3_xattn_bo, L3_ffn_W1, L3_ffn_b1, L3_ffn_W2, L3_ffn_b2):
    import jax
    import jax.numpy as jnp

    def _L0_xattn_ref(query, key, value, cell_mask, seq_mask, W_k, b_k, W_o, b_o):
        import jax, jax.numpy as jnp
        import numpy as np
        k_proj = jnp.einsum('bkd,qd->bkq', key, W_k) + b_k
        scores = jnp.einsum('bqd,bkd->bqk', query, k_proj)
        scores = scores + jnp.log(cell_mask) + jnp.log(seq_mask)[:, None, :]
        p_attn = jax.nn.softmax(scores, axis=-1)
        x = jnp.einsum('bqk,bkd->bqd', p_attn, value)
        return jnp.einsum('bqd,od->bqo', x, W_o) + b_o

    def _L0_ffn_ref(x, w_gate, w_up, w_down):
        import jax, jax.numpy as jnp
        import numpy as np
        BLOCK = 32
        W_BITS = 4
        ACT_BITS = 16

        def act_qdq(x):
            qmax = 2.0 ** (ACT_BITS - 1) - 1.0
            scale = jnp.maximum(jnp.max(jnp.abs(x)) / qmax, 1e-12)
            return jnp.clip(jnp.round(x / scale), -qmax - 1.0, qmax) * scale

        def fixed_qdq_u16(x):
            scale = 1.0 / 65536.0
            return jnp.clip(jnp.round(x / scale), 0.0, 65535.0) * scale

        def lpbq_dequant(w):
            O, I = w.shape
            qmax = 2.0 ** (W_BITS - 1) - 1.0
            wb = w.reshape(O, I // BLOCK, BLOCK)
            s = jnp.maximum(jnp.max(jnp.abs(wb), axis=-1, keepdims=True) / qmax, 1e-12)
            wq = jnp.clip(jnp.round(wb / s), -qmax - 1.0, qmax) * s
            return wq.reshape(O, I)
        x = act_qdq(x)
        up = act_qdq(x @ lpbq_dequant(w_up).T)
        gate = act_qdq(x @ lpbq_dequant(w_gate).T)
        sig = fixed_qdq_u16(jax.nn.sigmoid(gate))
        gate = act_qdq(gate * sig)
        o = act_qdq(gate * up)
        return o @ lpbq_dequant(w_down).T

    def _L1_xattn_ref(Q, K, V):
        import jax, jax.numpy as jnp
        import numpy as np
        import math
        HIDDEN = 128
        HEADS = 16
        HEAD = HIDDEN // HEADS
        SCALE_BASE = 512.0

        def _gammas(heads):
            return 1.0 - jnp.exp(jnp.linspace(math.log(1.0 / 32.0), math.log(1.0 / 512.0), heads))

        def _xpos(x, downscale):
            S, d = (x.shape[2], x.shape[3])
            half = d // 2
            base_scale = (jnp.arange(0, d, 2, dtype=jnp.float32) + 0.4 * d) / (1.4 * d)
            pos = jnp.arange(S, dtype=jnp.float32)
            scale = base_scale[None, :] ** (pos / SCALE_BASE)[:, None]
            if downscale:
                scale = 1.0 / scale
            inv_freq = 1.0 / 10000.0 ** (jnp.arange(half, dtype=jnp.float32) / half)
            sinusoid = pos[:, None] * inv_freq[None, :]
            sin = jnp.repeat(jnp.sin(sinusoid) * scale, 2, axis=-1)
            cos = jnp.repeat(jnp.cos(sinusoid) * scale, 2, axis=-1)
            x1 = x[..., ::2]
            x2 = x[..., 1::2]
            rot = jnp.stack([-x2, x1], axis=-1).reshape(x.shape)
            return x * cos + rot * sin

        def _decay_mask(S, gammas):
            n = jnp.arange(S)[:, None]
            m = jnp.arange(S)[None, :]
            diff = (n - m).astype(jnp.float32)
            mask = n >= m
            pw = jnp.maximum(diff, 0.0)[None, :, :]
            return jnp.where(mask[None, :, :], gammas[:, None, None] ** pw, 0.0)

        def retention_forward(Q, K, V):
            B, S, _ = Q.shape

            def split(x, hd):
                return x.reshape(B, S, HEADS, hd).transpose(0, 2, 1, 3)
            q = _xpos(split(Q, HEAD), downscale=False)
            k = _xpos(split(K, HEAD), downscale=True)
            v = split(V, HEAD)
            D = _decay_mask(S, _gammas(HEADS).astype(Q.dtype))
            scores = jnp.einsum('bhsd,bhtd->bhst', q, k) * D[None]
            out = jnp.einsum('bhst,bhtd->bhsd', scores, v)
            return out.transpose(0, 2, 1, 3).reshape(B, S, HEADS * HEAD)
        return retention_forward(Q, K, V)

    def _L1_ffn_ref(x, dw_kernel, dw_bias, pw_w, pw_b, router_w, router_b, expert_w, expert_b, out_w, out_b, norm_w, ff_down_w, ff_down_b, ff_up_w, ff_up_b):
        import jax, jax.numpy as jnp
        import numpy as np
        from jax import lax
        B, L, D = (4, 256, 128)
        E, TOPK = (8, 2)
        K, DIL = (3, 1)
        HID = D // 4
        EPS = 1e-06

        def _rmsnorm(h, w):
            rms = jnp.sqrt(jnp.mean(h * h, axis=-1, keepdims=True) + EPS)
            return w * (h / rms)

        def _forward(x, dw_kernel, dw_bias, pw_w, pw_b, router_w, router_b, expert_w, expert_b, out_w, out_b, norm_w, ff_down_w, ff_down_b, ff_up_w, ff_up_b):
            pad = (K - 1) * DIL
            xc = jnp.transpose(x, (0, 2, 1))
            xc = lax.conv_general_dilated(xc, dw_kernel, window_strides=(1,), padding=((pad, 0),), rhs_dilation=(DIL,), dimension_numbers=('NCH', 'OIH', 'NCH'), feature_group_count=D) + dw_bias[None, :, None]
            xc = jax.nn.silu(jnp.einsum('bdl,ed->bel', xc, pw_w) + pw_b[None, :, None])
            x1 = x + jnp.transpose(xc, (0, 2, 1))
            logits = jnp.einsum('bsd,ed->bse', x1, router_w) + router_b
            top_v, top_i = lax.top_k(logits, TOPK)
            top_w = jax.nn.softmax(top_v, axis=-1)
            rw = jnp.sum(jax.nn.one_hot(top_i, E, dtype=x1.dtype) * top_w[..., None], axis=-2)
            ye = jax.nn.silu(jnp.einsum('bsd,eod->bseo', x1, expert_w) + expert_b)
            combined = jnp.einsum('bse,bseo->bso', rw, ye)
            moe_out = jnp.einsum('bsd,od->bso', combined, out_w) + out_b
            h = _rmsnorm(x1 + moe_out, norm_w)
            ff = jax.nn.gelu(jnp.einsum('bsd,hd->bsh', h, ff_down_w) + ff_down_b, approximate=False)
            ff = jnp.einsum('bsh,dh->bsd', ff, ff_up_w) + ff_up_b
            return h + ff
        return _forward(x, dw_kernel, dw_bias, pw_w, pw_b, router_w, router_b, expert_w, expert_b, out_w, out_b, norm_w, ff_down_w, ff_down_b, ff_up_w, ff_up_b)

    def _L2_xattn_ref(q, k, v, igate_w, igate_b, fgate_w, fgate_b, out_w):
        import jax, jax.numpy as jnp
        import numpy as np
        import math
        EPS = 1e-08
        LN_EPS = 1e-05
        B, S, E, NH = (2, 256, 128, 4)
        DH = E // NH

        def _mlstm_cell(q, k, v, igate_w, igate_b, fgate_w, fgate_b, out_w):
            Bq, Sq, Eq = q.shape
            if_in = jnp.concatenate([q, k, v], axis=-1)
            ig = jnp.einsum('bsf,hf->bsh', if_in, igate_w) + igate_b
            fg = jnp.einsum('bsf,hf->bsh', if_in, fgate_w) + fgate_b
            ig = jnp.transpose(ig, (0, 2, 1))[..., None]
            fg = jnp.transpose(fg, (0, 2, 1))[..., None]
            qh = q.reshape(Bq, Sq, NH, DH).transpose(0, 2, 1, 3)
            kh = k.reshape(Bq, Sq, NH, DH).transpose(0, 2, 1, 3)
            vh = v.reshape(Bq, Sq, NH, DH).transpose(0, 2, 1, 3)
            log_fg = jax.nn.log_sigmoid(fg)
            cs = jnp.cumsum(log_fg, axis=2)
            cs_shift = jnp.concatenate([jnp.zeros_like(cs[:, :, :1]), cs[:, :, :-1]], axis=2)
            logfg_mat = cs - jnp.swapaxes(cs_shift, -2, -1)
            ltr = jnp.tril(jnp.ones((Sq, Sq), dtype=bool))
            logfg_mat = jnp.where(ltr, logfg_mat, -jnp.inf)
            log_D = logfg_mat + jnp.swapaxes(ig, -2, -1)
            max_log_D = jnp.max(log_D, axis=-1, keepdims=True)
            D = jnp.exp(log_D - max_log_D)
            qk = jnp.einsum('bhsd,bhtd->bhst', qh, kh / math.sqrt(DH))
            C = qk * D
            sum_C_abs = jnp.abs(jnp.sum(C, axis=-1, keepdims=True))
            normaliser = jnp.maximum(sum_C_abs, jnp.exp(-max_log_D))
            C_norm = C / (normaliser + EPS)
            h = jnp.einsum('bhst,bhtd->bhsd', C_norm, vh)
            mean = jnp.mean(h, axis=-1, keepdims=True)
            var = jnp.mean((h - mean) ** 2, axis=-1, keepdims=True)
            h_norm = (h - mean) / jnp.sqrt(var + LN_EPS)
            scale = (1.0 + out_w).reshape(1, NH, 1, DH)
            h_norm = h_norm * scale
            return h_norm.transpose(0, 2, 1, 3).reshape(Bq, Sq, Eq)
        return _mlstm_cell(q, k, v, igate_w, igate_b, fgate_w, fgate_b, out_w)

    def _L2_ffn_ref(x, Wq, Wkv, Ws, Wo, bo):
        import jax, jax.numpy as jnp
        import numpy as np
        B, T, DIM, H, DH, TOPK = (4, 256, 128, 8, 64, 3)
        b, t, _ = x.shape
        s = jax.nn.sigmoid(x @ Ws)
        vals, idx = jax.lax.top_k(s, TOPK)
        bi = jnp.arange(b)[:, None, None]
        ti = jnp.arange(t)[None, :, None]
        scores = jnp.zeros_like(s).at[bi, ti, idx].set(vals)
        q = (x @ Wq).reshape(b, t, H, DH).transpose(0, 2, 1, 3)
        kv = (x @ Wkv).reshape(b, t, 2, H, DH).transpose(2, 0, 3, 1, 4)
        k, v = (kv[0], kv[1])
        scale = DH ** (-0.5)
        attn = jax.nn.softmax(jnp.einsum('bhid,bhjd->bhij', q * scale, k), axis=-1)
        out = jnp.einsum('bhij,bhjd->bhid', attn, v)
        proj = jnp.einsum('bhtd,hde->bhte', out, Wo) + bo[None, :, None, :]
        return jnp.einsum('bhte,bth->bte', proj, scores)

    def _L3_xattn_ref(q, k, v, mask, Wq, bq, Aq, Bq, Wk, bk, Ak, Bk, Wv, bv, Av, Bv, Wo, bo):
        import jax, jax.numpy as jnp
        import numpy as np
        D_MODEL = 128
        NUM_HEADS = 16
        D_K = D_MODEL // NUM_HEADS
        R = 8
        ALPHA = 16
        SCALING = ALPHA / R

        def _lora_linear(x, W, b, A, Bm):
            base = jnp.einsum('btd,od->bto', x, W) + b
            lora = jnp.einsum('btr,or->bto', jnp.einsum('btd,rd->btr', x, A), Bm) * SCALING
            return base + lora
        B, Tq, _ = q.shape
        Tk = k.shape[1]
        Q = _lora_linear(q, Wq, bq, Aq, Bq).reshape(B, Tq, NUM_HEADS, D_K).transpose(0, 2, 1, 3)
        K = _lora_linear(k, Wk, bk, Ak, Bk).reshape(B, Tk, NUM_HEADS, D_K).transpose(0, 2, 1, 3)
        V = _lora_linear(v, Wv, bv, Av, Bv).reshape(B, Tk, NUM_HEADS, D_K).transpose(0, 2, 1, 3)
        scores = jnp.einsum('bhqd,bhkd->bhqk', Q, K) / jnp.sqrt(jnp.float32(D_K))
        scores = jnp.where(mask == 0, jnp.float32(-1000000000.0), scores)
        attn = jax.nn.softmax(scores, axis=-1)
        out = jnp.einsum('bhqk,bhkd->bhqd', attn, V)
        out = out.transpose(0, 2, 1, 3).reshape(B, Tq, D_MODEL)
        return jnp.einsum('btd,od->bto', out, Wo) + bo

    def _L3_ffn_ref(x, W1, b1, W2, b2):
        import jax, jax.numpy as jnp
        import numpy as np
        EPS = 1e-05

        def _quantize(W):
            gamma = jnp.mean(jnp.abs(W))
            return jnp.clip(jnp.round(W / (gamma + EPS)), -1.0, 1.0)
        Wq1 = _quantize(W1)
        Wq2 = _quantize(W2)
        h = jax.nn.relu(jnp.einsum('bsd,fd->bsf', x, Wq1) + b1)
        out = jnp.einsum('bsf,df->bsd', h, Wq2) + b2
        return out
    x = x + jnp.tanh(g_xattn[0]) * _L0_xattn_ref(_layernorm(x, axis=-1), ctx_1024, ctx_1024, mask_BxSxS2_ff1, mask_BxS2_ff1, L0_xattn_W_k, L0_xattn_b_k, L0_xattn_W_o, L0_xattn_b_o)
    x = x + jnp.tanh(g_ffn[0]) * _L0_ffn_ref(_layernorm(x, axis=-1), L0_ffn_w_gate, L0_ffn_w_up, L0_ffn_w_down)
    x = x + jnp.tanh(g_xattn[1]) * _L1_xattn_ref(_layernorm(x, axis=-1), ctx_1024, ctx_1024)
    x = x + jnp.tanh(g_ffn[1]) * _L1_ffn_ref(_layernorm(x, axis=-1), L1_ffn_dw_kernel, L1_ffn_dw_bias, L1_ffn_pw_w, L1_ffn_pw_b, L1_ffn_router_w, L1_ffn_router_b, L1_ffn_expert_w, L1_ffn_expert_b, L1_ffn_out_w, L1_ffn_out_b, L1_ffn_norm_w, L1_ffn_ff_down_w, L1_ffn_ff_down_b, L1_ffn_ff_up_w, L1_ffn_ff_up_b)
    x = x + jnp.tanh(g_xattn[2]) * _L2_xattn_ref(_layernorm(x, axis=-1), ctx_1024, ctx_1024, L2_xattn_igate_w, L2_xattn_igate_b, L2_xattn_fgate_w, L2_xattn_fgate_b, L2_xattn_out_w)
    x = x + jnp.tanh(g_ffn[2]) * _L2_ffn_ref(_layernorm(x, axis=-1), L2_ffn_Wq, L2_ffn_Wkv, L2_ffn_Ws, L2_ffn_Wo, L2_ffn_bo)
    x = x + jnp.tanh(g_xattn[3]) * _L3_xattn_ref(_layernorm(x, axis=-1), ctx_1024, ctx_1024, mask_1x1xSxS2_if1, L3_xattn_Wq, L3_xattn_bq, L3_xattn_Aq, L3_xattn_Bq, L3_xattn_Wk, L3_xattn_bk, L3_xattn_Ak, L3_xattn_Bk, L3_xattn_Wv, L3_xattn_bv, L3_xattn_Av, L3_xattn_Bv, L3_xattn_Wo, L3_xattn_bo)
    x = x + jnp.tanh(g_ffn[3]) * _L3_ffn_ref(_layernorm(x, axis=-1), L3_ffn_W1, L3_ffn_b1, L3_ffn_W2, L3_ffn_b2)
    return x

_drawn_inputs = setup_inputs


def setup_inputs(seed=0):
    import zlib

    import numpy as np

    out = dict(_drawn_inputs(seed))
    spreads = {'L0_xattn_b_k': (0.0, 2.0),
     'L0_xattn_b_o': (0.0, 0.1),
     'L1_ffn_dw_bias': (0.0, 0.8),
     'L1_ffn_pw_b': (0.0, 0.8),
     'L1_ffn_router_b': (0.0, 0.8),
     'L1_ffn_expert_b': (0.0, 0.8),
     'L1_ffn_out_b': (0.0, 0.8),
     'L1_ffn_norm_w': (1.0, 0.6),
     'L1_ffn_ff_down_b': (0.0, 0.8),
     'L1_ffn_ff_up_b': (0.0, 0.8),
     'L2_xattn_out_w': (0.0, 0.8),
     'L3_xattn_bq': (0.0, 0.8),
     'L3_xattn_bk': (0.0, 2.0),
     'L3_xattn_bv': (0.0, 2.0),
     'L3_xattn_bo': (0.0, 2.0)}
    factors = {'L0_ffn_w_gate': 8.0,
     'L0_ffn_w_up': 8.0,
     'L0_ffn_w_down': 8.0,
     'L1_ffn_dw_kernel': 8.0,
     'L1_ffn_pw_w': 8.0,
     'L1_ffn_router_w': 8.0,
     'L1_ffn_expert_w': 8.0,
     'L1_ffn_out_w': 8.0,
     'L1_ffn_ff_down_w': 8.0,
     'L1_ffn_ff_up_w': 8.0,
     'L2_xattn_igate_w': 6.856,
     'L2_xattn_igate_b': 64.0,
     'L2_xattn_fgate_w': 64.0,
     'L2_xattn_fgate_b': 64.0,
     'L2_ffn_Wq': 5.891,
     'L2_ffn_Wkv': 3.653,
     'L2_ffn_Ws': 4.534,
     'L2_ffn_Wo': 3.641,
     'L2_ffn_bo': 64.0,
     'L3_xattn_Wq': 8.0,
     'L3_xattn_Aq': 29.448,
     'L3_xattn_Bq': 28.445,
     'L3_xattn_Wk': 8.0,
     'L3_xattn_Ak': 26.978,
     'L3_xattn_Bk': 27.258,
     'L3_xattn_Wv': 8.0,
     'L3_xattn_Av': 34.022,
     'L3_xattn_Bv': 32.272,
     'L3_xattn_Wo': 8.0,
     'L3_ffn_b1': 8.0,
     'L3_ffn_b2': 200.0}
    for name, (base, spread) in spreads.items():
        noise = np.random.default_rng([zlib.crc32(name.encode()), seed]).standard_normal(out[name].shape)
        drawn = base * np.exp(spread * noise) if base else spread * noise
        out[name] = jnp.asarray(drawn.astype(out[name].dtype))
    for name, factor in factors.items():
        out[name] = (out[name] * factor).astype(out[name].dtype)
    return out
```

```python
from contextlib import ExitStack
import math

import numpy as np

import concourse.bass as bass
from concourse import mybir

ALU = mybir.AluOpType
ACT = mybir.ActivationFunctionType
F32 = mybir.dt.float32
BF16 = mybir.dt.bfloat16
I32 = mybir.dt.int32
AX_X = mybir.AxisListType.X

B, S, D = 16, 128, 128
GB = 4
NG = B // GB
T = GB * S
LAYERS = 8
L0A, L0F, L1A, L1F, L2A, L2F, L3A, L3F = range(LAYERS)
LN_EPS = 1e-5

FF0, BLOCK = 384, 32
C0 = FF0 // 128
QMAX16, QMAX4 = 32767.0, 7.0
ROUND = 1.5 * 2.0 ** 23

H16, DH8 = 16, 8
PADH = 32
E1, TOP1, HID1 = 8, 2, 32
RMS_EPS = 1e-6
H4, DH32 = 4, 32
MLSTM_EPS = 1e-8
H8, DH64, TOP2 = 8, 64, 3
C2 = H8 * DH64 // 128
RANK = 8
LORA_SCALE = 16.0 / 8.0
FF3 = 512
C3 = FF3 // 128
X0 = 16
BIG = 1e30


def pieces():
    return [
        ("ident", 128, 128), ("ones", 128, 128), ("gates", 128, 8), ("eye8", 8, 8 * 128),
        ("l0_WkT", 128, 128), ("l0_bk", 128, 1), ("l0_WoT", 128, 128), ("l0_bo", 1, 128),
        ("l0_gate", 128, C0 * 128), ("l0_up", 128, C0 * 128), ("l0_down", 128, FF0),
        ("cosq", 128, 128), ("sinq", 128, 128), ("cosk", 128, 128), ("sink", 128, 128),
        ("causalT", 128, 128),
        ("l1_dw", 128, 3), ("l1_dwb", 128, 1), ("l1_pwT", 128, 128), ("l1_pwb", 128, 1),
        ("l1_routerT", 128, E1), ("l1_routerb", 128, E1), ("l1_expertT", 128, E1 * 128),
        ("l1_expertb", 128, E1), ("l1_outT", 128, 128), ("l1_outb", 128, 1), ("l1_norm", 128, 1),
        ("l1_downT", 128, HID1), ("l1_downb", HID1, 1), ("l1_upT", HID1, 128), ("l1_upb", 128, 1),
        ("before", 128, 64),
        ("l2_igT", 128, 3 * H4), ("l2_fgT", 128, 3 * H4), ("l2_igb", H4, 1), ("l2_fgb", H4, 1),
        ("l2_outw", 128, 128), ("keep", H4, T), ("restart", H4, T), ("futureT", 128, 128),
        ("l2_Wq", 128, 512), ("l2_Wk", 128, 512), ("l2_Wv", 128, 512), ("l2_Ws", 128, H8),
        ("l2_Wo", 128, C2 * 128), ("l2_bo", H8, 128),
        ("l3_WqP", 128, 512), ("l3_WkP", 128, 512), ("l3_WvT", 128, 128),
        ("l3_Aq", RANK, 128), ("l3_Ak", RANK, 128), ("l3_Av", RANK, 128),
        ("l3_BqP", RANK, 512), ("l3_BkP", RANK, 512), ("l3_BvT", RANK, 128),
        ("l3_bqP", 128, 4), ("l3_bkP", 128, 4), ("l3_bv", 1, 128), ("l3_WoP", 128, 512),
        ("l3_bo", 1, 128),
        ("l3_W1T", 128, FF3), ("l3_b1", 128, C3), ("l3_W2T", 128, C3 * 128), ("l3_b2", 1, 128),
    ]


def columns():
    at, where = 0, {}
    for name, p, n in pieces():
        where[name] = (p, at, n)
        at += n
    return where, at


WHERE, COLS = columns()
PARTS = ["l0_bo", "l0_down", "causalT", "before", "futureT", "l2_bo", "l3_b2"]


class Ended:

    def __init__(self, eng, sem):
        self.eng, self.sem, self.total, self.base, self.n = eng, sem, 0, 0, 0

    def __call__(self, ins):
        self.n += 1
        ins.then_inc(self.sem, 1)
        self.eng.wait_ge(self.sem, self.base + self.n)

    def turn(self, i, per):
        self.base, self.n, self.per = self.total + i * per, 0, per

    def loop_over(self, turns):
        assert self.n == self.per, f"{self.n} in one turn, not {self.per}"
        self.total += turns * self.per
        self.base, self.n = self.total, 0

    def straight_over(self):
        self.total += self.n
        self.base, self.n = self.total, 0


def build(nc, x_in, ctx_in, ctxT_in, cell_in, seq_in, imask_in, pack_in, out, layers=LAYERS):
    with ExitStack() as stack:
        def sb(name, shape, dt=F32):
            return stack.enter_context(nc.sbuf_tensor(name, shape, dt))

        def sem(name):
            return stack.enter_context(nc.semaphore(name))

        x_all = sb("x_all", [128, B * D])
        ctx = sb("ctx", [128, B * D])
        ctxT = sb("ctxT", [128, B * S])
        pack = sb("pack", [128, COLS])
        tg = sb("tg", [128, LAYERS])
        identb = sb("identb", [128, 128], BF16)
        imask = sb("imask", [128, S], I32)

        def W(name, a=0, n=None):
            p, at, cols = WHERE[name]
            return pack[0:p, at + a:at + (cols if n is None else a + n)]

        stats = sb("stats", [128, GB, 6])
        moment = sb("moment", [128, GB, 3])
        mean = sb("mean", [128, GB])
        var = sb("var", [128, GB])              
        rstd = sb("rstd", [128, GB])
        minus_half = sb("minus_half", [128, 16])
        xn = sb("xn", [128, GB, D])
        xnT = sb("xnT", [128, GB, S])
        area = sb("area", [128, 24576])
        areas = [0]

        def work(*shape, p=128, dt=F32):
            n = int(np.prod(shape)) // (2 if dt == BF16 else 1)
            a = area[0:p, areas[0]:areas[0] + n]
            areas[0] += n
            assert areas[0] <= 24576
            if dt == BF16:
                a = a.bitcast(BF16)
            if len(shape) == 2:
                a = a.rearrange("p (a b) -> p a b", a=shape[0])
            if len(shape) == 3:
                a = a.rearrange("p (a b c) -> p a b c", a=shape[0], b=shape[1])
            return a

        bank = [stack.enter_context(nc.psum_tensor(f"bank{k}", [128, 512], F32)) for k in range(8)]

        def by4(k):
            return bank[k][:, :].rearrange("p (b s) -> p b s", b=GB)

        ctx_loaded = sem("ctx_loaded")
        masks_loaded = sem("masks_loaded")
        imask_loaded = sem("imask_loaded")
        part_loaded = [sem(f"part{n}_loaded") for n in range(len(PARTS))]
        x_updated = sem("x_updated")
        ln_var = sem("ln_var")
        ln_rstd = sem("ln_rstd")
        xn_ready = sem("xn_ready")
        xnT_psum = sem("xnT_psum")
        xnT_ready = sem("xnT_ready")
        y_ready = sem("y_ready")
        gates_ready = sem("gates_ready")
        dve_ended = sem("dve_ended")
        act_ended = sem("act_ended")
        pool_ended = sem("pool_ended")
        stored = sem("stored")

        def weights(eng, layer_part):
            eng.wait_ge(part_loaded[layer_part], 16)

        def group(t, i, b=0, n=GB):
            return t[:, bass.ds(i * T + b * 128, n * 128)]

        def group4(t, i):
            return group(t, i).rearrange("p (b d) -> p b d", b=GB)

        def norm_stats_dve(dve, ended, l, i):
            for b in range(GB):
                last = dve.bn_stats(stats[:, b, :], group(x_all, i, b, 1))
            ended(last)
            even, odd = stats[:, :, 1:3], stats[:, :, 4:6]
            dve.tensor_tensor(moment[:, :, 0:2], even, odd, ALU.add)
            ended(dve.tensor_tensor(moment[:, :, 2], even[:, :, 0], odd[:, :, 0], ALU.subtract))
            dve.tensor_scalar(mean[:, :], moment[:, :, 0], 0.5, None, ALU.mult)
            dve.tensor_scalar(var[:, :], moment[:, :, 1], 1.0 / D, LN_EPS, ALU.mult, ALU.add)
            ended(dve.tensor_tensor(moment[:, :, 2], moment[:, :, 2], moment[:, :, 2], ALU.mult))
            dve.scalar_tensor_tensor(var[:, :], moment[:, :, 2], 0.25, var[:, :], ALU.mult, ALU.add).then_inc(ln_var, 1)

        def norm_apply_dve(dve, ended, l, i, dst=lambda b: xn[:, b, :]):
            dve.wait_ge(ln_rstd, 4 * l + i + 1)
            for b in range(GB):
                last = dve.tensor_scalar(dst(b), group(x_all, i, b, 1), mean[:, b:b + 1],
                                         rstd[:, b:b + 1], ALU.subtract, ALU.mult)
            last.then_inc(xn_ready, 1)
            dve.wait_ge(xn_ready, 4 * l + i + 1)

        def over_groups_dve(dve, ended, l, per, body):
            def norms(l, i):
                return (lambda: norm_stats_dve(dve, ended, l, i)), (lambda: norm_apply_dve(dve, ended, l, i))

            def nothing():
                pass

            if l in (L0A, L1A):
                for step in norms(l, 0):
                    step()
                ended.straight_over()
            with dve.Fori(0, NG - 1) as i:
                ended.turn(i, per)
                body(i, *norms(l, i + 1))
            ended.loop_over(NG - 1)
            body(NG - 1, *(norms(l + 1, 0) if l not in (L0A, L3F) and l + 1 < layers else (nothing, nothing)))
            ended.straight_over()

        def norm_pool(pool, l, i):
            pool.wait_ge(ln_var, 4 * l + i + 1)
            pool.tensor_tensor(rstd[:, :], var[:, :], minus_half[:, 0:GB], ALU.pow).then_inc(ln_rstd, 1)

        def norms_pool(pool, l):
            with pool.Fori(0, NG) as i:
                norm_pool(pool, l, i)

        def turned(l):
            return 4 * (l if l < L1A else l - 1)

        def turn_pe(pe, l, i, src=xn, ready=xn_ready):
            pe.wait_ge(ready, (4 * l if ready is xn_ready else 0) + i + 1)
            for b in range(GB):
                last = pe.transpose(by4(0)[:, b, :], src[:, b, :], W("ident"))
            last.then_inc(xnT_psum, 1)

        def turned_act(act, l, i, dst=None):
            act.wait_ge(xnT_psum, turned(l) + i + 1)
            act.activation(xnT[:, :, :] if dst is None else dst, by4(0), ACT.Copy).then_inc(xnT_ready, 1)

        def update_dve(dve, l, i, k=None, src=None):
            dve.wait_ge(y_ready, 4 * l + i + 1)
            xs = group(x_all, i)
            dve.scalar_tensor_tensor(xs, bank[k][:, :] if src is None else src, tg[:, l:l + 1], xs,
                                     ALU.mult, ALU.add).then_inc(x_updated, 1)
            dve.wait_ge(x_updated, X0 + 4 * l + i + 1)

        def bias_pe(pe, k, row):
            pe.matmul(bank[k][:, :], W("ones")[0:1, :],
                      row.unsqueeze(1).to_broadcast([1, GB, 128]), start=True, stop=False)

        def begun(eng, l, i):
            eng.wait_ge(x_updated, X0 + 4 * l + i)

        def bc(ap, *shape):
            for axis, n in enumerate(shape):
                if n < 0:
                    ap = ap.unsqueeze(axis + 1)
            return ap.to_broadcast([ap.shape[0], *map(abs, shape)])

        def rank_dve(dve, ended, logit, sel, wide, top):
            lj = logit.unsqueeze(2).to_broadcast([128, GB, 8, 8])
            le = logit.unsqueeze(3).to_broadcast([128, GB, 8, 8])
            before = W("before").rearrange("p (e j) -> p e j", e=8).unsqueeze(1).to_broadcast([128, GB, 8, 8])
            gt, ge = wide[0], wide[1]
            dve.tensor_tensor(gt, lj, le, ALU.is_gt)
            ended(dve.tensor_tensor(ge, lj, le, ALU.is_ge))
            ended(dve.tensor_tensor(ge, ge, gt, ALU.subtract))
            ended(dve.tensor_tensor(ge, ge, before, ALU.mult))
            ended(dve.tensor_tensor(gt, gt, ge, ALU.add))
            ended(dve.tensor_reduce(sel, gt, AX_X, ALU.add))
            ended(dve.tensor_scalar(sel, sel, float(top), None, ALU.is_lt))

        areas[0] = 0
        cell, seqm = work(B * S), work(B * S)
        a_kT, a_s, a_p, a_pT, a_o, a_oT = (work(GB, 128) for _ in range(6))
        a_nmax, a_sum, a_rsum = work(GB), work(GB), work(GB)
        l0a_logs, l0a_k_psum, l0a_k, l0a_s_psum, l0a_masked, l0a_p, l0a_pT_psum, l0a_pT, l0a_o_psum, l0a_o, \
            l0a_oT_psum, l0a_oT = (sem(f"l0a_{n}") for n in "logs k_psum k s_psum masked p pT_psum pT o_psum o "
                                   "oT_psum oT".split())

        def l0a_act(act, ended):
            act.wait_ge(masks_loaded, 32)
            act.activation(cell, cell, ACT.Ln)
            act.activation(seqm, seqm, ACT.Ln).then_inc(l0a_logs, 1)
            with act.Fori(0, NG) as i:
                ended.turn(i, 0)
                turned_act(act, L0A, i)
                act.wait_ge(l0a_masked, i + 1)
                for b in range(GB):
                    last = act.activation(a_p[:, b, :], a_s[:, b, :], ACT.Exp, bias=a_nmax[:, b:b + 1],
                                          accum_out=a_sum[:, b:b + 1])
                last.then_inc(l0a_p, 1)
                act.wait_ge(l0a_oT_psum, i + 1)
                act.activation(a_oT, by4(5), ACT.Copy).then_inc(l0a_oT, 1)
            ended.loop_over(NG)

        def l0a_dve(dve, ended):
            dve.wait_ge(l0a_logs, 1)
            ended(dve.tensor_tensor(cell, cell, seqm, ALU.add))
            ended.straight_over()

            def body(i, stats, apply):
                dve.wait_ge(l0a_k_psum, i + 1)
                dve.tensor_scalar(a_kT, by4(1), W("l0_bk"), None, ALU.add).then_inc(l0a_k, 1)
                dve.wait_ge(l0a_s_psum, i + 1)
                ended(dve.tensor_tensor(a_s, by4(2), group4(cell, i), ALU.add))
                dve.tensor_reduce(a_nmax, a_s, AX_X, ALU.max, negate=True).then_inc(l0a_masked, 1)
                stats()
                dve.wait_ge(l0a_pT_psum, i + 1)
                dve.tensor_copy(a_pT, by4(3)).then_inc(l0a_pT, 1)
                apply()
                dve.wait_ge(l0a_p, i + 1)
                ended(dve.reciprocal(a_rsum, a_sum))
                dve.wait_ge(l0a_o_psum, i + 1)
                dve.tensor_tensor(a_o, by4(4), bc(a_rsum, GB, -128), ALU.mult).then_inc(l0a_o, 1)
                update_dve(dve, L0A, i, 6)
            over_groups_dve(dve, ended, L0A, 5, body)

        def l0a_pe(pe):
            pe.wait_ge(ctx_loaded, 32)
            with pe.Fori(0, NG) as i:
                turn_pe(pe, L0A, i)
                begun(pe, L0A, i)
                pe.matmul(bank[1][:, :], W("l0_WkT"), group(ctxT, i), start=True, stop=True).then_inc(l0a_k_psum, 1)
                pe.wait_ge(l0a_k, i + 1)
                pe.wait_ge(xnT_ready, turned(L0A) + i + 1)
                for b in range(GB):
                    last = pe.matmul(by4(2)[:, b, :], xnT[:, b, :], a_kT[:, b, :], start=True, stop=True)
                last.then_inc(l0a_s_psum, 1)
                pe.wait_ge(l0a_p, i + 1)
                for b in range(GB):
                    last = pe.transpose(by4(3)[:, b, :], a_p[:, b, :], W("ident"))
                last.then_inc(l0a_pT_psum, 1)
                pe.wait_ge(l0a_pT, i + 1)
                for b in range(GB):
                    last = pe.matmul(by4(4)[:, b, :], a_pT[:, b, :], group(ctx, i, b, 1), start=True, stop=True)
                last.then_inc(l0a_o_psum, 1)
                pe.wait_ge(l0a_o, i + 1)
                for b in range(GB):
                    last = pe.transpose(by4(5)[:, b, :], a_o[:, b, :], W("ident"))
                last.then_inc(l0a_oT_psum, 1)
                bias_pe(pe, 6, W("l0_bo"))
                pe.wait_ge(l0a_oT, i + 1)
                for b in range(GB):
                    last = pe.matmul(by4(6)[:, b, :], a_oT[:, b, :], W("l0_WoT"), start=False, stop=(b == GB - 1))
                last.then_inc(y_ready, 1)

        areas[0] = 0
        GW = C0 * T
        f_xn = work(B * D)
        f_gate, f_up, f_t, f_sig, f_q = work(NG * GW), work(NG * GW), work(GW), work(GW), work(C0, T)
        f_wmax, f_winv = work(3 * FF0 // BLOCK), work(3 * FF0 // BLOCK)
        f_wT = work(9, 128)
        f_amax, f_scale = work(5, 12), work(5, 4)
        l0f_w, l0f_wT_psum, l0f_wT, l0f_max, l0f_allmax, l0f_xq, l0f_psum, l0f_copied, l0f_gq, l0f_sig, l0f_oq = (
            sem(f"l0f_{n}") for n in "w wT_psum wT max allmax xq psum copied gq sig oq".split())

        def l0f_scale_dve(dve, ended, k, n):
            dve.tensor_reduce(f_scale[:, k, 0:1], f_amax[:, k, 0:n], AX_X, ALU.max).then_inc(l0f_max, 1)
            dve.wait_ge(l0f_allmax, k + 1)
            ended(dve.tensor_scalar(f_scale[:, k, 2:3], f_scale[:, k, 1:2], 1.0 / QMAX16, 1e-12, ALU.mult, ALU.max))
            ended(dve.reciprocal(f_scale[:, k, 3:4], f_scale[:, k, 2:3]))

        def l0f_round_dve(dve, ended, k, dst, src, tmp):
            ended(dve.tensor_scalar(tmp, src, f_scale[:, k, 3:4], ROUND, ALU.mult, ALU.add))
            return dve.tensor_scalar(dst, tmp, ROUND, f_scale[:, k, 2:3], ALU.subtract, ALU.mult)

        def l0f_pool(pool, ended):
            norms_pool(pool, L0F)
            for k in range(5):
                pool.wait_ge(l0f_max, k + 1)
                pool.partition_all_reduce(f_scale[:, k, 1:2], f_scale[:, k, 0:1], 128,
                                          bass.bass_isa.ReduceOp.max).then_inc(l0f_allmax, 1)

        def l0f_act(act, ended):
            for k in range(3):
                act.wait_ge(l0f_wT_psum, k + 1)
                act.activation(f_wT[:, 3 * k:3 * k + 3, :], by4(1 + k)[:, 0:3, :], ACT.Copy).then_inc(l0f_wT, 1)
            with act.Fori(0, NG) as i:
                ended.turn(i, 0)
            ended.loop_over(NG)
            with act.Fori(0, NG) as i:
                turned_act(act, L0F, i)
                for c in range(C0):
                    act.wait_ge(l0f_psum, i * 6 + c + 1)
                    act.activation(f_gate[:, bass.ds(i * GW + c * T, T)], bank[1 + c][:, :], ACT.Copy).then_inc(l0f_copied, 1)
            with act.Fori(0, NG) as i:
                act.wait_ge(l0f_gq, i + 1)
                act.activation(f_sig, f_gate[:, bass.ds(i * GW, GW)], ACT.Sigmoid).then_inc(l0f_sig, 1)

        def l0f_dve(dve, ended):
            weights(dve, 1)
            dve.wait_ge(x_updated, X0 + 4 * L0F)
            w = W("l0_gate")
            _, at, _ = WHERE["l0_gate"]
            w3 = pack[:, at:at + 3 * FF0].rearrange("p (n k) -> p n k", k=BLOCK)
            n = 3 * FF0 // BLOCK
            ended(dve.tensor_reduce(f_wmax, w3, AX_X, ALU.max, apply_absolute_value=True))
            ended(dve.tensor_scalar(f_wmax, f_wmax, 1.0 / QMAX4, 1e-12, ALU.mult, ALU.max))
            ended(dve.reciprocal(f_winv, f_wmax))
            ended(dve.tensor_tensor(w3, w3, bc(f_winv, n, -BLOCK), ALU.mult))
            ended(dve.tensor_scalar(w3, w3, ROUND, ROUND, ALU.add, ALU.subtract))
            ended(dve.tensor_scalar(w3, w3, -QMAX4 - 1.0, QMAX4, ALU.max, ALU.min))
            dve.tensor_tensor(w3, w3, bc(f_wmax, n, -BLOCK), ALU.mult).then_inc(l0f_w, 1)
            ended.straight_over()
            with dve.Fori(0, NG) as i:
                ended.turn(i, 4)
                norm_stats_dve(dve, ended, L0F, i)
                norm_apply_dve(dve, ended, L0F, i, lambda b: group(f_xn, i, b, 1))
                ended(dve.tensor_reduce(f_amax[:, 0, bass.ds(i, 1)], group(f_xn, i), AX_X, ALU.max,
                                        apply_absolute_value=True))
            ended.loop_over(NG)
            l0f_scale_dve(dve, ended, 0, NG)
            ended.straight_over()
            with dve.Fori(0, NG) as i:
                ended.turn(i, 3)
                l0f_round_dve(dve, ended, 0, xn[:, :, :].rearrange("p b d -> p (b d)"), group(f_xn, i),
                              f_t[:, 0:T]).then_inc(l0f_xq, 1)
                for c in range(C0):
                    dve.wait_ge(l0f_psum, i * 6 + C0 + c + 1)
                    last = dve.tensor_copy(f_up[:, bass.ds(i * GW + c * T, T)], bank[4 + c][:, :])
                ended(last)
                dve.wait_ge(l0f_copied, i * C0 + C0)
                dve.tensor_reduce(f_amax[:, 1, bass.ds(i, 1)], f_gate[:, bass.ds(i * GW, GW)], AX_X, ALU.max,
                                  apply_absolute_value=True)
                ended(dve.tensor_reduce(f_amax[:, 2, bass.ds(i, 1)], f_up[:, bass.ds(i * GW, GW)], AX_X, ALU.max,
                                        apply_absolute_value=True))
            ended.loop_over(NG)
            l0f_scale_dve(dve, ended, 1, NG)
            l0f_scale_dve(dve, ended, 2, NG)
            ended.straight_over()
            with dve.Fori(0, NG) as i:
                ended.turn(i, 7)
                g, u = f_gate[:, bass.ds(i * GW, GW)], f_up[:, bass.ds(i * GW, GW)]
                l0f_round_dve(dve, ended, 1, g, g, f_t).then_inc(l0f_gq, 1)
                dve.wait_ge(l0f_gq, i + 1)
                ended(l0f_round_dve(dve, ended, 2, u, u, f_t))
                dve.wait_ge(l0f_sig, i + 1)
                ended(dve.tensor_scalar(f_sig, f_sig, 65536.0, ROUND, ALU.mult, ALU.add))
                ended(dve.tensor_scalar(f_sig, f_sig, ROUND, 65535.0, ALU.subtract, ALU.min))
                ended(dve.scalar_tensor_tensor(g, f_sig, 1.0 / 65536.0, g, ALU.mult, ALU.mult))
                ended(dve.tensor_reduce(f_amax[:, 3, bass.ds(i, 1)], g, AX_X, ALU.max, apply_absolute_value=True))
            ended.loop_over(NG)
            l0f_scale_dve(dve, ended, 3, NG)
            ended.straight_over()
            with dve.Fori(0, NG) as i:
                ended.turn(i, 4)
                g, u = f_gate[:, bass.ds(i * GW, GW)], f_up[:, bass.ds(i * GW, GW)]
                ended(l0f_round_dve(dve, ended, 3, g, g, f_t))
                ended(dve.tensor_tensor(g, g, u, ALU.mult))
                ended(dve.tensor_reduce(f_amax[:, 4, bass.ds(i, 1)], g, AX_X, ALU.max, apply_absolute_value=True))
            ended.loop_over(NG)
            l0f_scale_dve(dve, ended, 4, NG)
            ended.straight_over()
            with dve.Fori(0, NG) as i:
                ended.turn(i, 1)
                l0f_round_dve(dve, ended, 4, f_q.rearrange("p c t -> p (c t)"), f_gate[:, bass.ds(i * GW, GW)],
                              f_t).then_inc(l0f_oq, 1)
                update_dve(dve, L0F, i, 1)
            ended.loop_over(NG)

        def l0f_pe(pe):
            pe.wait_ge(l0f_w, 1)
            w = pack[:, WHERE["l0_gate"][1]:][:, 0:3 * FF0].rearrange("p (n k) -> p n k", k=128)
            for k in range(3):
                for c in range(3):
                    last = pe.transpose(by4(1 + k)[:, c, :], w[:, 3 * k + c, :], W("ident"))
                last.then_inc(l0f_wT_psum, 1)
            pe.wait_ge(l0f_wT, 3)
            with pe.Fori(0, NG) as i:
                turn_pe(pe, L0F, i, ready=l0f_xq)
                pe.wait_ge(xnT_ready, turned(L0F) + i + 1)
                for c in range(2 * C0):
                    pe.matmul(bank[1 + c][:, :], f_wT[:, c, :], xnT[:, :, :], start=True, stop=True)\
                      .then_inc(l0f_psum, 1)
            with pe.Fori(0, NG) as i:
                pe.wait_ge(l0f_oq, i + 1)
                for b in range(GB):
                    for c in range(C0):
                        last = pe.matmul(by4(1)[:, b, :], f_q[:, c, b * 128:b * 128 + 128], f_wT[:, 6 + c, :],
                                         start=(c == 0), stop=(c == C0 - 1))
                last.then_inc(y_ready, 1)

        areas[0] = 0
        r_t, r_r, r_kt, r_kr = (work(GB, D) for _ in range(4))
        r_q, r_k = work(GB * H16, PADH), work(GB * H16, PADH)
        r_qT, r_kT = work(GB, 4, S), work(GB, 4, S)
        r_s = work(2, 4, S)
        l1a_zeroed, l1a_q, l1a_k, l1a_qT_psum, l1a_kT_psum, l1a_qT, l1a_kT, l1a_s_psum, l1a_s, l1a_pv = (
            sem(f"l1a_{n}") for n in "zeroed q k qT_psum kT_psum qT kT s_psum s pv".split())
        NQ = GB * 4

        def pairs(ap, k):
            return ap.rearrange("p b (h two) -> p b h two", two=2)[:, :, :, k]

        def pairs2(ap, k):
            return ap.rearrange("p (h two) -> p h two", two=2)[:, :, k].unsqueeze(1).to_broadcast([128, GB, 64])

        def l1a_rotate(eng, ended, src, cos, sin, t, r, dst):
            c = W(cos).unsqueeze(1).to_broadcast([128, GB, D])
            eng.tensor_tensor(t, src, c, ALU.mult)
            eng.tensor_tensor(pairs(r, 0), pairs(src, 1), pairs2(W(sin), 0), ALU.mult)
            ended(eng.tensor_tensor(pairs(r, 1), pairs(src, 0), pairs2(W(sin), 1), ALU.mult))
            for b in range(GB):
                last = eng.tensor_tensor(dst.rearrange("p (b g j) c -> p b j g c", b=GB, g=4)[:, b, :, :, 0:DH8],
                                         t[:, b, :].rearrange("p (j g d) -> p j g d", j=4, g=4),
                                         r[:, b, :].rearrange("p (j g d) -> p j g d", j=4, g=4), ALU.add)
            return last

        def l1a_pool(pool, ended):
            weights(pool, 2)
            pool.wait_ge(x_updated, X0 + 4 * L1A)
            pool.memset(r_k, 0.0)
            pool.memset(r_q, 0.0).then_inc(l1a_zeroed, 1)
            pool.wait_ge(l1a_zeroed, 1)
            pool.wait_ge(ctx_loaded, 32)
            with pool.Fori(0, NG) as i:
                ended.turn(i, 1)
                norm_pool(pool, L1A, i)
                begun(pool, L1A, i)
                l1a_rotate(pool, ended, group4(ctx, i), "cosk", "sink", r_kt, r_kr, r_k).then_inc(l1a_k, 1)
            ended.loop_over(NG)

        def l1a_act(act, ended):
            with act.Fori(0, NG) as i:
                ended.turn(i, 0)
                for b in range(GB):
                    act.wait_ge(l1a_qT_psum, i * GB + b + 1)
                    act.activation(r_qT[:, b, :, :], by4(b % 2), ACT.Copy).then_inc(l1a_qT, 1)
            ended.loop_over(NG)

        def l1a_dve(dve, ended):
            weights(dve, 2)
            dve.wait_ge(l1a_zeroed, 1)

            def body(i, stats, apply):
                l1a_rotate(dve, ended, xn[:, :, :], "cosq", "sinq", r_t, r_r, r_q).then_inc(l1a_q, 1)
                for b in range(GB):
                    dve.wait_ge(l1a_kT_psum, i * GB + b + 1)
                    dve.tensor_copy(r_kT[:, b, :, :], by4(2 + b % 2)).then_inc(l1a_kT, 1)
                causal = W("causalT").unsqueeze(1).to_broadcast([128, 4, S])
                for n in range(NQ):
                    dve.wait_ge(l1a_s_psum, i * NQ + n + 1)
                    if n >= 2:
                        dve.wait_ge(l1a_pv, i * (NQ - 1) + n - 1)
                    dve.tensor_tensor(r_s[:, n % 2, :, :], by4(4 + n % 2), causal, ALU.mult).then_inc(l1a_s, 1)
                    if n == 6:
                        stats()
                    if n == 9:
                        apply()
                update_dve(dve, L1A, i, 6)
            over_groups_dve(dve, ended, L1A, 4, body)

        def l1a_pe(pe):
            with pe.Fori(0, NG) as i:
                pe.wait_ge(l1a_k, i + 1)
                pe.wait_ge(l1a_q, i + 1)
                q = r_q.rearrange("p (n j) c -> p n (j c)", j=4)
                k = r_k.rearrange("p (n j) c -> p n (j c)", j=4)
                for b in range(GB):
                    if b >= 2:
                        pe.wait_ge(l1a_qT, i * GB + b - 1)
                    for g in range(4):
                        last = pe.transpose(by4(b % 2)[:, g, :], q[:, 4 * b + g, :], W("ident"))
                    last.then_inc(l1a_qT_psum, 1)
                    if b >= 2:
                        pe.wait_ge(l1a_kT, i * GB + b - 1)
                    for g in range(4):
                        last = pe.transpose(by4(2 + b % 2)[:, g, :], k[:, 4 * b + g, :], W("ident"))
                    last.then_inc(l1a_kT_psum, 1)

                def scores(n):
                    b, j = divmod(n, 4)
                    rows = slice(PADH * j, PADH * j + DH8)
                    if j == 0:
                        pe.wait_ge(l1a_qT, i * GB + b + 1)
                        pe.wait_ge(l1a_kT, i * GB + b + 1)
                    if n >= 2:
                        pe.wait_ge(l1a_s, i * NQ + n - 1)
                    for g in range(4):
                        last = pe.matmul(by4(4 + n % 2)[:, g, :], r_kT[rows, b, g, :], r_qT[rows, b, g, :],
                                         start=True, stop=True)
                    last.then_inc(l1a_s_psum, 1)

                scores(0)
                for n in range(NQ):
                    if n + 1 < NQ:
                        scores(n + 1)
                    b, j = divmod(n, 4)
                    pe.wait_ge(l1a_s, i * NQ + n + 1)
                    for g in range(4):
                        h = 4 * j + g
                        last = pe.matmul(bank[6][:, b * D + h * DH8:b * D + (h + 1) * DH8], r_s[:, n % 2, g, :],
                                         ctx[:, bass.ds(i * T + b * D + h * DH8, DH8)], start=True, stop=True)
                    last.then_inc(l1a_pv if n < NQ - 1 else y_ready, 1)

        areas[0] = 0
        e_x = work(GB, S + 2)
        e_conv, e_silu, e_x1, e_y, e_sq, e_rr, e_h, e_o = (work(GB, S) for _ in range(8))
        e_logit, e_shift, e_exp, e_sel, e_rw = (work(GB, E1) for _ in range(5))
        e_wide = work(2, GB, 64).rearrange("p k b (e j) -> p k b e j", e=8)
        e_max, e_sum, e_rsum = work(GB), work(GB), work(GB)
        e_rwT, e_gelu = work(GB, S, p=E1), work(GB, S, p=HID1)
        e_ye, e_ys = work(2, T), work(2, T)
        l1f_conv, l1f_pw_psum, l1f_silu, l1f_x1, l1f_logit_psum, l1f_shift, l1f_exp, l1f_rw, l1f_rwT_psum, l1f_rwT, \
            l1f_ye_psum, l1f_ye, l1f_rwb_psum, l1f_ys, l1f_moe, l1f_sq, l1f_ms_psum, l1f_rr, l1f_h, l1f_down_psum, \
            l1f_gelu, l1f_up_psum, l1f_o = (
                sem(f"l1f_{n}") for n in "conv pw_psum silu x1 logit_psum shift exp rw rwT_psum rwT ye_psum ye "
                "rwb_psum ys moe sq ms_psum rr h down_psum gelu up_psum o".split())

        def l1f_act(act, ended):
            with act.Fori(0, NG) as i:
                ended.turn(i, 1)
                turned_act(act, L1F, i, e_x[:, :, 2:])
                act.wait_ge(l1f_pw_psum, i + 1)
                act.activation(e_silu, by4(1), ACT.Silu, bias=W("l1_pwb")).then_inc(l1f_silu, 1)
                act.wait_ge(l1f_shift, i + 1)
                act.activation(e_exp, e_shift, ACT.Exp).then_inc(l1f_exp, 1)
                act.wait_ge(l1f_rwT_psum, i + 1)
                act.activation(e_rwT, by4(3)[0:E1], ACT.Copy).then_inc(l1f_rwT, 1)
                for e in range(E1):
                    act.wait_ge(l1f_ye_psum, i * E1 + e + 1)
                    if e >= 2:
                        act.wait_ge(l1f_ys, i * E1 + e - 1)
                    act.activation(e_ye[:, e % 2, :], bank[4 + e % 2][:, :], ACT.Silu,
                                   bias=W("l1_expertb", e, 1)).then_inc(l1f_ye, 1)
                act.wait_ge(l1f_ms_psum, i + 1)
                ended(act.activation(e_rr, by4(0), ACT.Ln, scale=1.0 / D, bias=RMS_EPS))
                act.activation(e_rr, e_rr, ACT.Exp, scale=-0.5).then_inc(l1f_rr, 1)
                act.wait_ge(l1f_down_psum, i + 1)
                act.activation(e_gelu, by4(2)[0:HID1], ACT.Gelu, bias=W("l1_downb")).then_inc(l1f_gelu, 1)
            ended.loop_over(NG)

        def l1f_dve(dve, ended):
            weights(dve, 3)
            ended(dve.memset(e_x[:, :, 0:2], 0.0))
            ended.straight_over()

            def body(i, stats, apply):
                dve.wait_ge(xnT_ready, turned(L1F) + i + 1)
                ended(dve.tensor_scalar(e_conv, e_x[:, :, 0:S], W("l1_dw", 0, 1), W("l1_dwb"), ALU.mult, ALU.add))
                ended(dve.scalar_tensor_tensor(e_conv, e_x[:, :, 1:S + 1], W("l1_dw", 1, 1), e_conv, ALU.mult, ALU.add))
                dve.scalar_tensor_tensor(e_conv, e_x[:, :, 2:], W("l1_dw", 2, 1), e_conv, ALU.mult, ALU.add)\
                   .then_inc(l1f_conv, 1)
                dve.wait_ge(l1f_silu, i + 1)
                dve.tensor_tensor(e_x1, e_x[:, :, 2:], e_silu, ALU.add).then_inc(l1f_x1, 1)
                dve.wait_ge(l1f_logit_psum, i + 1)
                ended(dve.tensor_tensor(e_logit, bank[2][:, 0:GB * E1].rearrange("p (b e) -> p b e", b=GB),
                                        W("l1_routerb").unsqueeze(1).to_broadcast([128, GB, E1]), ALU.add))
                ended(dve.tensor_reduce(e_max, e_logit, AX_X, ALU.max))
                dve.tensor_tensor(e_shift, e_logit, bc(e_max, GB, -E1), ALU.subtract).then_inc(l1f_shift, 1)
                rank_dve(dve, ended, e_logit, e_sel, (e_wide[:, 0], e_wide[:, 1]), TOP1)
                dve.wait_ge(l1f_exp, i + 1)
                ended(dve.tensor_tensor(e_sel, e_exp, e_sel, ALU.mult))
                ended(dve.tensor_reduce(e_sum, e_sel, AX_X, ALU.add))
                ended(dve.reciprocal(e_rsum, e_sum))
                dve.tensor_tensor(e_rw, e_sel, bc(e_rsum, GB, -E1), ALU.mult).then_inc(l1f_rw, 1)
                for e in range(E1):
                    dve.wait_ge(l1f_rwb_psum, i * E1 + e + 1)
                    dve.wait_ge(l1f_ye, i * E1 + e + 1)
                    if e >= 2:
                        dve.wait_ge(l1f_moe, i * E1 + e - 1)
                    dve.tensor_tensor(e_ys[:, e % 2, :], bank[(6, 1)[e % 2]][:, :], e_ye[:, e % 2, :], ALU.mult)\
                       .then_inc(l1f_ys, 1)
                    if e == 2:
                        stats()
                    if e == 4:
                        apply()
                dve.wait_ge(l1f_moe, i * E1 + E1)
                dve.wait_ge(l1f_x1, i + 1)
                ended(dve.scalar_tensor_tensor(e_y, by4(7), W("l1_outb"), e_x1, ALU.add, ALU.add))
                dve.tensor_tensor(e_sq, e_y, e_y, ALU.mult).then_inc(l1f_sq, 1)
                dve.wait_ge(l1f_rr, i + 1)
                dve.scalar_tensor_tensor(e_h, e_y, W("l1_norm"), e_rr, ALU.mult, ALU.mult).then_inc(l1f_h, 1)
                dve.wait_ge(l1f_up_psum, i + 1)
                dve.wait_ge(l1f_h, i + 1)
                dve.scalar_tensor_tensor(e_o, by4(3), W("l1_upb"), e_h, ALU.add, ALU.add).then_inc(l1f_o, 1)
                update_dve(dve, L1F, i, 5)
            over_groups_dve(dve, ended, L1F, 17, body)

        def l1f_pe(pe):
            weights(pe, 3)
            with pe.Fori(0, NG) as i:
                turn_pe(pe, L1F, i)
                pe.wait_ge(l1f_conv, i + 1)
                pe.matmul(bank[1][:, :], W("l1_pwT"), e_conv, start=True, stop=True).then_inc(l1f_pw_psum, 1)
                pe.wait_ge(l1f_x1, i + 1)
                for b in range(GB):
                    last = pe.matmul(bank[2][:, b * E1:(b + 1) * E1], e_x1[:, b, :], W("l1_routerT"), start=True, stop=True)
                last.then_inc(l1f_logit_psum, 1)

                def expert(e):
                    if e >= 2:
                        pe.wait_ge(l1f_ye, i * E1 + e - 1)
                    pe.matmul(bank[4 + e % 2][:, :], W("l1_expertT", e * 128, 128), e_x1, start=True, stop=True)\
                      .then_inc(l1f_ye_psum, 1)

                def mix(e):
                    pe.wait_ge(l1f_ys, i * E1 + e + 1)
                    pe.matmul(bank[7][:, :], W("l1_outT"), e_ys[:, e % 2, :], start=(e == 0), stop=(e == E1 - 1))\
                      .then_inc(l1f_moe, 1)

                expert(0)
                expert(1)
                pe.wait_ge(l1f_rw, i + 1)
                for b in range(GB):
                    last = pe.transpose(by4(3)[0:E1, b, :], e_rw[:, b, :], W("ident"))
                last.then_inc(l1f_rwT_psum, 1)
                pe.wait_ge(l1f_rwT, i + 1)
                for e in range(E1):
                    pe.matmul(bank[(6, 1)[e % 2]][:, :], W("eye8", e * 128, 128), e_rwT, start=True, stop=True)\
                      .then_inc(l1f_rwb_psum, 1)
                    if e + 2 < E1:
                        expert(e + 2)
                    if e >= 1:
                        mix(e - 1)
                mix(E1 - 1)
                pe.wait_ge(l1f_sq, i + 1)
                pe.matmul(bank[0][:, :], W("ones"), e_sq, start=True, stop=True).then_inc(l1f_ms_psum, 1)
                pe.wait_ge(l1f_h, i + 1)
                pe.matmul(bank[2][0:HID1, :], W("l1_downT"), e_h, start=True, stop=True).then_inc(l1f_down_psum, 1)
                pe.wait_ge(l1f_gelu, i + 1)
                pe.matmul(bank[3][:, :], W("l1_upT"), e_gelu, start=True, stop=True).then_inc(l1f_up_psum, 1)
                pe.wait_ge(l1f_o, i + 1)
                for b in range(GB):
                    last = pe.transpose(by4(5)[:, b, :], e_o[:, b, :], W("ident"))
                last.then_inc(y_ready, 1)

        areas[0] = 0
        m_z, m_abs, m_lf, m_cs, m_a, m_nM, m_end = (work(GB, S, p=H4) for _ in range(7))
        m_aT = work(2 * GB * H4)
        m_kT = work(GB, S)
        m_v = work(GB * H4, DH32 + 1)
        m_arg, m_d, m_c = work(2, T), work(2, T), work(2, T)
        m_den, m_abs2, m_h, m_sq = work(GB * H4), work(GB * H4), work(GB * H4, DH32), work(GB * H4, DH32)
        m_mean, m_var, m_rstd = work(GB * H4), work(GB * H4), work(GB * H4)
        m_scale = work(D)
        m_future = work(S, dt=BF16)
        l2a_gates_psum, l2a_z, l2a_log, l2a_end_in, l2a_end, l2a_nM, l2a_ctx, l2a_aT_psum, l2a_bias_psum, \
            l2a_qk_psum, l2a_arg, l2a_d, l2a_c, l2a_hv, l2a_var, l2a_rstd, l2a_const = (
                sem(f"l2a_{n}") for n in "gates_psum z log end_in end nM ctx aT_psum bias_psum qk_psum arg d c hv "
                "var rstd const".split())

        def l2a_act(act, ended):
            act.wait_ge(l2a_const, 1)
            with act.Fori(0, NG) as i:
                ended.turn(i, 3)
                begun(act, L2A, i)
                act.activation(m_kT, group4(ctxT, i), ACT.Copy, scale=DH32 ** -0.5)
                act.activation(m_v[:, :, 0:DH32], group(ctx, i).rearrange("p (n d) -> p n d", d=DH32), ACT.Copy)\
                   .then_inc(l2a_ctx, 1)
                turned_act(act, L2A, i)
                act.wait_ge(l2a_z, i + 1)
                ended(act.activation(m_abs, m_z, ACT.Abs))
                ended(act.activation(m_abs, m_abs, ACT.Exp, scale=-1.0))
                act.activation(m_abs, m_abs, ACT.Ln, bias=1.0).then_inc(l2a_log, 1)
                act.wait_ge(l2a_end_in, i + 1)
                act.activation(m_end, m_end, ACT.Exp, scale=-1.0).then_inc(l2a_end, 1)
                for h in range(H4):
                    act.wait_ge(l2a_arg, i * H4 + h + 1)
                    if h >= 2:
                        act.wait_ge(l2a_c, i * H4 + h - 1)
                    act.activation(m_d[:, h % 2, :], m_arg[:, h % 2, :], ACT.Exp).then_inc(l2a_d, 1)
                act.wait_ge(l2a_var, i + 1)
                ended(act.activation(m_rstd, m_var, ACT.Ln, scale=1.0 / DH32, bias=LN_EPS))
                act.activation(m_rstd, m_rstd, ACT.Exp, scale=-0.5).then_inc(l2a_rstd, 1)
            ended.loop_over(NG)

        def l2a_dve(dve, ended):
            weights(dve, 4)
            dve.memset(m_v[:, :, DH32:], 1.0)
            dve.tensor_copy(m_future, W("futureT"))
            dve.tensor_scalar(m_scale, W("l2_outw"), 1.0, None, ALU.add).then_inc(l2a_const, 1)
            dve.wait_ge(l2a_const, 1)

            def flat(t):
                return t.rearrange("p b s -> p (b s)")


            def body(i, stats, apply):
                dve.wait_ge(l2a_gates_psum, i + 1)
                dve.tensor_scalar(m_z, by4(2)[0:H4], W("l2_fgb"), None, ALU.add).then_inc(l2a_z, 1)
                ended(dve.tensor_scalar(m_a, by4(1)[0:H4], W("l2_igb"), None, ALU.add))
                dve.wait_ge(l2a_log, i + 1)
                ended(dve.scalar_tensor_tensor(m_lf, m_z, 0.0, m_abs, ALU.min, ALU.subtract))
                ended(dve.tensor_tensor_scan(flat(m_cs), W("keep"), flat(m_lf), 0.0, ALU.mult, ALU.add))
                ended(dve.tensor_tensor(m_a[:, :, 1:], m_a[:, :, 1:], m_cs[:, :, :S - 1], ALU.subtract))
                ended(dve.tensor_tensor_scan(flat(m_nM), W("restart"), flat(m_a), -BIG, ALU.add, ALU.max))
                dve.tensor_tensor(m_end, m_nM, m_cs, ALU.add).then_inc(l2a_end_in, 1)
                dve.wait_ge(l2a_end_in, i + 1)
                dve.tensor_scalar(m_nM, m_nM, -1.0, None, ALU.mult).then_inc(l2a_nM, 1)
                dve.wait_ge(l2a_aT_psum, i + 1)
                ended(dve.tensor_copy(m_aT, bank[3][:, 0:2 * GB * H4]))
                for h in range(H4):
                    dve.wait_ge(l2a_bias_psum, i * H4 + h + 1)
                    if h >= 2:
                        dve.wait_ge(l2a_d, i * H4 + h - 1)
                    a_h = m_aT[:, 0:GB * H4].rearrange("p (b h) -> p h b", b=GB)[:, h, :]
                    dve.tensor_tensor(m_arg[:, h % 2, :].rearrange("p (b s) -> p b s", b=GB), by4(4 + h % 2),
                                      bc(a_h, GB, -S), ALU.add).then_inc(l2a_arg, 1)
                    dve.wait_ge(l2a_qk_psum, i * H4 + h + 1)
                    dve.wait_ge(l2a_d, i * H4 + h + 1)
                    if h >= 2:
                        dve.wait_ge(l2a_hv, i * (H4 - 1) + h - 1)
                    dve.tensor_tensor(m_c[:, h % 2, :], bank[6 + h % 2][:, :], m_d[:, h % 2, :], ALU.mult)\
                       .then_inc(l2a_c, 1)
                    if h == 1:
                        stats()
                    if h == 2:
                        apply()
                dve.wait_ge(y_ready, 4 * L2A + i + 1)
                n = GB * H4 // 2
                for half in range(2):
                    hv = bank[1 + half][:, 0:n * (DH32 + 1)].rearrange("p (n d) -> p n d", d=DH32 + 1)
                    last = dve.tensor_copy(m_den[:, half * n:(half + 1) * n], hv[:, :, DH32])
                ended(last)
                ended(dve.scalar_tensor_tensor(m_abs2, m_den, -1.0, m_den, ALU.mult, ALU.max))
                ended(dve.tensor_tensor(m_abs2, m_abs2, m_aT[:, GB * H4:], ALU.max))
                ended(dve.tensor_scalar(m_abs2, m_abs2, MLSTM_EPS, None, ALU.add))
                ended(dve.reciprocal(m_den, m_abs2))
                for half in range(2):
                    hv = bank[1 + half][:, 0:n * (DH32 + 1)].rearrange("p (n d) -> p n d", d=DH32 + 1)
                    last = dve.tensor_tensor(m_h[:, half * n:(half + 1) * n, :], hv[:, :, 0:DH32],
                                             bc(m_den[:, half * n:(half + 1) * n], n, -DH32), ALU.mult)
                ended(last)
                ended(dve.tensor_reduce(m_mean, m_h, AX_X, ALU.add))
                ended(dve.tensor_scalar(m_mean, m_mean, 1.0 / DH32, None, ALU.mult))
                ended(dve.tensor_tensor(m_h, m_h, bc(m_mean, 2 * n, -DH32), ALU.subtract))
                ended(dve.tensor_tensor(m_sq, m_h, m_h, ALU.mult))
                dve.tensor_reduce(m_var, m_sq, AX_X, ALU.add).then_inc(l2a_var, 1)
                dve.wait_ge(l2a_rstd, i + 1)
                ended(dve.tensor_tensor(m_h, m_h, bc(m_rstd, 2 * n, -DH32), ALU.mult))
                h4 = m_h.rearrange("p (b h) d -> p b (h d)", b=GB)
                ended(dve.tensor_tensor(h4, h4, m_scale.unsqueeze(1).to_broadcast([128, GB, D]), ALU.mult))
                update_dve(dve, L2A, i, src=m_h.rearrange("p n d -> p (n d)"))
            over_groups_dve(dve, ended, L2A, 21, body)

        def l2a_pe(pe):
            weights(pe, 4)
            pe.wait_ge(l2a_const, 1)
            with pe.Fori(0, NG) as i:
                begun(pe, L2A, i)
                gates = ((1, "l2_igT"), (2, "l2_fgT"))
                for k, w in gates:
                    pe.matmul(bank[k][0:H4, :], W(w, H4, H4), group(ctxT, i), start=True, stop=False)
                    pe.matmul(bank[k][0:H4, :], W(w, 2 * H4, H4), group(ctxT, i), start=False, stop=False)
                turn_pe(pe, L2A, i)
                pe.wait_ge(xnT_ready, turned(L2A) + i + 1)
                for k, w in gates:
                    last = pe.matmul(bank[k][0:H4, :], W(w, 0, H4), xnT[:, :, :], start=False, stop=True)
                last.then_inc(l2a_gates_psum, 1)
                pe.wait_ge(l2a_ctx, i + 1)

                def products(h):
                    if h >= 2:
                        pe.wait_ge(l2a_c, i * H4 + h - 1)
                    pe.matmul(by4(4 + h % 2), identb[:, :], m_future.unsqueeze(1).to_broadcast([128, GB, S]),
                              start=True, stop=False)
                    pe.matmul(bank[4 + h % 2][:, :], W("eye8", h * 128, 128)[0:H4], m_nM, start=False, stop=True)\
                      .then_inc(l2a_bias_psum, 1)
                    rows = slice(h * DH32, (h + 1) * DH32)
                    for b in range(GB):
                        last = pe.matmul(by4(6 + h % 2)[:, b, :], m_kT[rows, b, :], xnT[rows, b, :], start=True, stop=True)
                    last.then_inc(l2a_qk_psum, 1)

                pe.wait_ge(l2a_nM, i + 1)
                pe.wait_ge(l2a_end, i + 1)
                for k, t in enumerate((m_a, m_end)):
                    for b in range(GB):
                        at = (k * GB + b) * H4
                        last = pe.matmul(bank[3][:, at:at + H4], t[:, b, :], W("ident")[0:H4, 0:H4], start=True, stop=True)
                last.then_inc(l2a_aT_psum, 1)
                products(0)
                for h in range(H4):
                    if h + 1 < H4:
                        products(h + 1)
                    pe.wait_ge(l2a_c, i * H4 + h + 1)
                    for b in range(GB):
                        at = (b % 2 * H4 + h) * (DH32 + 1)
                        last = pe.matmul(bank[1 + b // 2][:, at:at + DH32 + 1], m_c[:, h % 2, b * S:(b + 1) * S],
                                         m_v[:, b * H4 + h, :], start=True, stop=True)
                    last.then_inc(l2a_hv if h < H4 - 1 else y_ready, 1)

        areas[0] = 0
        t_q, t_k = work(C2, T), work(C2, T)
        t_v = work(GB * H8, DH64)
        t_sig, t_sel, t_sc = work(GB, H8), work(GB, H8), work(GB, H8)
        t_wide = work(2, GB, 64).rearrange("p k b (e j) -> p k b e j", e=8)
        t_scT = work(GB, S, p=H8)
        t_nmax, t_sum, t_r = work(2, 4), work(2, 4), work(2, 4)
        t_p, t_pT = work(2, C2, S), work(2, C2, S)
        t_oT = work(2, C2, S)
        l2f_gate_psum, l2f_e, l2f_sc, l2f_psum, l2f_by_act, l2f_by_dve, l2f_s_psum, l2f_max, l2f_scT_psum, l2f_scT, \
            l2f_exp, l2f_p, l2f_pT_psum, l2f_pT, l2f_oT_psum, l2f_oT = (
                sem(f"l2f_{n}") for n in "gate_psum e sc psum by_act by_dve s_psum max scT_psum scT "
                "exp p pT_psum pT oT_psum oT".split())
        NH = 2 * GB

        def l2f_out(n):
            if n < 2 * C2:
                return (t_q, t_k)[n % 2][:, n // 2, :]
            return t_v[:, (n - 2 * C2) * H8:(n - 2 * C2 + 1) * H8, :]

        def l2f_in(n):
            a = bank[1 + n % 4][:, :]
            return a if n < 2 * C2 else a.rearrange("p (h d) -> p h d", d=DH64)

        def l2f_act(act, ended):
            with act.Fori(0, NG) as i:
                turned_act(act, L2F, i)
                act.wait_ge(l2f_gate_psum, i + 1)
                act.activation(t_sig, bank[5][:, 0:GB * H8].rearrange("p (b h) -> p b h", b=GB), ACT.Exp, scale=-1.0)\
                   .then_inc(l2f_e, 1)
                for n in range(0, 12, 2):
                    act.wait_ge(l2f_psum, i * 12 + n + 1)
                    act.activation(l2f_out(n), l2f_in(n), ACT.Copy, scale=DH64 ** -0.5 if n < 2 * C2 else 1.0)\
                       .then_inc(l2f_by_act, 1)

                def turned_p(m):
                    act.wait_ge(l2f_pT_psum, i * NH + m + 1)
                    act.activation(t_pT[:, m % 2, :, :], by4(1 + m % 2), ACT.Copy).then_inc(l2f_pT, 1)

                for m in range(NH):
                    act.wait_ge(l2f_max, i * NH + m + 1)
                    for c in range(C2):
                        last = act.activation(t_p[:, m % 2, c, :], by4(6 + m % 2)[:, c, :], ACT.Exp,
                                              bias=t_nmax[:, m % 2, c:c + 1], accum_out=t_sum[:, m % 2, c:c + 1])
                    last.then_inc(l2f_exp, 1)
                    if m:
                        turned_p(m - 1)
                turned_p(NH - 1)

        def l2f_dve(dve, ended):
            weights(dve, 5)

            def body(i, stats, apply):
                dve.wait_ge(l2f_e, i + 1)
                ended(dve.tensor_scalar(t_sig, t_sig, 1.0, None, ALU.add))
                ended(dve.reciprocal(t_sig, t_sig))
                rank_dve(dve, ended, t_sig, t_sel, (t_wide[:, 0], t_wide[:, 1]), TOP2)
                dve.tensor_tensor(t_sc, t_sig, t_sel, ALU.mult).then_inc(l2f_sc, 1)
                for n in range(1, 12, 2):
                    dve.wait_ge(l2f_psum, i * 12 + n + 1)
                    dve.tensor_copy(l2f_out(n), l2f_in(n)).then_inc(l2f_by_dve, 1)
                dve.wait_ge(l2f_scT_psum, i + 1)
                dve.tensor_copy(t_scT, by4(0)[0:H8]).then_inc(l2f_scT, 1)
                dve.wait_ge(l2f_sc, i + 1)

                def normed(m):
                    b, half = divmod(m, 2)
                    dve.wait_ge(l2f_exp, i * NH + m + 1)
                    ended(dve.reciprocal(t_r[:, m % 2, :], t_sum[:, m % 2, :]))
                    ended(dve.tensor_tensor(t_r[:, m % 2, :], t_r[:, m % 2, :], t_sc[:, b, half::2], ALU.mult))
                    dve.tensor_tensor(t_p[:, m % 2, :, :], t_p[:, m % 2, :, :], bc(t_r[:, m % 2, :], C2, -S), ALU.mult)\
                       .then_inc(l2f_p, 1)

                for m in range(NH):
                    dve.wait_ge(l2f_s_psum, i * NH + m + 1)
                    dve.tensor_reduce(t_nmax[:, m % 2, :], by4(6 + m % 2), AX_X, ALU.max, negate=True)\
                       .then_inc(l2f_max, 1)
                    if m:
                        normed(m - 1)
                    if m > 1 and m % 2 == 1:
                        l2f_out_dve(dve, i, m // 2 - 1)
                    if m == 4:
                        stats()
                    if m == 6:
                        apply()
                normed(NH - 1)
                l2f_out_dve(dve, i, GB - 1)
                update_dve(dve, L2F, i, 5)
            over_groups_dve(dve, ended, L2F, 27, body)

        def l2f_out_dve(dve, i, b):
            dve.wait_ge(l2f_oT_psum, i * GB + b + 1)
            dve.tensor_copy(t_oT[:, b % 2, :, :], by4(3 + b % 2)).then_inc(l2f_oT, 1)

        def l2f_pe(pe):
            weights(pe, 5)
            with pe.Fori(0, NG) as i:
                turn_pe(pe, L2F, i)
                begun(pe, L2F, i)
                pe.wait_ge(xnT_ready, turned(L2F) + i + 1)
                for b in range(GB):
                    last = pe.matmul(bank[5][:, b * H8:(b + 1) * H8], xnT[:, b, :], W("l2_Ws"), start=True, stop=True)
                last.then_inc(l2f_gate_psum, 1)
                for n in range(12):
                    if n >= 4:
                        pe.wait_ge((l2f_by_act, l2f_by_dve)[n % 2], i * 6 + (n - 4) // 2 + 1)
                    if n < 2 * C2:
                        w = W(("l2_Wq", "l2_Wk")[n % 2], n // 2 * 128, 128)
                        last = pe.matmul(bank[1 + n % 4][:, :], w, xnT[:, :, :], start=True, stop=True)
                    else:
                        last = pe.matmul(bank[1 + n % 4][:, :], xnT[:, n - 2 * C2, :], W("l2_Wv"), start=True, stop=True)
                    last.then_inc(l2f_psum, 1)

                def scores(m):
                    b, half = divmod(m, 2)
                    rows = slice(DH64 * half, DH64 * (half + 1))
                    if m >= 2:
                        pe.wait_ge(l2f_exp, i * NH + m - 1)
                    for c in range(C2):
                        last = pe.matmul(by4(6 + m % 2)[:, c, :], t_q[rows, c, b * S:(b + 1) * S],
                                         t_k[rows, c, b * S:(b + 1) * S], start=True, stop=True)
                    last.then_inc(l2f_s_psum, 1)

                def turn_p(m):
                    pe.wait_ge(l2f_p, i * NH + m + 1)
                    if m >= 2:
                        pe.wait_ge(l2f_pT, i * NH + m - 1)
                    for c in range(C2):
                        last = pe.transpose(by4(1 + m % 2)[:, c, :], t_p[:, m % 2, c, :], W("ident"))
                    last.then_inc(l2f_pT_psum, 1)

                def weighted(m):
                    b, half = divmod(m, 2)
                    pe.wait_ge(l2f_pT, i * NH + m + 1)
                    if half == 0 and b >= 2:
                        pe.wait_ge(l2f_oT, i * GB + b - 1)
                    for c in range(C2):
                        last = pe.matmul(by4(3 + b % 2)[DH64 * half:DH64 * (half + 1), c, :],
                                         t_v[:, b * H8 + 2 * c + half, :], t_pT[:, m % 2, c, :], start=True, stop=True)
                    if half:
                        last.then_inc(l2f_oT_psum, 1)

                def project(b):
                    pe.wait_ge(l2f_oT, i * GB + b + 1)
                    pe.matmul(by4(5)[:, b, :], t_scT[:, b, :], W("l2_bo"), start=True, stop=False)
                    for c in range(C2):
                        last = pe.matmul(by4(5)[:, b, :], t_oT[:, b % 2, c, :], W("l2_Wo", c * 128, 128),
                                         start=False, stop=(c == C2 - 1))
                    if b == GB - 1:
                        last.then_inc(y_ready, 1)

                pe.wait_ge(l2f_by_act, i * 6 + 6)
                pe.wait_ge(l2f_by_dve, i * 6 + 6)
                scores(0)
                scores(1)
                pe.wait_ge(l2f_sc, i + 1)
                for b in range(GB):
                    last = pe.transpose(by4(0)[0:H8, b, :], t_sc[:, b, :], W("ident"))
                last.then_inc(l2f_scT_psum, 1)
                pe.wait_ge(l2f_scT, i + 1)
                for m in range(NH):
                    if m + 2 < NH:
                        scores(m + 2)
                    turn_p(m)
                    if m:
                        weighted(m - 1)
                    if m % 2 == 0 and m > 2:
                        project(m // 2 - 2)
                weighted(NH - 1)
                project(GB - 2)
                project(GB - 1)

        areas[0] = 0
        c_T = work(GB, S)
        c_q, c_k = work(4, T), work(4, T)
        c_v = work(GB * H16, PADH)
        c_nmax, c_sum, c_r = work(2, 4), work(2, 4), work(2, 4)
        c_p, c_pT = work(2, 4, S), work(2, 4, S)
        c_oT = work(2, 4, S)
        c_mask = work(S, dt=BF16)
        l3a_w_psum, l3a_const, l3a_ctxT, l3a_q_psum, l3a_k_psum, l3a_q, l3a_k, l3a_v_psum, l3a_v, l3a_s_psum, \
            l3a_max, l3a_exp, l3a_p, l3a_pT_psum, l3a_pT, l3a_oT_psum, l3a_oT = (
                sem(f"l3a_{n}") for n in "w_psum const ctxT q_psum k_psum q k v_psum v s_psum "
                "max exp p pT_psum pT oT_psum oT".split())

        def l3a_act(act, ended):
            act.wait_ge(l3a_const, 1)
            with act.Fori(0, NG) as i:
                begun(act, L3A, i)
                act.activation(c_T, group4(ctxT, i), ACT.Copy).then_inc(l3a_ctxT, 1)
                for g in range(4):
                    act.wait_ge(l3a_k_psum, i * 4 + g + 1)
                    act.activation(c_k[:, g, :], bank[4 + g % 2][:, :], ACT.Identity, bias=W("l3_bkP", g, 1))\
                       .then_inc(l3a_k, 1)
                    if g == 1:
                        turned_act(act, L3A, i)

                def turned_p(m):
                    act.wait_ge(l3a_pT_psum, i * NQ + m + 1)
                    act.activation(c_pT[:, m % 2, :, :], by4(6 + m % 2), ACT.Copy).then_inc(l3a_pT, 1)

                for m in range(NQ):
                    act.wait_ge(l3a_max, i * NQ + m + 1)
                    for g in range(4):
                        last = act.activation(c_p[:, m % 2, g, :], by4(4 + m % 2)[:, g, :], ACT.Exp,
                                              bias=c_nmax[:, m % 2, g:g + 1], accum_out=c_sum[:, m % 2, g:g + 1])
                    last.then_inc(l3a_exp, 1)
                    if m:
                        turned_p(m - 1)
                turned_p(NQ - 1)

        def l3a_dve(dve, ended):
            weights(dve, 6)
            dve.wait_ge(l3a_w_psum, 1)
            for k, w in ((1, "l3_WqP"), (2, "l3_WkP"), (3, "l3_WvT")):
                n = WHERE[w][2]
                dve.scalar_tensor_tensor(W(w), bank[k][:, 0:n], LORA_SCALE, W(w), ALU.mult, ALU.add)
            dve.memset(c_v[:, :, :], 0.0)
            dve.wait_ge(imask_loaded, 16)
            dve.tensor_scalar(c_mask, imask[:, :], 0.0, -BIG, ALU.is_equal, ALU.mult).then_inc(l3a_const, 1)
            dve.wait_ge(l3a_const, 1)

            def body(i, stats, apply):
                for g in range(4):
                    dve.wait_ge(l3a_q_psum, i * 4 + g + 1)
                    dve.tensor_scalar(c_q[:, g, :], bank[6 + g % 2][:, :], W("l3_bqP", g, 1), DH8 ** -0.5,
                                      ALU.add, ALU.mult).then_inc(l3a_q, 1)
                dve.wait_ge(l3a_v_psum, i + 1)
                dve.tensor_copy(c_v[:, :, 0:DH8], bank[2][:, :].rearrange("p (n d) -> p n d", d=DH8)).then_inc(l3a_v, 1)

                def normed(m):
                    dve.wait_ge(l3a_exp, i * NQ + m + 1)
                    ended(dve.reciprocal(c_r[:, m % 2, :], c_sum[:, m % 2, :]))
                    dve.tensor_tensor(c_p[:, m % 2, :, :], c_p[:, m % 2, :, :], bc(c_r[:, m % 2, :], 4, -S), ALU.mult)\
                       .then_inc(l3a_p, 1)

                for m in range(NQ):
                    b, j = divmod(m, 4)
                    dve.wait_ge(l3a_s_psum, i * NQ + m + 1)
                    dve.tensor_reduce(c_nmax[:, m % 2, :], by4(4 + m % 2), AX_X, ALU.max, negate=True)\
                       .then_inc(l3a_max, 1)
                    if m:
                        normed(m - 1)
                    if j == 2 and b:
                        l3a_out_dve(dve, i, b - 1)
                    if m == 8:
                        stats()
                    if m == 11:
                        apply()
                normed(NQ - 1)
                l3a_out_dve(dve, i, GB - 1)
                update_dve(dve, L3A, i, 1)
            over_groups_dve(dve, ended, L3A, 19, body)

        def l3a_out_dve(dve, i, b):
            dve.wait_ge(l3a_oT_psum, i * GB + b + 1)
            dve.tensor_copy(c_oT[:, b % 2, :, :], by4(2 + b % 2)).then_inc(l3a_oT, 1)

        def l3a_pe(pe):
            weights(pe, 6)
            begun(pe, L3A, 0)
            pe.matmul(bank[1][:, :], W("l3_Aq"), W("l3_BqP"), start=True, stop=True)
            pe.matmul(bank[2][:, :], W("l3_Ak"), W("l3_BkP"), start=True, stop=True)
            pe.matmul(bank[3][:, 0:128], W("l3_Av"), W("l3_BvT"), start=True, stop=True).then_inc(l3a_w_psum, 1)
            pe.wait_ge(l3a_const, 1)
            with pe.Fori(0, NG) as i:
                begun(pe, L3A, i)
                pe.wait_ge(l3a_ctxT, i + 1)

                def project_k(g):
                    if g >= 2:
                        pe.wait_ge(l3a_k, i * 4 + g - 1)
                    pe.matmul(bank[4 + g % 2][:, :], W("l3_WkP", g * 128, 128), c_T, start=True, stop=True)\
                      .then_inc(l3a_k_psum, 1)

                def project_q(g):
                    if g >= 2:
                        pe.wait_ge(l3a_q, i * 4 + g - 1)
                    pe.matmul(bank[6 + g % 2][:, :], W("l3_WqP", g * 128, 128), xnT[:, :, :], start=True, stop=True)\
                      .then_inc(l3a_q_psum, 1)

                project_k(0)
                project_k(1)
                bias_pe(pe, 2, W("l3_bv"))
                for b in range(GB):
                    last = pe.matmul(by4(2)[:, b, :], c_T[:, b, :], W("l3_WvT"), start=False, stop=(b == GB - 1))
                last.then_inc(l3a_v_psum, 1)
                turn_pe(pe, L3A, i)
                project_k(2)
                project_k(3)
                bias_pe(pe, 1, W("l3_bo"))
                pe.wait_ge(xnT_ready, turned(L3A) + i + 1)
                for g in range(4):
                    project_q(g)

                def scores(m):
                    b, j = divmod(m, 4)
                    if m >= 2:
                        pe.wait_ge(l3a_exp, i * NQ + m - 1)
                    k, rows = 4 + m % 2, slice(PADH * j, PADH * j + DH8)
                    pe.matmul(by4(k), identb[:, :], c_mask.unsqueeze(1).to_broadcast([128, 4, S]),
                              start=True, stop=False)
                    for g in range(4):
                        last = pe.matmul(by4(k)[:, g, :], c_q[rows, g, b * S:(b + 1) * S], c_k[rows, g, b * S:(b + 1) * S],
                                         start=False, stop=(g == 3))
                    last.then_inc(l3a_s_psum, 1)

                def turn_p(m):
                    pe.wait_ge(l3a_p, i * NQ + m + 1)
                    if m >= 2:
                        pe.wait_ge(l3a_pT, i * NQ + m - 1)
                    for g in range(4):
                        last = pe.transpose(by4(6 + m % 2)[:, g, :], c_p[:, m % 2, g, :], W("ident"))
                    last.then_inc(l3a_pT_psum, 1)

                def weighted(m):
                    b, j = divmod(m, 4)
                    pe.wait_ge(l3a_pT, i * NQ + m + 1)
                    if j == 0 and b >= 2:
                        pe.wait_ge(l3a_oT, i * GB + b - 1)
                    for g in range(4):
                        last = pe.matmul(by4(2 + b % 2)[PADH * j:PADH * (j + 1), g, :], c_v[:, b * H16 + 4 * j + g, :],
                                         c_pT[:, m % 2, g, :], start=True, stop=True)
                    if j == 3:
                        last.then_inc(l3a_oT_psum, 1)

                def project(b):
                    pe.wait_ge(l3a_oT, i * GB + b + 1)
                    for g in range(4):
                        last = pe.matmul(by4(1)[:, b, :], c_oT[:, b % 2, g, :], W("l3_WoP", g * 128, 128),
                                         start=False, stop=(b == GB - 1 and g == 3))
                    if b == GB - 1:
                        last.then_inc(y_ready, 1)

                pe.wait_ge(l3a_k, i * 4 + 4)
                pe.wait_ge(l3a_q, i * 4 + 4)
                pe.wait_ge(l3a_v, i + 1)
                scores(0)
                scores(1)
                for m in range(NQ):
                    if m + 2 < NQ:
                        scores(m + 2)
                    turn_p(m)
                    if m:
                        weighted(m - 1)
                    if m % 4 == 3 and m > 4:
                        project(m // 4 - 1)
                weighted(NQ - 1)
                project(GB - 1)

        areas[0] = 0
        g_h = work(C3, T)
        g_tmp = work(FF3)
        g_sum = work(2, 4)
        l3f_sum, l3f_allsum, l3f_w, l3f_psum, l3f_by_act, l3f_by_dve = (
            sem(f"l3f_{n}") for n in "sum allsum w psum by_act by_dve".split())

        def l3f_pool(pool, ended):
            norm_pool(pool, L3F, 0)
            pool.wait_ge(l3f_sum, 1)
            for k in range(2):
                last = pool.partition_all_reduce(g_sum[:, k, 1:2], g_sum[:, k, 0:1], 128, bass.bass_isa.ReduceOp.add)
            last.then_inc(l3f_allsum, 1)
            with pool.Fori(1, NG) as i:
                norm_pool(pool, L3F, i)

        def l3f_act(act, ended):
            with act.Fori(0, NG) as i:
                ended.turn(i, 0)
                turned_act(act, L3F, i)
                for c in (0, 2):
                    act.wait_ge(l3f_psum, i * C3 + c + 1)
                    act.activation(g_h[:, c, :], bank[1 + c][:, :], ACT.Relu, bias=W("l3_b1", c, 1)).then_inc(l3f_by_act, 1)
            ended.loop_over(NG)

        def l3f_dve(dve, ended):
            for k, w in enumerate(("l3_W1T", "l3_W2T")):
                last = dve.tensor_reduce(g_sum[:, k, 0:1], W(w), AX_X, ALU.add, apply_absolute_value=True)
            last.then_inc(l3f_sum, 1)
            dve.wait_ge(l3f_allsum, 1)
            ended(dve.tensor_scalar(g_sum[:, :, 2], g_sum[:, :, 1], 1.0 / (D * FF3), LN_EPS, ALU.mult, ALU.add))
            ended(dve.reciprocal(g_sum[:, :, 3], g_sum[:, :, 2]))
            for k, w in enumerate(("l3_W1T", "l3_W2T")):
                ended(dve.tensor_scalar(g_tmp, W(w), g_sum[:, k, 3:4], ROUND, ALU.mult, ALU.add))
                ended(dve.tensor_scalar(g_tmp, g_tmp, ROUND, -1.0, ALU.subtract, ALU.max))
                dve.tensor_scalar(W(w), g_tmp, 1.0, None, ALU.min).then_inc(l3f_w, 1)
                dve.wait_ge(l3f_w, k + 1)
            ended.straight_over()

            def body(i, stats, apply):
                for c in (1, 3):
                    dve.wait_ge(l3f_psum, i * C3 + c + 1)
                    dve.tensor_scalar(g_h[:, c, :], bank[1 + c][:, :], W("l3_b1", c, 1), 0.0, ALU.add, ALU.max)\
                       .then_inc(l3f_by_dve, 1)
                stats()
                apply()
                update_dve(dve, L3F, i, 5)
            over_groups_dve(dve, ended, L3F, 3, body)

        def l3f_pe(pe):
            pe.wait_ge(l3f_w, 2)
            with pe.Fori(0, NG) as i:
                turn_pe(pe, L3F, i)
                pe.wait_ge(xnT_ready, turned(L3F) + i + 1)
                for c in range(C3):
                    pe.matmul(bank[1 + c][:, :], W("l3_W1T", c * 128, 128), xnT[:, :, :], start=True, stop=True)\
                      .then_inc(l3f_psum, 1)
                begun(pe, L3F, i)
                bias_pe(pe, 5, W("l3_b2"))
                pe.wait_ge(l3f_by_act, i * 2 + 2)
                pe.wait_ge(l3f_by_dve, i * 2 + 2)
                for b in range(GB):
                    for c in range(C3):
                        last = pe.matmul(by4(5)[:, b, :], g_h[:, c, b * S:(b + 1) * S], W("l3_W2T", c * 128, 128),
                                         start=False, stop=(b == GB - 1 and c == C3 - 1))
                last.then_inc(y_ready, 1)

        programs = {
            L0A: (l0a_act, l0a_dve, l0a_pe, lambda pool, ended: norms_pool(pool, L0A)), L0F: (l0f_act, l0f_dve, l0f_pe, l0f_pool),
            L1A: (l1a_act, l1a_dve, l1a_pe, l1a_pool), L1F: (l1f_act, l1f_dve, l1f_pe, lambda pool, ended: norms_pool(pool, L1F)),
            L2A: (l2a_act, l2a_dve, l2a_pe, lambda pool, ended: norms_pool(pool, L2A)), L2F: (l2f_act, l2f_dve, l2f_pe, lambda pool, ended: norms_pool(pool, L2F)),
            L3A: (l3a_act, l3a_dve, l3a_pe, lambda pool, ended: norms_pool(pool, L3A)), L3F: (l3f_act, l3f_dve, l3f_pe, l3f_pool),
        }

        block = stack.enter_context(nc.Block())

        @block.sync
        def _(sp):
            sp.dma_start(x_all[:, :], x_in).then_inc(x_updated, X0)
            first = 0
            for n, name in enumerate(PARTS):
                _, at, cols = WHERE[name]
                sp.dma_start(pack[:, first:at + cols], pack_in[:, first:at + cols]).then_inc(part_loaded[n], 16)
                first = at + cols
                if n == 0:
                    sp.dma_start(cell, cell_in).then_inc(masks_loaded, 16)
                    sp.dma_start(seqm, seq_in.partition_broadcast(128)).then_inc(masks_loaded, 16)
                    sp.dma_start(ctxT[:, :], ctxT_in).then_inc(ctx_loaded, 16)
                    sp.dma_start(ctx[:, :], ctx_in).then_inc(ctx_loaded, 16)
                    sp.dma_start(imask[:, :], imask_in).then_inc(imask_loaded, 16)
            sp.wait_ge(x_updated, X0 + NG * layers)
            sp.dma_start(out, x_all[:, :]).then_inc(stored, 16)
            sp.wait_ge(stored, 16)

        @block.gpsimd
        def _(pool):
            ended = Ended(pool, pool_ended)
            ended(pool.memset(minus_half[:, :], -0.5))
            ended.straight_over()
            for l in range(layers):
                if programs[l][3]:
                    programs[l][3](pool, ended)

        @block.scalar
        def _(act):
            ended = Ended(act, act_ended)
            weights(act, 0)
            act.activation(tg[:, :], W("gates"), ACT.Tanh).then_inc(gates_ready, 1)
            for l in range(layers):
                programs[l][0](act, ended)

        @block.vector
        def _(dve):
            ended = Ended(dve, dve_ended)
            weights(dve, 0)
            ended(dve.tensor_copy(identb[:, :], W("ident")))
            ended.straight_over()
            dve.wait_ge(gates_ready, 1)
            begun(dve, 0, 0)
            for l in range(layers):
                programs[l][1](dve, ended)

        @block.tensor
        def _(pe):
            weights(pe, 0)
            pe.wait_ge(dve_ended, 1)
            for l in range(layers):
                programs[l][2](pe)


def packed(a):
    put = {}

    def t(name):
        return np.asarray(a[name], np.float32).T

    def col(v):
        return np.asarray(v, np.float32).reshape(-1, 1)

    def tiles(w):
        w = np.asarray(w, np.float32)
        return w.reshape(-1, 128, w.shape[1]).transpose(1, 0, 2).reshape(128, -1)

    def spread(w):
        w = np.asarray(w, np.float32)
        out = np.zeros(w.shape[:-1] + (4, 4, PADH), np.float32)
        out[..., :DH8] = w.reshape(w.shape[:-1] + (4, 4, DH8)).swapaxes(-3, -2)
        return out.reshape(w.shape[:-1] + (4, 128))

    put["ident"] = np.eye(128)
    put["ones"] = np.ones((128, 128))
    gates = np.stack([np.asarray(a["g_xattn"]), np.asarray(a["g_ffn"])], 1).reshape(1, 8)
    put["gates"] = np.broadcast_to(gates, (128, 8))
    put["eye8"] = np.repeat(np.eye(8), 128, 1)
    put["l0_WkT"], put["l0_WoT"] = t("L0_xattn_W_k"), t("L0_xattn_W_o")
    put["l0_bk"], put["l0_bo"] = col(a["L0_xattn_b_k"]), np.asarray(a["L0_xattn_b_o"])[None]
    put["l0_gate"], put["l0_up"] = tiles(a["L0_ffn_w_gate"]), tiles(a["L0_ffn_w_up"])
    put["l0_down"] = np.asarray(a["L0_ffn_w_down"])

    pos = np.arange(S, dtype=np.float64)[:, None]
    pair = np.arange(DH8 // 2, dtype=np.float64)
    base = (2 * pair + 0.4 * DH8) / (1.4 * DH8)
    scale = base[None, :] ** (pos / 512.0)
    angle = pos / 10000.0 ** (pair / (DH8 // 2))[None, :]
    gamma = 1.0 - np.exp(np.linspace(math.log(1 / 32), math.log(1 / 512), H16))
    decay = gamma[None, :, None] ** pos[:, :, None]
    sign = np.tile([-1.0, 1.0], DH8 // 2)

    def table(f, scale, decay):
        one = np.repeat(f * scale, 2, axis=1)
        return (one[:, None, :] * decay).reshape(S, D)

    put["cosq"] = table(np.cos(angle), scale, decay)
    put["sinq"] = table(np.sin(angle), scale, decay) * np.tile(sign, H16)
    put["cosk"] = table(np.cos(angle), 1.0 / scale, 1.0 / decay)
    put["sink"] = table(np.sin(angle), 1.0 / scale, 1.0 / decay) * np.tile(sign, H16)
    key, query = np.arange(S)[:, None], np.arange(S)[None, :]
    put["causalT"] = (query >= key).astype(np.float32)
    put["futureT"] = np.where(query >= key, 0.0, -BIG)

    put["l1_dw"] = np.asarray(a["L1_ffn_dw_kernel"]).reshape(128, 3)
    put["l1_dwb"], put["l1_pwb"] = col(a["L1_ffn_dw_bias"]), col(a["L1_ffn_pw_b"])
    put["l1_pwT"], put["l1_routerT"] = t("L1_ffn_pw_w"), t("L1_ffn_router_w")
    put["l1_routerb"] = np.broadcast_to(np.asarray(a["L1_ffn_router_b"])[None], (128, E1))
    put["l1_expertT"] = np.asarray(a["L1_ffn_expert_w"]).transpose(2, 0, 1).reshape(128, -1)
    put["l1_expertb"] = t("L1_ffn_expert_b")
    put["l1_outT"], put["l1_outb"] = t("L1_ffn_out_w"), col(a["L1_ffn_out_b"])
    put["l1_norm"] = col(a["L1_ffn_norm_w"])
    put["l1_downT"], put["l1_downb"] = t("L1_ffn_ff_down_w"), col(a["L1_ffn_ff_down_b"])
    put["l1_upT"], put["l1_upb"] = t("L1_ffn_ff_up_w"), col(a["L1_ffn_ff_up_b"])
    e, j = np.arange(8)[:, None], np.arange(8)[None, :]
    put["before"] = np.broadcast_to((j < e).astype(np.float32).reshape(1, 64), (128, 64))

    def gate_w(w):
        return np.asarray(w).reshape(H4, 3, 128).transpose(2, 1, 0).reshape(128, -1)

    put["l2_igT"], put["l2_fgT"] = gate_w(a["L2_xattn_igate_w"]), gate_w(a["L2_xattn_fgate_w"])
    put["l2_igb"], put["l2_fgb"] = col(a["L2_xattn_igate_b"]), col(a["L2_xattn_fgate_b"])
    put["l2_outw"] = np.broadcast_to(np.asarray(a["L2_xattn_out_w"])[None], (128, 128))
    first = (np.arange(T) % S == 0)[None]
    put["keep"] = np.broadcast_to(np.where(first, 0.0, 1.0), (H4, T))
    put["restart"] = np.broadcast_to(np.where(first, -BIG, 0.0), (H4, T))
    kv = np.asarray(a["L2_ffn_Wkv"])
    put["l2_Wq"], put["l2_Wk"], put["l2_Wv"] = np.asarray(a["L2_ffn_Wq"]), kv[:, :512], kv[:, 512:]
    put["l2_Ws"], put["l2_bo"] = np.asarray(a["L2_ffn_Ws"]), np.asarray(a["L2_ffn_bo"])
    put["l2_Wo"] = tiles(np.asarray(a["L2_ffn_Wo"]).reshape(512, 128))

    put["l3_WqP"], put["l3_WkP"] = (spread(t(n)).reshape(128, -1) for n in ("L3_xattn_Wq", "L3_xattn_Wk"))
    put["l3_WvT"] = t("L3_xattn_Wv")
    put["l3_WoP"] = spread(np.asarray(a["L3_xattn_Wo"])).transpose(2, 1, 0).reshape(128, -1)
    for n in "qkv":
        put[f"l3_A{n}"] = np.asarray(a[f"L3_xattn_A{n}"])
    put["l3_BqP"], put["l3_BkP"] = (spread(t(n)).reshape(RANK, -1) for n in ("L3_xattn_Bq", "L3_xattn_Bk"))
    put["l3_BvT"] = t("L3_xattn_Bv")
    put["l3_bqP"], put["l3_bkP"] = spread(a["L3_xattn_bq"]).T, spread(a["L3_xattn_bk"]).T
    put["l3_bv"], put["l3_bo"] = np.asarray(a["L3_xattn_bv"])[None], np.asarray(a["L3_xattn_bo"])[None]
    put["l3_W1T"], put["l3_b1"] = t("L3_ffn_W1"), np.asarray(a["L3_ffn_b1"]).reshape(C3, 128).T
    put["l3_W2T"], put["l3_b2"] = tiles(t("L3_ffn_W2")), np.asarray(a["L3_ffn_b2"])[None]

    out = np.zeros((128, COLS), np.float32)
    for name, p, n in pieces():
        _, at, _ = WHERE[name]
        out[:p, at:at + n] = put[name]
    return out


def kernel(**inputs):
    import concourse.bacc as bacc
    from concourse.bass_utils import run_bass_kernel_spmd

    a = {k: np.asarray(v) for k, v in inputs.items()}

    def tokens(v):
        return np.ascontiguousarray(v.transpose(1, 0, 2).reshape(128, -1))

    imask = a["mask_1x1xSxS2_if1"].reshape(S, S)
    arrays = {
        "x": tokens(a["x"]), "ctx": tokens(a["ctx_1024"]),
        "ctxT": np.ascontiguousarray(a["ctx_1024"].transpose(2, 0, 1).reshape(128, -1)),
        "cell": tokens(a["mask_BxSxS2_ff1"]), "seq": np.ascontiguousarray(a["mask_BxS2_ff1"].reshape(-1)),
        "imask": np.ascontiguousarray(imask),
        "pack": packed(a),
    }
    nc = bacc.Bacc("TRN2", target_bir_lowering=False, num_devices=1)
    aps = [nc.dram_tensor(f"in_{n}", v.shape, mybir.dt.from_np(v.dtype), kind="ExternalInput").ap()
           for n, v in arrays.items()]
    out = nc.dram_tensor("out", (128, B * D), F32, kind="ExternalOutput").ap()
    build(nc, *aps, out)
    r = run_bass_kernel_spmd(nc, [{f"in_{n}": v for n, v in arrays.items()}], core_ids=[0])
    got = r.results[0]["out"]
    return got.reshape(S, B, D).transpose(1, 0, 2)
```

```python
from contextlib import ExitStack
import math

import numpy as np

import concourse.bass as bass
from concourse import mybir

ALU = mybir.AluOpType
ACT = mybir.ActivationFunctionType
F32 = mybir.dt.float32
BF16 = mybir.dt.bfloat16
I32 = mybir.dt.int32
AX_X = mybir.AxisListType.X

B, S, D = 16, 128, 128
GB = 4
NG = B // GB
T = GB * S
LAYERS = 8
L0A, L0F, L1A, L1F, L2A, L2F, L3A, L3F = range(LAYERS)
LN_EPS = 1e-5

FF0, BLOCK = 384, 32
C0 = FF0 // 128
QMAX16, QMAX4 = 32767.0, 7.0
ROUND = 1.5 * 2.0 ** 23

H16, DH8 = 16, 8
PADH = 32
NQ = GB * 4
E1, TOP1, HID1 = 8, 2, 32
RMS_EPS = 1e-6
H4, DH32 = 4, 32
MLSTM_EPS = 1e-8
H8, DH64, TOP2 = 8, 64, 3
C2 = H8 * DH64 // 128
RANK = 8
LORA_SCALE = 16.0 / 8.0
FF3 = 512
C3 = FF3 // 128
X0 = 16
BIG = 1e30


def pieces():
    return [
        ("ident", 128, 128), ("ones", 128, 128), ("gates", 128, 8), ("eye8", 8, 8 * 128),
        ("l0_WkT", 128, 128), ("l0_bk", 128, 1), ("l0_WoT", 128, 128), ("l0_bo", 1, 128),
        ("l0_gate", 128, C0 * 128), ("l0_up", 128, C0 * 128), ("l0_down", 128, FF0),
        ("cosq", 128, 128), ("sinq", 128, 128), ("cosk", 128, 128), ("sink", 128, 128),
        ("causalT", 128, 128),
        ("l1_dw", 128, 3), ("l1_dwb", 128, 1), ("l1_pwT", 128, 128), ("l1_pwb", 128, 1),
        ("l1_routerT", 128, E1), ("l1_routerb", 128, E1), ("l1_expertT", 128, E1 * 128),
        ("l1_expertb", 128, E1), ("l1_outT", 128, 128), ("l1_outb", 128, 1), ("l1_norm", 128, 1),
        ("l1_downT", 128, HID1), ("l1_downb", HID1, 1), ("l1_upT", HID1, 128), ("l1_upb", 128, 1),
        ("before", 128, 64),
        ("l2_igT", 128, 3 * H4), ("l2_fgT", 128, 3 * H4), ("l2_igb", H4, 1), ("l2_fgb", H4, 1),
        ("l2_outw", 128, 128), ("keep", H4, T), ("restart", H4, T), ("futureT", 128, 128),
        ("l2_Wq", 128, 512), ("l2_Wk", 128, 512), ("l2_Wv", 128, 512), ("l2_Ws", 128, H8),
        ("l2_Wo", 128, C2 * 128), ("l2_bo", H8, 128),
        ("l3_WqP", 128, 512), ("l3_WkP", 128, 512), ("l3_WvT", 128, 128),
        ("l3_Aq", RANK, 128), ("l3_Ak", RANK, 128), ("l3_Av", RANK, 128),
        ("l3_BqP", RANK, 512), ("l3_BkP", RANK, 512), ("l3_BvT", RANK, 128),
        ("l3_bqP", 128, 4), ("l3_bkP", 128, 4), ("l3_bv", 1, 128), ("l3_WoP", 128, 512),
        ("l3_bo", 1, 128),
        ("l3_W1T", 128, FF3), ("l3_b1", 128, C3), ("l3_W2T", 128, C3 * 128), ("l3_b2", 1, 128),
    ]


def columns():
    at, where = 0, {}
    for name, p, n in pieces():
        where[name] = (p, at, n)
        at += n
    return where, at


WHERE, COLS = columns()
PARTS = ["l0_bo", "l0_down", "causalT", "before", "futureT", "l2_bo", "l3_b2"]


class Ended:

    def __init__(self, eng, sem):
        self.eng, self.sem, self.total, self.base, self.n = eng, sem, 0, 0, 0

    def __call__(self, ins):
        self.n += 1
        ins.then_inc(self.sem, 1)
        self.eng.wait_ge(self.sem, self.base + self.n)

    def turn(self, i, per):
        self.base, self.n, self.per = self.total + i * per, 0, per

    def loop_over(self, turns):
        assert self.n == self.per, f"{self.n} in one turn, not {self.per}"
        self.total += turns * self.per
        self.base, self.n = self.total, 0

    def straight_over(self):
        self.total += self.n
        self.base, self.n = self.total, 0


def build(nc, x_in, ctx_in, ctxT_in, cell_in, seq_in, imask_in, pack_in, out, layers=LAYERS):
    with ExitStack() as stack:
        def sb(name, shape, dt=F32):
            return stack.enter_context(nc.sbuf_tensor(name, shape, dt))

        def sem(name):
            return stack.enter_context(nc.semaphore(name))

        x_all = sb("x_all", [128, B * D])
        ctx = sb("ctx", [128, B * D])
        ctxT = sb("ctxT", [128, B * S])
        pack = sb("pack", [128, COLS])
        tg = sb("tg", [128, LAYERS])
        identb = sb("identb", [128, 128], BF16)
        imask = sb("imask", [128, S], I32)

        def W(name, a=0, n=None):
            p, at, cols = WHERE[name]
            return pack[0:p, at + a:at + (cols if n is None else a + n)]

        stats = sb("stats", [128, GB, 6])
        moment = sb("moment", [128, GB, 3])
        mean = sb("mean", [128, GB])
        var = sb("var", [128, GB])              
        rstd = sb("rstd", [128, GB])
        minus_half = sb("minus_half", [128, 16])
        xn = sb("xn", [128, GB, D])
        xnT = sb("xnT", [128, GB, S])
        k_rot = sb("k_rot", [128, B * D])
        kr_t = sb("kr_t", [128, GB, D])
        kr_r = sb("kr_r", [128, GB, D])
        area = sb("area", [128, 24576])
        areas = [0]

        def work(*shape, p=128, dt=F32):
            n = int(np.prod(shape)) // (2 if dt == BF16 else 1)
            a = area[0:p, areas[0]:areas[0] + n]
            areas[0] += n
            assert areas[0] <= 24576
            if dt == BF16:
                a = a.bitcast(BF16)
            if len(shape) == 2:
                a = a.rearrange("p (a b) -> p a b", a=shape[0])
            if len(shape) == 3:
                a = a.rearrange("p (a b c) -> p a b c", a=shape[0], b=shape[1])
            return a

        bank = [stack.enter_context(nc.psum_tensor(f"bank{k}", [128, 512], F32)) for k in range(8)]

        def by4(k):
            return bank[k][:, :].rearrange("p (b s) -> p b s", b=GB)

        ctx_loaded = sem("ctx_loaded")
        masks_loaded = sem("masks_loaded")
        imask_loaded = sem("imask_loaded")
        part_loaded = [sem(f"part{n}_loaded") for n in range(len(PARTS))]
        x_updated = sem("x_updated")
        ln_var = sem("ln_var")
        ln_rstd = sem("ln_rstd")
        xn_ready = sem("xn_ready")
        xnT_psum = sem("xnT_psum")
        xnT_ready = sem("xnT_ready")
        y_ready = sem("y_ready")
        gates_ready = sem("gates_ready")
        dve_ended = sem("dve_ended")
        act_ended = sem("act_ended")
        pool_ended = sem("pool_ended")
        stored = sem("stored")

        def weights(eng, layer_part):
            eng.wait_ge(part_loaded[layer_part], 16)

        def group(t, i, b=0, n=GB):
            return t[:, bass.ds(i * T + b * 128, n * 128)]

        def group4(t, i):
            return group(t, i).rearrange("p (b d) -> p b d", b=GB)

        def norm_stats_dve(dve, ended, l, i):
            for b in range(GB):
                last = dve.bn_stats(stats[:, b, :], group(x_all, i, b, 1))
            ended(last)
            even, odd = stats[:, :, 1:3], stats[:, :, 4:6]
            dve.tensor_tensor(moment[:, :, 0:2], even, odd, ALU.add)
            ended(dve.tensor_tensor(moment[:, :, 2], even[:, :, 0], odd[:, :, 0], ALU.subtract))
            dve.tensor_scalar(mean[:, :], moment[:, :, 0], 0.5, None, ALU.mult)
            dve.tensor_scalar(var[:, :], moment[:, :, 1], 1.0 / D, LN_EPS, ALU.mult, ALU.add)
            ended(dve.tensor_tensor(moment[:, :, 2], moment[:, :, 2], moment[:, :, 2], ALU.mult))
            dve.scalar_tensor_tensor(var[:, :], moment[:, :, 2], 0.25, var[:, :], ALU.mult, ALU.add).then_inc(ln_var, 1)

        def norm_apply_dve(dve, ended, l, i, dst=lambda b: xn[:, b, :]):
            dve.wait_ge(ln_rstd, 4 * l + i + 1)
            for b in range(GB):
                last = dve.tensor_scalar(dst(b), group(x_all, i, b, 1), mean[:, b:b + 1],
                                         rstd[:, b:b + 1], ALU.subtract, ALU.mult)
            last.then_inc(xn_ready, 1)
            dve.wait_ge(xn_ready, 4 * l + i + 1)

        def over_groups_dve(dve, ended, l, per, body):
            def norms(l, i):
                return (lambda: norm_stats_dve(dve, ended, l, i)), (lambda: norm_apply_dve(dve, ended, l, i))

            def nothing():
                pass

            if l in (L0A, L1A):
                for step in norms(l, 0):
                    step()
                ended.straight_over()
            with dve.Fori(0, NG - 1) as i:
                ended.turn(i, per)
                body(i, *norms(l, i + 1))
            ended.loop_over(NG - 1)
            body(NG - 1, *(norms(l + 1, 0) if l not in (L0A, L3F) and l + 1 < layers else (nothing, nothing)))
            ended.straight_over()

        def norm_pool(pool, l, i):
            pool.wait_ge(ln_var, 4 * l + i + 1)
            pool.tensor_tensor(rstd[:, :], var[:, :], minus_half[:, 0:GB], ALU.pow).then_inc(ln_rstd, 1)

        def norms_pool(pool, l):
            with pool.Fori(0, NG) as i:
                norm_pool(pool, l, i)

        def turned(l):
            return 4 * (l if l < L1A else l - 1)

        def turn_pe(pe, l, i, src=xn, ready=xn_ready):
            pe.wait_ge(ready, (4 * l if ready is xn_ready else 0) + i + 1)
            for b in range(GB):
                last = pe.transpose(by4(0)[:, b, :], src[:, b, :], W("ident"))
            last.then_inc(xnT_psum, 1)

        def turned_act(act, l, i, dst=None):
            act.wait_ge(xnT_psum, turned(l) + i + 1)
            act.activation(xnT[:, :, :] if dst is None else dst, by4(0), ACT.Copy).then_inc(xnT_ready, 1)

        def update_dve(dve, l, i, k=None, src=None):
            dve.wait_ge(y_ready, 4 * l + i + 1)
            xs = group(x_all, i)
            dve.scalar_tensor_tensor(xs, bank[k][:, :] if src is None else src, tg[:, l:l + 1], xs,
                                     ALU.mult, ALU.add).then_inc(x_updated, 1)
            dve.wait_ge(x_updated, X0 + 4 * l + i + 1)

        def bias_pe(pe, k, row):
            pe.matmul(bank[k][:, :], W("ones")[0:1, :],
                      row.unsqueeze(1).to_broadcast([1, GB, 128]), start=True, stop=False)

        def begun(eng, l, i):
            eng.wait_ge(x_updated, X0 + 4 * l + i)

        def bc(ap, *shape):
            for axis, n in enumerate(shape):
                if n < 0:
                    ap = ap.unsqueeze(axis + 1)
            return ap.to_broadcast([ap.shape[0], *map(abs, shape)])

        def rank_dve(dve, ended, logit, sel, wide, top):
            lj = logit.unsqueeze(2).to_broadcast([128, GB, 8, 8])
            le = logit.unsqueeze(3).to_broadcast([128, GB, 8, 8])
            before = W("before").rearrange("p (e j) -> p e j", e=8).unsqueeze(1).to_broadcast([128, GB, 8, 8])
            gt, ge = wide[0], wide[1]
            dve.tensor_tensor(gt, lj, le, ALU.is_gt)
            ended(dve.tensor_tensor(ge, lj, le, ALU.is_ge))
            ended(dve.tensor_tensor(ge, ge, gt, ALU.subtract))
            ended(dve.tensor_tensor(ge, ge, before, ALU.mult))
            ended(dve.tensor_tensor(gt, gt, ge, ALU.add))
            ended(dve.tensor_reduce(sel, gt, AX_X, ALU.add))
            ended(dve.tensor_scalar(sel, sel, float(top), None, ALU.is_lt))

        areas[0] = 0
        cell, seqm = work(B * S), work(B * S)
        a_kT, a_s, a_p, a_pT, a_o, a_oT = (work(GB, 128) for _ in range(6))
        a_nmax, a_sum, a_rsum = work(GB), work(GB), work(GB)
        l0a_logs, l0a_k_psum, l0a_k, l0a_s_psum, l0a_masked, l0a_p, l0a_pT_psum, l0a_pT, l0a_o_psum, l0a_o, \
            l0a_oT_psum, l0a_oT = (sem(f"l0a_{n}") for n in "logs k_psum k s_psum masked p pT_psum pT o_psum o "
                                   "oT_psum oT".split())

        def l0a_act(act, ended):
            act.wait_ge(masks_loaded, 32)
            act.activation(cell, cell, ACT.Ln)
            act.activation(seqm, seqm, ACT.Ln).then_inc(l0a_logs, 1)
            with act.Fori(0, NG) as i:
                ended.turn(i, 0)
                turned_act(act, L0A, i)
                act.wait_ge(l0a_masked, i + 1)
                for b in range(GB):
                    last = act.activation(a_p[:, b, :], a_s[:, b, :], ACT.Exp, bias=a_nmax[:, b:b + 1],
                                          accum_out=a_sum[:, b:b + 1])
                last.then_inc(l0a_p, 1)
                act.wait_ge(l0a_oT_psum, i + 1)
                act.activation(a_oT, by4(5), ACT.Copy).then_inc(l0a_oT, 1)
            ended.loop_over(NG)

        def l0a_dve(dve, ended):
            dve.wait_ge(l0a_logs, 1)
            ended(dve.tensor_tensor(cell, cell, seqm, ALU.add))
            ended.straight_over()

            def body(i, stats, apply):
                dve.wait_ge(l0a_k_psum, i + 1)
                dve.tensor_scalar(a_kT, by4(1), W("l0_bk"), None, ALU.add).then_inc(l0a_k, 1)
                dve.wait_ge(l0a_s_psum, i + 1)
                ended(dve.tensor_tensor(a_s, by4(2), group4(cell, i), ALU.add))
                dve.tensor_reduce(a_nmax, a_s, AX_X, ALU.max, negate=True).then_inc(l0a_masked, 1)
                stats()
                dve.wait_ge(l0a_pT_psum, i + 1)
                dve.tensor_copy(a_pT, by4(3)).then_inc(l0a_pT, 1)
                apply()
                dve.wait_ge(l0a_p, i + 1)
                ended(dve.reciprocal(a_rsum, a_sum))
                dve.wait_ge(l0a_o_psum, i + 1)
                dve.tensor_tensor(a_o, by4(4), bc(a_rsum, GB, -128), ALU.mult).then_inc(l0a_o, 1)
                update_dve(dve, L0A, i, 6)
            over_groups_dve(dve, ended, L0A, 5, body)

        def l0a_pe(pe):
            pe.wait_ge(ctx_loaded, 32)
            with pe.Fori(0, NG) as i:
                turn_pe(pe, L0A, i)
                begun(pe, L0A, i)
                pe.matmul(bank[1][:, :], W("l0_WkT"), group(ctxT, i), start=True, stop=True).then_inc(l0a_k_psum, 1)
                pe.wait_ge(l0a_k, i + 1)
                pe.wait_ge(xnT_ready, turned(L0A) + i + 1)
                for b in range(GB):
                    last = pe.matmul(by4(2)[:, b, :], xnT[:, b, :], a_kT[:, b, :], start=True, stop=True)
                last.then_inc(l0a_s_psum, 1)
                pe.wait_ge(l0a_p, i + 1)
                for b in range(GB):
                    last = pe.transpose(by4(3)[:, b, :], a_p[:, b, :], W("ident"))
                last.then_inc(l0a_pT_psum, 1)
                pe.wait_ge(l0a_pT, i + 1)
                for b in range(GB):
                    last = pe.matmul(by4(4)[:, b, :], a_pT[:, b, :], group(ctx, i, b, 1), start=True, stop=True)
                last.then_inc(l0a_o_psum, 1)
                pe.wait_ge(l0a_o, i + 1)
                for b in range(GB):
                    last = pe.transpose(by4(5)[:, b, :], a_o[:, b, :], W("ident"))
                last.then_inc(l0a_oT_psum, 1)
                bias_pe(pe, 6, W("l0_bo"))
                pe.wait_ge(l0a_oT, i + 1)
                for b in range(GB):
                    last = pe.matmul(by4(6)[:, b, :], a_oT[:, b, :], W("l0_WoT"), start=False, stop=(b == GB - 1))
                last.then_inc(y_ready, 1)

        areas[0] = 0
        GW = C0 * T
        f_xn = work(B * D)
        f_gate, f_up, f_sig = (work(NG * GW) for _ in range(3))
        f_t, f_q = work(T), work(C0, T)
        f_s = f_q.rearrange("p c t -> p (c t)")
        f_unit = work(1)
        f_wmax, f_winv = work(3 * FF0 // BLOCK), work(3 * FF0 // BLOCK)
        f_wT = work(9, 128)
        f_amax, f_scale = work(5, 12), work(5, 4)
        l0f_w, l0f_wT_psum, l0f_wT, l0f_max, l0f_allmax, l0f_xq, l0f_psum, l0f_copied, l0f_gq, l0f_sig, l0f_u, \
            l0f_scaled, l0f_t2, l0f_t3, l0f_t4, l0f_oq = (
                sem(f"l0f_{n}") for n in "w wT_psum wT max allmax xq psum copied gq sig u scaled t2 t3 t4 oq".split())

        def l0f_scale_dve(dve, ended, k, n, unit=None):
            dve.tensor_reduce(f_scale[:, k, 0:1], f_amax[:, k, 0:n], AX_X, ALU.max).then_inc(l0f_max, 1)
            dve.wait_ge(l0f_allmax, k + 1)
            if unit is not None:
                ended(dve.tensor_tensor(f_scale[:, k, 1:2], f_scale[:, k, 1:2], unit, ALU.mult))
            ended(dve.tensor_scalar(f_scale[:, k, 2:3], f_scale[:, k, 1:2], 1.0 / QMAX16, 1e-12, ALU.mult, ALU.max))
            last = dve.reciprocal(f_scale[:, k, 3:4], f_scale[:, k, 2:3])
            if unit is not None:
                ended(last)
                last = dve.tensor_tensor(f_scale[:, k, 3:4], f_scale[:, k, 3:4], unit, ALU.mult)
            last.then_inc(l0f_scaled, 1)
            dve.wait_ge(l0f_scaled, k + 1)

        def l0f_round_dve(dve, ended, k, dst, src, tmp):
            ended(dve.tensor_scalar(tmp, src, f_scale[:, k, 3:4], ROUND, ALU.mult, ALU.add))
            return dve.tensor_scalar(dst, tmp, ROUND, f_scale[:, k, 2:3], ALU.subtract, ALU.mult)

        def l0f_group(t, i):
            return t[:, bass.ds(i * GW, GW)]

        def l0f_pool(pool, ended):
            norms_pool(pool, L0F)
            for k in range(5):
                pool.wait_ge(l0f_max, k + 1)
                pool.partition_all_reduce(f_scale[:, k, 1:2], f_scale[:, k, 0:1], 128,
                                          bass.bass_isa.ReduceOp.max).then_inc(l0f_allmax, 1)

        def l0f_round_act(act, k, dst, src):
            return act.activation(dst, src, ACT.Identity, scale=f_scale[:, k, 3:4], bias=ROUND)

        def l0f_act(act, ended):
            for k in range(3):
                act.wait_ge(l0f_wT_psum, k + 1)
                act.activation(f_wT[:, 3 * k:3 * k + 3, :], by4(1 + k)[:, 0:3, :], ACT.Copy).then_inc(l0f_wT, 1)
            with act.Fori(0, NG) as i:
                turned_act(act, L0F, i)
                for c in range(2 * C0):
                    act.wait_ge(l0f_psum, i * 2 * C0 + c + 1)
                    act.activation((f_gate, f_up)[c // C0][:, bass.ds(i * GW + c % C0 * T, T)], bank[1 + c][:, :],
                                   ACT.Copy).then_inc(l0f_copied, 1)
            with act.Fori(0, NG) as i:
                ended.turn(i, 1)
                act.wait_ge(l0f_gq, i + 1)
                ended(act.activation(f_s, l0f_group(f_gate, i), ACT.Sigmoid))
                act.activation(l0f_group(f_sig, i), f_s, ACT.Identity, scale=65536.0, bias=ROUND).then_inc(l0f_sig, 1)
                act.wait_ge(l0f_sig, i + 1)
                l0f_round_act(act, 2, l0f_group(f_up, i), l0f_group(f_up, i)).then_inc(l0f_t2, 1)
            ended.loop_over(NG)
            act.wait_ge(l0f_t2, NG)
            with act.Fori(0, NG) as i:
                act.activation(l0f_group(f_up, i), l0f_group(f_up, i), ACT.Identity, bias=-ROUND).then_inc(l0f_u, 1)
            for k, done in ((3, l0f_t3), (4, l0f_t4)):
                act.wait_ge(l0f_scaled, k + 1)
                with act.Fori(0, NG) as i:
                    l0f_round_act(act, k, l0f_group(f_gate, i), l0f_group(f_gate, i)).then_inc(done, 1)

        def l0f_dve(dve, ended):
            weights(dve, 1)
            dve.wait_ge(x_updated, X0 + 4 * L0F)
            w = W("l0_gate")
            _, at, _ = WHERE["l0_gate"]
            w3 = pack[:, at:at + 3 * FF0].rearrange("p (n k) -> p n k", k=BLOCK)
            n = 3 * FF0 // BLOCK
            ended(dve.tensor_reduce(f_wmax, w3, AX_X, ALU.max, apply_absolute_value=True))
            ended(dve.tensor_scalar(f_wmax, f_wmax, 1.0 / QMAX4, 1e-12, ALU.mult, ALU.max))
            ended(dve.reciprocal(f_winv, f_wmax))
            ended(dve.tensor_tensor(w3, w3, bc(f_winv, n, -BLOCK), ALU.mult))
            ended(dve.tensor_scalar(w3, w3, ROUND, ROUND, ALU.add, ALU.subtract))
            ended(dve.tensor_scalar(w3, w3, -QMAX4 - 1.0, QMAX4, ALU.max, ALU.min))
            dve.tensor_tensor(w3, w3, bc(f_wmax, n, -BLOCK), ALU.mult).then_inc(l0f_w, 1)
            ended.straight_over()
            with dve.Fori(0, NG) as i:
                ended.turn(i, 4)
                norm_stats_dve(dve, ended, L0F, i)
                norm_apply_dve(dve, ended, L0F, i, lambda b: group(f_xn, i, b, 1))
                ended(dve.tensor_reduce(f_amax[:, 0, bass.ds(i, 1)], group(f_xn, i), AX_X, ALU.max,
                                        apply_absolute_value=True))
            ended.loop_over(NG)
            l0f_scale_dve(dve, ended, 0, NG)
            ended.straight_over()
            with dve.Fori(0, NG) as i:
                ended.turn(i, 3)
                l0f_round_dve(dve, ended, 0, xn[:, :, :].rearrange("p b d -> p (b d)"), group(f_xn, i), f_t)\
                    .then_inc(l0f_xq, 1)
                for k, t in ((1, f_gate), (2, f_up)):
                    dve.wait_ge(l0f_copied, (i * 2 + k) * C0)
                    ended(dve.tensor_reduce(f_amax[:, k, bass.ds(i, 1)], l0f_group(t, i), AX_X, ALU.max,
                                            apply_absolute_value=True))
            ended.loop_over(NG)
            l0f_scale_dve(dve, ended, 1, NG)
            l0f_scale_dve(dve, ended, 2, NG)
            ended.straight_over()
            with dve.Fori(0, NG) as i:
                ended.turn(i, 1)
                g = l0f_group(f_gate, i)
                l0f_round_dve(dve, ended, 1, g, g, g).then_inc(l0f_gq, 1)
            ended.loop_over(NG)
            with dve.Fori(0, NG) as i:
                ended.turn(i, 3)
                g = l0f_group(f_gate, i)
                s = l0f_group(f_sig, i)
                dve.wait_ge(l0f_sig, i + 1)
                ended(dve.tensor_scalar(s, s, ROUND, 65535.0, ALU.subtract, ALU.min))
                ended(dve.scalar_tensor_tensor(g, s, 1.0 / 65536.0, g, ALU.mult, ALU.mult))
                ended(dve.tensor_reduce(f_amax[:, 3, bass.ds(i, 1)], g, AX_X, ALU.max, apply_absolute_value=True))
            ended.loop_over(NG)
            l0f_scale_dve(dve, ended, 3, NG)
            ended(dve.tensor_tensor(f_unit, f_scale[:, 3, 2:3], f_scale[:, 2, 2:3], ALU.mult))
            ended.straight_over()
            dve.wait_ge(l0f_u, NG)
            with dve.Fori(0, NG) as i:
                ended.turn(i, 2)
                g = l0f_group(f_gate, i)
                dve.wait_ge(l0f_t3, i + 1)
                ended(dve.scalar_tensor_tensor(g, g, ROUND, l0f_group(f_up, i), ALU.subtract, ALU.mult))
                ended(dve.tensor_reduce(f_amax[:, 4, bass.ds(i, 1)], g, AX_X, ALU.max, apply_absolute_value=True))
            ended.loop_over(NG)
            l0f_scale_dve(dve, ended, 4, NG, unit=f_unit)
            ended.straight_over()
            with dve.Fori(0, NG) as i:
                dve.wait_ge(l0f_t4, i + 1)
                dve.tensor_scalar(f_q.rearrange("p c t -> p (c t)"), l0f_group(f_gate, i), ROUND,
                                  f_scale[:, 4, 2:3], ALU.subtract, ALU.mult).then_inc(l0f_oq, 1)
                update_dve(dve, L0F, i, 1)

        def l0f_pe(pe):
            pe.wait_ge(l0f_w, 1)
            w = pack[:, WHERE["l0_gate"][1]:][:, 0:3 * FF0].rearrange("p (n k) -> p n k", k=128)
            for k in range(3):
                for c in range(3):
                    last = pe.transpose(by4(1 + k)[:, c, :], w[:, 3 * k + c, :], W("ident"))
                last.then_inc(l0f_wT_psum, 1)
            pe.wait_ge(l0f_wT, 3)
            with pe.Fori(0, NG) as i:
                turn_pe(pe, L0F, i, ready=l0f_xq)
                pe.wait_ge(xnT_ready, turned(L0F) + i + 1)
                for c in range(2 * C0):
                    pe.matmul(bank[1 + c][:, :], f_wT[:, c, :], xnT[:, :, :], start=True, stop=True)\
                      .then_inc(l0f_psum, 1)
            with pe.Fori(0, NG) as i:
                pe.wait_ge(l0f_oq, i + 1)
                for b in range(GB):
                    for c in range(C0):
                        last = pe.matmul(by4(1)[:, b, :], f_q[:, c, b * 128:b * 128 + 128], f_wT[:, 6 + c, :],
                                         start=(c == 0), stop=(c == C0 - 1))
                last.then_inc(y_ready, 1)

        HALF = 512
        NK = 2 * GB
        areas[0] = 0
        r_kv = work(NK, HALF)
        r_t, r_r, r_q, r_o = (work(GB, D) for _ in range(4))
        r_m = work(2, HALF)
        l1a_k, l1a_q, l1a_kv, l1a_sum_psum, l1a_m, l1a_o = (
            sem(f"l1a_{n}") for n in "k q kv sum_psum m o".split())

        def pairs(ap, k):
            return ap.rearrange("p b (h two) -> p b h two", two=2)[:, :, :, k]

        def pairs2(ap, k):
            return ap.rearrange("p (h two) -> p h two", two=2)[:, :, k].unsqueeze(1).to_broadcast([128, GB, 64])

        def l1a_rotate(eng, ended, src, cos, sin, t, r, dst):
            c = W(cos).unsqueeze(1).to_broadcast([128, GB, D])
            eng.tensor_tensor(t, src, c, ALU.mult)
            eng.tensor_tensor(pairs(r, 0), pairs(src, 1), pairs2(W(sin), 0), ALU.mult)
            ended(eng.tensor_tensor(pairs(r, 1), pairs(src, 0), pairs2(W(sin), 1), ALU.mult))
            return eng.tensor_tensor(dst, t, r, ALU.add)

        def l1a_half(ap, n, last):
            b, half = divmod(n, 2)
            a = ap[:, b * D + half * 64:b * D + half * 64 + 64].rearrange("p (h f) -> p h f", h=8)
            return a.unsqueeze(3 if last else 2).to_broadcast([128, 8, DH8, DH8])

        def l1a_ahead_pool(pool, ended):
            weights(pool, 2)
            pool.wait_ge(ctx_loaded, 32)
            with pool.Fori(0, NG) as i:
                ended.turn(i, 2)
                norm_pool(pool, L0A, i)
                ended(l1a_rotate(pool, ended, group4(ctx, i), "cosk", "sink", kr_t[:, :, :], kr_r[:, :, :],
                                 group4(k_rot, i)))
            ended.loop_over(NG)

        def l1a_pool(pool, ended):
            pool.wait_ge(x_updated, X0 + 4 * L1A)

            def outer(i, first):
                norm_pool(pool, L1A, i)
                k, v = group(k_rot, i), group(ctx, i)
                for n in range(NK):
                    if not first:
                        pool.wait_ge(l1a_sum_psum, (i - 1) * NK + n + 1)
                    pool.tensor_tensor(r_kv[:, n, :].rearrange("p (h e d) -> p h e d", h=8, e=DH8),
                                       l1a_half(v, n, True), l1a_half(k, n, False), ALU.mult).then_inc(l1a_kv, 1)

            outer(0, True)
            with pool.Fori(1, NG) as i:
                outer(i, False)

        def l1a_dve(dve, ended):
            weights(dve, 2)

            def body(i, stats, apply):
                l1a_rotate(dve, ended, xn[:, :, :], "cosq", "sinq", r_t, r_r, r_q).then_inc(l1a_q, 1)
                dve.wait_ge(l1a_q, i + 1)
                q = r_q.rearrange("p b d -> p (b d)")

                def by_q(n):
                    dve.wait_ge(l1a_sum_psum, i * NK + n + 1)
                    dve.tensor_tensor(r_m[:, n % 2, :].rearrange("p (h e d) -> p h e d", h=8, e=DH8),
                                      bank[n][:, :].rearrange("p (h e d) -> p h e d", h=8, e=DH8),
                                      l1a_half(q, n, False), ALU.mult).then_inc(l1a_m, 1)

                by_q(0)
                for n in range(NK):
                    if n + 1 < NK:
                        if n:
                            dve.wait_ge(l1a_o, i * (NK - 1) + n)
                        by_q(n + 1)
                    dve.wait_ge(l1a_m, i * NK + n + 1)
                    b, half = divmod(n, 2)
                    last = dve.tensor_reduce(r_o[:, b, half * 64:half * 64 + 64],
                                             r_m[:, n % 2, :].rearrange("p (f d) -> p f d", d=DH8), AX_X, ALU.add)
                    last.then_inc(l1a_o if n < NK - 1 else y_ready, 1)
                    if n == 3:
                        stats()
                    if n == 5:
                        apply()
                update_dve(dve, L1A, i, src=r_o.rearrange("p b d -> p (b d)"))
            over_groups_dve(dve, ended, L1A, 4, body)

        def l1a_pe(pe):
            weights(pe, 2)
            begun(pe, L1A, 0)

            def sums(i, first):
                for n in range(NK):
                    pe.wait_ge(l1a_kv, i * NK + n + 1)
                    if not first:
                        pe.wait_ge(l1a_m, (i - 1) * NK + n + 1)
                    pe.matmul(bank[n][:, :], W("causalT"), r_kv[:, n, :], start=True, stop=True)\
                      .then_inc(l1a_sum_psum, 1)

            sums(0, True)
            with pe.Fori(1, NG) as i:
                sums(i, False)

        areas[0] = 0
        e_x = work(GB, S + 2)
        e_conv, e_silu, e_x1, e_y, e_sq, e_rr, e_h, e_o = (work(GB, S) for _ in range(8))
        e_logit, e_shift, e_exp, e_sel, e_rw = (work(GB, E1) for _ in range(5))
        e_wide = work(2, GB, 64).rearrange("p k b (e j) -> p k b e j", e=8)
        e_max, e_sum, e_rsum = work(GB), work(GB), work(GB)
        e_rwT, e_gelu = work(GB, S, p=E1), work(GB, S, p=HID1)
        e_ye, e_ys = work(2, T), work(2, T)
        l1f_conv, l1f_pw_psum, l1f_silu, l1f_x1, l1f_logit_psum, l1f_shift, l1f_exp, l1f_rw, l1f_rwT_psum, l1f_rwT, \
            l1f_ye_psum, l1f_ye, l1f_rwb_psum, l1f_ys, l1f_moe, l1f_sq, l1f_ms_psum, l1f_rr, l1f_h, l1f_down_psum, \
            l1f_gelu, l1f_up_psum, l1f_o = (
                sem(f"l1f_{n}") for n in "conv pw_psum silu x1 logit_psum shift exp rw rwT_psum rwT ye_psum ye "
                "rwb_psum ys moe sq ms_psum rr h down_psum gelu up_psum o".split())

        def l1f_act(act, ended):
            with act.Fori(0, NG) as i:
                ended.turn(i, 1)
                turned_act(act, L1F, i, e_x[:, :, 2:])
                act.wait_ge(l1f_pw_psum, i + 1)
                act.activation(e_silu, by4(1), ACT.Silu, bias=W("l1_pwb")).then_inc(l1f_silu, 1)
                act.wait_ge(l1f_shift, i + 1)
                act.activation(e_exp, e_shift, ACT.Exp).then_inc(l1f_exp, 1)
                act.wait_ge(l1f_rwT_psum, i + 1)
                act.activation(e_rwT, by4(3)[0:E1], ACT.Copy).then_inc(l1f_rwT, 1)
                for e in range(E1):
                    act.wait_ge(l1f_ye_psum, i * E1 + e + 1)
                    if e >= 2:
                        act.wait_ge(l1f_ys, i * E1 + e - 1)
                    act.activation(e_ye[:, e % 2, :], bank[4 + e % 2][:, :], ACT.Silu,
                                   bias=W("l1_expertb", e, 1)).then_inc(l1f_ye, 1)
                act.wait_ge(l1f_ms_psum, i + 1)
                ended(act.activation(e_rr, by4(0), ACT.Ln, scale=1.0 / D, bias=RMS_EPS))
                act.activation(e_rr, e_rr, ACT.Exp, scale=-0.5).then_inc(l1f_rr, 1)
                act.wait_ge(l1f_down_psum, i + 1)
                act.activation(e_gelu, by4(2)[0:HID1], ACT.Gelu, bias=W("l1_downb")).then_inc(l1f_gelu, 1)
            ended.loop_over(NG)

        def l1f_dve(dve, ended):
            weights(dve, 3)
            ended(dve.memset(e_x[:, :, 0:2], 0.0))
            ended.straight_over()

            def body(i, stats, apply):
                dve.wait_ge(xnT_ready, turned(L1F) + i + 1)
                ended(dve.tensor_scalar(e_conv, e_x[:, :, 0:S], W("l1_dw", 0, 1), W("l1_dwb"), ALU.mult, ALU.add))
                ended(dve.scalar_tensor_tensor(e_conv, e_x[:, :, 1:S + 1], W("l1_dw", 1, 1), e_conv, ALU.mult, ALU.add))
                dve.scalar_tensor_tensor(e_conv, e_x[:, :, 2:], W("l1_dw", 2, 1), e_conv, ALU.mult, ALU.add)\
                   .then_inc(l1f_conv, 1)
                dve.wait_ge(l1f_silu, i + 1)
                dve.tensor_tensor(e_x1, e_x[:, :, 2:], e_silu, ALU.add).then_inc(l1f_x1, 1)
                dve.wait_ge(l1f_logit_psum, i + 1)
                ended(dve.tensor_tensor(e_logit, bank[2][:, 0:GB * E1].rearrange("p (b e) -> p b e", b=GB),
                                        W("l1_routerb").unsqueeze(1).to_broadcast([128, GB, E1]), ALU.add))
                ended(dve.tensor_reduce(e_max, e_logit, AX_X, ALU.max))
                dve.tensor_tensor(e_shift, e_logit, bc(e_max, GB, -E1), ALU.subtract).then_inc(l1f_shift, 1)
                rank_dve(dve, ended, e_logit, e_sel, (e_wide[:, 0], e_wide[:, 1]), TOP1)
                dve.wait_ge(l1f_exp, i + 1)
                ended(dve.tensor_tensor(e_sel, e_exp, e_sel, ALU.mult))
                ended(dve.tensor_reduce(e_sum, e_sel, AX_X, ALU.add))
                ended(dve.reciprocal(e_rsum, e_sum))
                dve.tensor_tensor(e_rw, e_sel, bc(e_rsum, GB, -E1), ALU.mult).then_inc(l1f_rw, 1)
                for e in range(E1):
                    dve.wait_ge(l1f_rwb_psum, i * E1 + e + 1)
                    dve.wait_ge(l1f_ye, i * E1 + e + 1)
                    if e >= 2:
                        dve.wait_ge(l1f_moe, i * E1 + e - 1)
                    dve.tensor_tensor(e_ys[:, e % 2, :], bank[(6, 1)[e % 2]][:, :], e_ye[:, e % 2, :], ALU.mult)\
                       .then_inc(l1f_ys, 1)
                    if e == 2:
                        stats()
                    if e == 4:
                        apply()
                dve.wait_ge(l1f_moe, i * E1 + E1)
                dve.wait_ge(l1f_x1, i + 1)
                ended(dve.scalar_tensor_tensor(e_y, by4(7), W("l1_outb"), e_x1, ALU.add, ALU.add))
                dve.tensor_tensor(e_sq, e_y, e_y, ALU.mult).then_inc(l1f_sq, 1)
                dve.wait_ge(l1f_rr, i + 1)
                dve.scalar_tensor_tensor(e_h, e_y, W("l1_norm"), e_rr, ALU.mult, ALU.mult).then_inc(l1f_h, 1)
                dve.wait_ge(l1f_up_psum, i + 1)
                dve.wait_ge(l1f_h, i + 1)
                dve.scalar_tensor_tensor(e_o, by4(3), W("l1_upb"), e_h, ALU.add, ALU.add).then_inc(l1f_o, 1)
                update_dve(dve, L1F, i, 5)
            over_groups_dve(dve, ended, L1F, 17, body)

        def l1f_pe(pe):
            weights(pe, 3)
            with pe.Fori(0, NG) as i:
                turn_pe(pe, L1F, i)
                pe.wait_ge(l1f_conv, i + 1)
                pe.matmul(bank[1][:, :], W("l1_pwT"), e_conv, start=True, stop=True).then_inc(l1f_pw_psum, 1)
                pe.wait_ge(l1f_x1, i + 1)
                for b in range(GB):
                    last = pe.matmul(bank[2][:, b * E1:(b + 1) * E1], e_x1[:, b, :], W("l1_routerT"), start=True, stop=True)
                last.then_inc(l1f_logit_psum, 1)

                def expert(e):
                    if e >= 2:
                        pe.wait_ge(l1f_ye, i * E1 + e - 1)
                    pe.matmul(bank[4 + e % 2][:, :], W("l1_expertT", e * 128, 128), e_x1, start=True, stop=True)\
                      .then_inc(l1f_ye_psum, 1)

                def mix(e):
                    pe.wait_ge(l1f_ys, i * E1 + e + 1)
                    pe.matmul(bank[7][:, :], W("l1_outT"), e_ys[:, e % 2, :], start=(e == 0), stop=(e == E1 - 1))\
                      .then_inc(l1f_moe, 1)

                expert(0)
                expert(1)
                pe.wait_ge(l1f_rw, i + 1)
                for b in range(GB):
                    last = pe.transpose(by4(3)[0:E1, b, :], e_rw[:, b, :], W("ident"))
                last.then_inc(l1f_rwT_psum, 1)
                pe.wait_ge(l1f_rwT, i + 1)
                for e in range(E1):
                    pe.matmul(bank[(6, 1)[e % 2]][:, :], W("eye8", e * 128, 128), e_rwT, start=True, stop=True)\
                      .then_inc(l1f_rwb_psum, 1)
                    if e + 2 < E1:
                        expert(e + 2)
                    if e >= 1:
                        mix(e - 1)
                mix(E1 - 1)
                pe.wait_ge(l1f_sq, i + 1)
                pe.matmul(bank[0][:, :], W("ones"), e_sq, start=True, stop=True).then_inc(l1f_ms_psum, 1)
                pe.wait_ge(l1f_h, i + 1)
                pe.matmul(bank[2][0:HID1, :], W("l1_downT"), e_h, start=True, stop=True).then_inc(l1f_down_psum, 1)
                pe.wait_ge(l1f_gelu, i + 1)
                pe.matmul(bank[3][:, :], W("l1_upT"), e_gelu, start=True, stop=True).then_inc(l1f_up_psum, 1)
                pe.wait_ge(l1f_o, i + 1)
                for b in range(GB):
                    last = pe.transpose(by4(5)[:, b, :], e_o[:, b, :], W("ident"))
                last.then_inc(y_ready, 1)

        areas[0] = 0
        m_z, m_abs, m_lf, m_cs, m_a, m_nM, m_end = (work(GB, S, p=H4) for _ in range(7))
        m_aT = work(2 * GB * H4)
        m_kT = work(GB, S)
        m_v = work(GB * H4, DH32 + 1)
        m_arg, m_d, m_c = work(2, T), work(2, T), work(2, T)
        m_den, m_abs2, m_h, m_sq = work(GB * H4), work(GB * H4), work(GB * H4, DH32), work(GB * H4, DH32)
        m_mean, m_var, m_rstd = work(GB * H4), work(GB * H4), work(GB * H4)
        m_scale = work(D)
        m_future = work(S, dt=BF16)
        l2a_gates_psum, l2a_z, l2a_log, l2a_end_in, l2a_end, l2a_nM, l2a_ctx, l2a_aT_psum, l2a_bias_psum, \
            l2a_qk_psum, l2a_arg, l2a_d, l2a_c, l2a_hv, l2a_var, l2a_rstd, l2a_const = (
                sem(f"l2a_{n}") for n in "gates_psum z log end_in end nM ctx aT_psum bias_psum qk_psum arg d c hv "
                "var rstd const".split())

        def l2a_act(act, ended):
            act.preload_act_table_set("natural_log_exp_and_others")
            act.wait_ge(l2a_const, 1)
            with act.Fori(0, NG) as i:
                ended.turn(i, 3)
                begun(act, L2A, i)
                act.activation(m_kT, group4(ctxT, i), ACT.Copy, scale=DH32 ** -0.5)
                act.activation(m_v[:, :, 0:DH32], group(ctx, i).rearrange("p (n d) -> p n d", d=DH32), ACT.Copy)\
                   .then_inc(l2a_ctx, 1)
                turned_act(act, L2A, i)
                act.wait_ge(l2a_z, i + 1)
                ended(act.activation(m_abs, m_z, ACT.Abs))
                ended(act.activation(m_abs, m_abs, ACT.Exp, scale=-1.0))
                act.activation(m_abs, m_abs, ACT.Ln, bias=1.0).then_inc(l2a_log, 1)
                act.wait_ge(l2a_end_in, i + 1)
                act.activation(m_end, m_end, ACT.Exp, scale=-1.0).then_inc(l2a_end, 1)
                for h in range(H4):
                    act.wait_ge(l2a_arg, i * H4 + h + 1)
                    if h >= 2:
                        act.wait_ge(l2a_c, i * H4 + h - 1)
                    act.activation(m_d[:, h % 2, :], m_arg[:, h % 2, :], ACT.Exp).then_inc(l2a_d, 1)
                act.wait_ge(l2a_var, i + 1)
                ended(act.activation(m_rstd, m_var, ACT.Ln, scale=1.0 / DH32, bias=LN_EPS))
                act.activation(m_rstd, m_rstd, ACT.Exp, scale=-0.5).then_inc(l2a_rstd, 1)
            ended.loop_over(NG)

        def l2a_dve(dve, ended):
            weights(dve, 4)
            dve.memset(m_v[:, :, DH32:], 1.0)
            dve.tensor_copy(m_future, W("futureT"))
            dve.tensor_scalar(m_scale, W("l2_outw"), 1.0, None, ALU.add).then_inc(l2a_const, 1)
            dve.wait_ge(l2a_const, 1)

            def flat(t):
                return t.rearrange("p b s -> p (b s)")


            def body(i, stats, apply):
                dve.wait_ge(l2a_gates_psum, i + 1)
                dve.tensor_scalar(m_z, by4(2)[0:H4], W("l2_fgb"), None, ALU.add).then_inc(l2a_z, 1)
                ended(dve.tensor_scalar(m_a, by4(1)[0:H4], W("l2_igb"), None, ALU.add))
                dve.wait_ge(l2a_log, i + 1)
                ended(dve.scalar_tensor_tensor(m_lf, m_z, 0.0, m_abs, ALU.min, ALU.subtract))
                ended(dve.tensor_tensor_scan(flat(m_cs), W("keep"), flat(m_lf), 0.0, ALU.mult, ALU.add))
                ended(dve.tensor_tensor(m_a[:, :, 1:], m_a[:, :, 1:], m_cs[:, :, :S - 1], ALU.subtract))
                ended(dve.tensor_tensor_scan(flat(m_nM), W("restart"), flat(m_a), -BIG, ALU.add, ALU.max))
                dve.tensor_tensor(m_end, m_nM, m_cs, ALU.add).then_inc(l2a_end_in, 1)
                dve.wait_ge(l2a_end_in, i + 1)
                dve.tensor_scalar(m_nM, m_nM, -1.0, None, ALU.mult).then_inc(l2a_nM, 1)
                dve.wait_ge(l2a_aT_psum, i + 1)
                ended(dve.tensor_copy(m_aT, bank[3][:, 0:2 * GB * H4]))
                for h in range(H4):
                    dve.wait_ge(l2a_bias_psum, i * H4 + h + 1)
                    if h >= 2:
                        dve.wait_ge(l2a_d, i * H4 + h - 1)
                    a_h = m_aT[:, 0:GB * H4].rearrange("p (b h) -> p h b", b=GB)[:, h, :]
                    dve.tensor_tensor(m_arg[:, h % 2, :].rearrange("p (b s) -> p b s", b=GB), by4(4 + h % 2),
                                      bc(a_h, GB, -S), ALU.add).then_inc(l2a_arg, 1)
                    dve.wait_ge(l2a_qk_psum, i * H4 + h + 1)
                    dve.wait_ge(l2a_d, i * H4 + h + 1)
                    if h >= 2:
                        dve.wait_ge(l2a_hv, i * (H4 - 1) + h - 1)
                    dve.tensor_tensor(m_c[:, h % 2, :], bank[6 + h % 2][:, :], m_d[:, h % 2, :], ALU.mult)\
                       .then_inc(l2a_c, 1)
                    if h == 1:
                        stats()
                    if h == 2:
                        apply()
                dve.wait_ge(y_ready, 4 * L2A + i + 1)
                n = GB * H4 // 2
                for half in range(2):
                    hv = bank[1 + half][:, 0:n * (DH32 + 1)].rearrange("p (n d) -> p n d", d=DH32 + 1)
                    last = dve.tensor_copy(m_den[:, half * n:(half + 1) * n], hv[:, :, DH32])
                ended(last)
                ended(dve.scalar_tensor_tensor(m_abs2, m_den, -1.0, m_den, ALU.mult, ALU.max))
                ended(dve.tensor_tensor(m_abs2, m_abs2, m_aT[:, GB * H4:], ALU.max))
                ended(dve.tensor_scalar(m_abs2, m_abs2, MLSTM_EPS, None, ALU.add))
                ended(dve.reciprocal(m_den, m_abs2))
                for half in range(2):
                    hv = bank[1 + half][:, 0:n * (DH32 + 1)].rearrange("p (n d) -> p n d", d=DH32 + 1)
                    last = dve.tensor_tensor(m_h[:, half * n:(half + 1) * n, :], hv[:, :, 0:DH32],
                                             bc(m_den[:, half * n:(half + 1) * n], n, -DH32), ALU.mult)
                ended(last)
                ended(dve.tensor_reduce(m_mean, m_h, AX_X, ALU.add))
                ended(dve.tensor_scalar(m_mean, m_mean, 1.0 / DH32, None, ALU.mult))
                ended(dve.tensor_tensor(m_h, m_h, bc(m_mean, 2 * n, -DH32), ALU.subtract))
                ended(dve.tensor_tensor(m_sq, m_h, m_h, ALU.mult))
                dve.tensor_reduce(m_var, m_sq, AX_X, ALU.add).then_inc(l2a_var, 1)
                dve.wait_ge(l2a_rstd, i + 1)
                ended(dve.tensor_tensor(m_h, m_h, bc(m_rstd, 2 * n, -DH32), ALU.mult))
                h4 = m_h.rearrange("p (b h) d -> p b (h d)", b=GB)
                ended(dve.tensor_tensor(h4, h4, m_scale.unsqueeze(1).to_broadcast([128, GB, D]), ALU.mult))
                update_dve(dve, L2A, i, src=m_h.rearrange("p n d -> p (n d)"))
            over_groups_dve(dve, ended, L2A, 21, body)

        def l2a_pe(pe):
            weights(pe, 4)
            pe.wait_ge(l2a_const, 1)
            with pe.Fori(0, NG) as i:
                begun(pe, L2A, i)
                gates = ((1, "l2_igT"), (2, "l2_fgT"))
                for k, w in gates:
                    pe.matmul(bank[k][0:H4, :], W(w, H4, H4), group(ctxT, i), start=True, stop=False)
                    pe.matmul(bank[k][0:H4, :], W(w, 2 * H4, H4), group(ctxT, i), start=False, stop=False)
                turn_pe(pe, L2A, i)
                pe.wait_ge(xnT_ready, turned(L2A) + i + 1)
                for k, w in gates:
                    last = pe.matmul(bank[k][0:H4, :], W(w, 0, H4), xnT[:, :, :], start=False, stop=True)
                last.then_inc(l2a_gates_psum, 1)
                pe.wait_ge(l2a_ctx, i + 1)

                def products(h):
                    if h >= 2:
                        pe.wait_ge(l2a_c, i * H4 + h - 1)
                    pe.matmul(by4(4 + h % 2), identb[:, :], m_future.unsqueeze(1).to_broadcast([128, GB, S]),
                              start=True, stop=False)
                    pe.matmul(bank[4 + h % 2][:, :], W("eye8", h * 128, 128)[0:H4], m_nM, start=False, stop=True)\
                      .then_inc(l2a_bias_psum, 1)
                    rows = slice(h * DH32, (h + 1) * DH32)
                    for b in range(GB):
                        last = pe.matmul(by4(6 + h % 2)[:, b, :], m_kT[rows, b, :], xnT[rows, b, :], start=True, stop=True)
                    last.then_inc(l2a_qk_psum, 1)

                pe.wait_ge(l2a_nM, i + 1)
                pe.wait_ge(l2a_end, i + 1)
                for k, t in enumerate((m_a, m_end)):
                    for b in range(GB):
                        at = (k * GB + b) * H4
                        last = pe.matmul(bank[3][:, at:at + H4], t[:, b, :], W("ident")[0:H4, 0:H4], start=True, stop=True)
                last.then_inc(l2a_aT_psum, 1)
                products(0)
                for h in range(H4):
                    if h + 1 < H4:
                        products(h + 1)
                    pe.wait_ge(l2a_c, i * H4 + h + 1)
                    for b in range(GB):
                        at = (b % 2 * H4 + h) * (DH32 + 1)
                        last = pe.matmul(bank[1 + b // 2][:, at:at + DH32 + 1], m_c[:, h % 2, b * S:(b + 1) * S],
                                         m_v[:, b * H4 + h, :], start=True, stop=True)
                    last.then_inc(l2a_hv if h < H4 - 1 else y_ready, 1)

        areas[0] = 0
        t_q, t_k = work(2 * C2, T), work(C2, T)
        t_v = work(GB * H8, DH64)
        t_sig, t_sel, t_sc = work(GB, H8), work(GB, H8), work(GB, H8)
        t_wide = work(2, GB, 64).rearrange("p k b (e j) -> p k b e j", e=8)
        t_scT = work(GB, S, p=H8)
        t_nmax, t_sum, t_r = work(2, 4), work(2, 4), work(2, 4)
        t_p, t_pT = work(2, C2, S), work(2, C2, S)
        t_oT = work(2, C2, S)
        l2f_zeroed, l2f_gate_psum, l2f_e, l2f_sc, l2f_psum, l2f_by_act, l2f_by_dve, l2f_s_psum, l2f_max, l2f_scT_psum, l2f_scT, \
            l2f_exp, l2f_p, l2f_pT_psum, l2f_pT, l2f_oT_psum, l2f_oT = (
                sem(f"l2f_{n}") for n in "zeroed gate_psum e sc psum by_act by_dve s_psum max scT_psum scT "
                "exp p pT_psum pT oT_psum oT".split())
        NH = 2 * GB

        def l2f_out(n):
            if n < 2 * C2:
                return t_k[:, n // 2, :]
            return t_v[:, (n - 2 * C2) * H8:(n - 2 * C2 + 1) * H8, :]

        def l2f_in(n):
            a = bank[1 + n % 4][:, :]
            return a if n < 2 * C2 else a.rearrange("p (h d) -> p h d", d=DH64)

        def l2f_act(act, ended):
            act.wait_ge(l2f_zeroed, 1)
            with act.Fori(0, NG) as i:
                turned_act(act, L2F, i)
                act.wait_ge(l2f_gate_psum, i + 1)
                act.activation(t_sig, bank[5][:, 0:GB * H8].rearrange("p (b h) -> p b h", b=GB), ACT.Exp, scale=-1.0)\
                   .then_inc(l2f_e, 1)

                def projected(n):
                    act.wait_ge(l2f_psum, i * 12 + n + 1)
                    if n < 2 * C2:
                        for half in range(2):
                            rows = slice(DH64 * half, DH64 * (half + 1))
                            last = act.activation(t_q[rows, n + half, :], l2f_in(n)[rows], ACT.Copy, scale=DH64 ** -0.5)
                    else:
                        last = act.activation(l2f_out(n), l2f_in(n), ACT.Copy)
                    last.then_inc(l2f_by_act, 1)

                for n in range(0, 2 * C2, 2):
                    projected(n)

                def turned_p(m):
                    act.wait_ge(l2f_pT_psum, i * NH + m + 1)
                    act.activation(t_pT[:, m % 2, :, :], by4(1 + m % 2), ACT.Copy).then_inc(l2f_pT, 1)

                for m in range(NH):
                    act.wait_ge(l2f_max, i * NH + m + 1)
                    for c in range(C2):
                        last = act.activation(t_p[:, m % 2, c, :], by4(6 + m % 2)[:, c, :], ACT.Exp,
                                              bias=t_nmax[:, m % 2, c:c + 1], accum_out=t_sum[:, m % 2, c:c + 1])
                    last.then_inc(l2f_exp, 1)
                    if m < 2:
                        projected(2 * C2 + 2 * m)
                    if m:
                        turned_p(m - 1)
                turned_p(NH - 1)

        def l2f_dve(dve, ended):
            weights(dve, 5)
            dve.memset(t_q[:, :, :], 0.0).then_inc(l2f_zeroed, 1)

            def body(i, stats, apply):
                dve.wait_ge(l2f_e, i + 1)
                ended(dve.tensor_scalar(t_sig, t_sig, 1.0, None, ALU.add))
                ended(dve.reciprocal(t_sig, t_sig))
                rank_dve(dve, ended, t_sig, t_sel, (t_wide[:, 0], t_wide[:, 1]), TOP2)
                dve.tensor_tensor(t_sc, t_sig, t_sel, ALU.mult).then_inc(l2f_sc, 1)

                def projected(n):
                    dve.wait_ge(l2f_psum, i * 12 + n + 1)
                    dve.tensor_copy(l2f_out(n), l2f_in(n)).then_inc(l2f_by_dve, 1)

                for n in range(1, 2 * C2, 2):
                    projected(n)

                def normed(m):
                    b, half = divmod(m, 2)
                    dve.wait_ge(l2f_exp, i * NH + m + 1)
                    ended(dve.reciprocal(t_r[:, m % 2, :], t_sum[:, m % 2, :]))
                    ended(dve.tensor_tensor(t_r[:, m % 2, :], t_r[:, m % 2, :], t_sc[:, b, half::2], ALU.mult))
                    dve.tensor_tensor(t_p[:, m % 2, :, :], t_p[:, m % 2, :, :], bc(t_r[:, m % 2, :], C2, -S), ALU.mult)\
                       .then_inc(l2f_p, 1)

                for m in range(NH):
                    dve.wait_ge(l2f_s_psum, i * NH + m + 1)
                    dve.tensor_reduce(t_nmax[:, m % 2, :], by4(6 + m % 2), AX_X, ALU.max, negate=True)\
                       .then_inc(l2f_max, 1)
                    if m == 1:
                        projected(2 * C2 + 1)
                        projected(2 * C2 + 3)
                        dve.wait_ge(l2f_scT_psum, i + 1)
                        dve.tensor_copy(t_scT, by4(0)[0:H8]).then_inc(l2f_scT, 1)
                        dve.wait_ge(l2f_sc, i + 1)
                    if m:
                        normed(m - 1)
                    if m > 1 and m % 2 == 1:
                        l2f_out_dve(dve, i, m // 2 - 1)
                    if m == 4:
                        stats()
                    if m == 6:
                        apply()
                normed(NH - 1)
                l2f_out_dve(dve, i, GB - 1)
                update_dve(dve, L2F, i, 5)
            over_groups_dve(dve, ended, L2F, 27, body)

        def l2f_out_dve(dve, i, b):
            dve.wait_ge(l2f_oT_psum, i * GB + b + 1)
            dve.tensor_copy(t_oT[:, b % 2, :, :], by4(3 + b % 2)).then_inc(l2f_oT, 1)

        def l2f_pe(pe):
            weights(pe, 5)
            with pe.Fori(0, NG) as i:
                turn_pe(pe, L2F, i)
                begun(pe, L2F, i)
                pe.wait_ge(xnT_ready, turned(L2F) + i + 1)
                for b in range(GB):
                    last = pe.matmul(bank[5][:, b * H8:(b + 1) * H8], xnT[:, b, :], W("l2_Ws"), start=True, stop=True)
                last.then_inc(l2f_gate_psum, 1)

                def projection(n):
                    if n >= 4:
                        pe.wait_ge((l2f_by_act, l2f_by_dve)[n % 2], i * 6 + (n - 4) // 2 + 1)
                    if n < 2 * C2:
                        w = W(("l2_Wq", "l2_Wk")[n % 2], n // 2 * 128, 128)
                        last = pe.matmul(bank[1 + n % 4][:, :], w, xnT[:, :, :], start=True, stop=True)
                    else:
                        last = pe.matmul(bank[1 + n % 4][:, :], xnT[:, n - 2 * C2, :], W("l2_Wv"), start=True, stop=True)
                    last.then_inc(l2f_psum, 1)

                for n in range(2 * C2):
                    projection(n)

                def scores(m):
                    b, half = divmod(m, 2)
                    if m >= 2:
                        pe.wait_ge(l2f_exp, i * NH + m - 1)
                    for c in range(C2):
                        last = pe.matmul(by4(6 + m % 2)[:, c, :], t_q[:, 2 * c + half, b * S:(b + 1) * S],
                                         t_k[:, c, b * S:(b + 1) * S], start=True, stop=True)
                    last.then_inc(l2f_s_psum, 1)

                def turn_p(m):
                    pe.wait_ge(l2f_p, i * NH + m + 1)
                    if m >= 2:
                        pe.wait_ge(l2f_pT, i * NH + m - 1)
                    for c in range(C2):
                        last = pe.transpose(by4(1 + m % 2)[:, c, :], t_p[:, m % 2, c, :], W("ident"))
                    last.then_inc(l2f_pT_psum, 1)

                def weighted(m):
                    b, half = divmod(m, 2)
                    pe.wait_ge(l2f_pT, i * NH + m + 1)
                    if half == 0 and b >= 2:
                        pe.wait_ge(l2f_oT, i * GB + b - 1)
                    for c in range(C2):
                        last = pe.matmul(by4(3 + b % 2)[DH64 * half:DH64 * (half + 1), c, :],
                                         t_v[:, b * H8 + 2 * c + half, :], t_pT[:, m % 2, c, :], start=True, stop=True)
                    if half:
                        last.then_inc(l2f_oT_psum, 1)

                def project(b):
                    pe.wait_ge(l2f_oT, i * GB + b + 1)
                    if b == 0:
                        pe.wait_ge(l2f_scT, i + 1)
                    pe.matmul(by4(5)[:, b, :], t_scT[:, b, :], W("l2_bo"), start=True, stop=False)
                    for c in range(C2):
                        last = pe.matmul(by4(5)[:, b, :], t_oT[:, b % 2, c, :], W("l2_Wo", c * 128, 128),
                                         start=False, stop=(c == C2 - 1))
                    if b == GB - 1:
                        last.then_inc(y_ready, 1)

                pe.wait_ge(l2f_by_act, i * 6 + C2)
                pe.wait_ge(l2f_by_dve, i * 6 + C2)
                scores(0)
                scores(1)
                for n in range(2 * C2, 12):
                    projection(n)
                pe.wait_ge(l2f_by_act, i * 6 + 6)
                pe.wait_ge(l2f_by_dve, i * 6 + 6)
                pe.wait_ge(l2f_sc, i + 1)
                for b in range(GB):
                    last = pe.transpose(by4(0)[0:H8, b, :], t_sc[:, b, :], W("ident"))
                last.then_inc(l2f_scT_psum, 1)
                for m in range(NH):
                    if m + 2 < NH:
                        scores(m + 2)
                    turn_p(m)
                    if m:
                        weighted(m - 1)
                    if m % 2 == 0 and m > 2:
                        project(m // 2 - 2)
                weighted(NH - 1)
                project(GB - 2)
                project(GB - 1)

        areas[0] = 0
        c_T = work(GB, S)
        c_q, c_k = work(H16, T), work(4, T)
        c_bq = work(4)
        c_v = work(GB * H16, PADH)
        c_nmax, c_sum, c_r = work(2, 4), work(2, 4), work(2, 4)
        c_p, c_pT = work(2, 4, S), work(2, 4, S)
        c_oT = work(2, 4, S)
        c_mask = work(S, dt=BF16)
        l3a_q_act, l3a_w_psum, l3a_const, l3a_ctxT, l3a_q_psum, l3a_k_psum, l3a_q, l3a_k, l3a_v_psum, l3a_v, l3a_s_psum, \
            l3a_max, l3a_exp, l3a_p, l3a_pT_psum, l3a_pT, l3a_oT_psum, l3a_oT = (
                sem(f"l3a_{n}") for n in "q_act w_psum const ctxT q_psum k_psum q k v_psum v s_psum "
                "max exp p pT_psum pT oT_psum oT".split())

        def l3a_act(act, ended):
            act.wait_ge(l3a_const, 1)
            with act.Fori(0, NG) as i:
                act.activation(c_T, group4(ctxT, i), ACT.Copy).then_inc(l3a_ctxT, 1)
                turned_act(act, L3A, i)
                for g in range(4):
                    act.wait_ge(l3a_k_psum, i * 4 + g + 1)
                    act.activation(c_k[:, g, :], bank[4 + g][:, :], ACT.Identity, bias=W("l3_bkP", g, 1))\
                       .then_inc(l3a_k, 1)
                for g in range(4):
                    act.wait_ge(l3a_q_psum, i * 4 + g + 1)
                    for j in (2, 3):
                        rows = slice(PADH * j, PADH * (j + 1))
                        last = act.activation(c_q[rows, 4 * g + j, :], bank[2 + g][rows, :], ACT.Identity,
                                              bias=c_bq[rows, g:g + 1], scale=DH8 ** -0.5)
                    last.then_inc(l3a_q_act, 1)

                def turned_p(m):
                    act.wait_ge(l3a_pT_psum, i * NQ + m + 1)
                    act.activation(c_pT[:, m % 2, :, :], by4(6 + m % 2), ACT.Copy).then_inc(l3a_pT, 1)

                for m in range(NQ):
                    act.wait_ge(l3a_max, i * NQ + m + 1)
                    for g in range(4):
                        last = act.activation(c_p[:, m % 2, g, :], by4(4 + m % 2)[:, g, :], ACT.Exp,
                                              bias=c_nmax[:, m % 2, g:g + 1], accum_out=c_sum[:, m % 2, g:g + 1])
                    last.then_inc(l3a_exp, 1)
                    if m:
                        turned_p(m - 1)
                turned_p(NQ - 1)

        def l3a_dve(dve, ended):
            weights(dve, 6)
            dve.wait_ge(l3a_w_psum, 1)
            for k, w in ((1, "l3_WqP"), (2, "l3_WkP"), (3, "l3_WvT")):
                n = WHERE[w][2]
                dve.scalar_tensor_tensor(W(w), bank[k][:, 0:n], LORA_SCALE, W(w), ALU.mult, ALU.add)
            dve.memset(c_v[:, :, :], 0.0)
            dve.memset(c_q[:, :, :], 0.0)
            dve.tensor_scalar(c_bq, W("l3_bqP"), DH8 ** -0.5, None, ALU.mult)
            dve.wait_ge(imask_loaded, 16)
            dve.tensor_scalar(c_mask, imask[:, :], 0.0, -BIG, ALU.is_equal, ALU.mult).then_inc(l3a_const, 1)
            dve.wait_ge(l3a_const, 1)

            def body(i, stats, apply):
                for g in range(4):
                    dve.wait_ge(l3a_q_psum, i * 4 + g + 1)
                    for j in (0, 1):
                        rows = slice(PADH * j, PADH * (j + 1))
                        last = dve.tensor_scalar(c_q[rows, 4 * g + j, :], bank[2 + g][rows, :],
                                                 W("l3_bqP", g, 1)[rows], DH8 ** -0.5, ALU.add, ALU.mult)
                    last.then_inc(l3a_q, 1)

                def normed(m):
                    dve.wait_ge(l3a_exp, i * NQ + m + 1)
                    ended(dve.reciprocal(c_r[:, m % 2, :], c_sum[:, m % 2, :]))
                    dve.tensor_tensor(c_p[:, m % 2, :, :], c_p[:, m % 2, :, :], bc(c_r[:, m % 2, :], 4, -S), ALU.mult)\
                       .then_inc(l3a_p, 1)

                for m in range(NQ):
                    b, j = divmod(m, 4)
                    dve.wait_ge(l3a_s_psum, i * NQ + m + 1)
                    dve.tensor_reduce(c_nmax[:, m % 2, :], by4(4 + m % 2), AX_X, ALU.max, negate=True)\
                       .then_inc(l3a_max, 1)
                    if m == 1:
                        dve.wait_ge(l3a_v_psum, i + 1)
                        dve.tensor_copy(c_v[:, :, 0:DH8], bank[2][:, :].rearrange("p (n d) -> p n d", d=DH8))\
                           .then_inc(l3a_v, 1)
                    if m:
                        normed(m - 1)
                    if j == 2 and b:
                        l3a_out_dve(dve, i, b - 1)
                    if m == 8:
                        stats()
                    if m == 11:
                        apply()
                normed(NQ - 1)
                l3a_out_dve(dve, i, GB - 1)
                update_dve(dve, L3A, i, 1)
            over_groups_dve(dve, ended, L3A, 19, body)

        def l3a_out_dve(dve, i, b):
            dve.wait_ge(l3a_oT_psum, i * GB + b + 1)
            dve.tensor_copy(c_oT[:, b % 2, :, :], by4(2 + b % 2)).then_inc(l3a_oT, 1)

        def l3a_pe(pe):
            weights(pe, 6)
            begun(pe, L3A, 0)
            pe.matmul(bank[1][:, :], W("l3_Aq"), W("l3_BqP"), start=True, stop=True)
            pe.matmul(bank[2][:, :], W("l3_Ak"), W("l3_BkP"), start=True, stop=True)
            pe.matmul(bank[3][:, 0:128], W("l3_Av"), W("l3_BvT"), start=True, stop=True).then_inc(l3a_w_psum, 1)
            pe.wait_ge(l3a_const, 1)
            with pe.Fori(0, NG) as i:
                turn_pe(pe, L3A, i)
                pe.wait_ge(l3a_ctxT, i + 1)
                for g in range(4):
                    pe.matmul(bank[4 + g][:, :], W("l3_WkP", g * 128, 128), c_T, start=True, stop=True)\
                      .then_inc(l3a_k_psum, 1)
                pe.wait_ge(xnT_ready, turned(L3A) + i + 1)
                for g in range(4):
                    if g >= 2:
                        pe.wait_ge(l3a_k, i * 4 + g - 1)
                    pe.matmul(bank[2 + g][:, :], W("l3_WqP", g * 128, 128), xnT[:, :, :], start=True, stop=True)\
                      .then_inc(l3a_q_psum, 1)

                def scores(m):
                    b, j = divmod(m, 4)
                    if m >= 2:
                        pe.wait_ge(l3a_exp, i * NQ + m - 1)
                    k = 4 + m % 2
                    pe.matmul(by4(k), identb[:, :], c_mask.unsqueeze(1).to_broadcast([128, 4, S]),
                              start=True, stop=False)
                    for g in range(4):
                        last = pe.matmul(by4(k)[:, g, :], c_q[:, 4 * g + j, b * S:(b + 1) * S], c_k[:, g, b * S:(b + 1) * S],
                                         start=False, stop=(g == 3))
                    last.then_inc(l3a_s_psum, 1)

                def turn_p(m):
                    pe.wait_ge(l3a_p, i * NQ + m + 1)
                    if m >= 2:
                        pe.wait_ge(l3a_pT, i * NQ + m - 1)
                    for g in range(4):
                        last = pe.transpose(by4(6 + m % 2)[:, g, :], c_p[:, m % 2, g, :], W("ident"))
                    last.then_inc(l3a_pT_psum, 1)

                def weighted(m):
                    b, j = divmod(m, 4)
                    pe.wait_ge(l3a_pT, i * NQ + m + 1)
                    if m == 0:
                        pe.wait_ge(l3a_v, i + 1)
                    if j == 0 and b >= 2:
                        pe.wait_ge(l3a_oT, i * GB + b - 1)
                    for g in range(4):
                        last = pe.matmul(by4(2 + b % 2)[PADH * j:PADH * (j + 1), g, :], c_v[:, b * H16 + 4 * j + g, :],
                                         c_pT[:, m % 2, g, :], start=True, stop=True)
                    if j == 3:
                        last.then_inc(l3a_oT_psum, 1)

                def project(b):
                    pe.wait_ge(l3a_oT, i * GB + b + 1)
                    for g in range(4):
                        last = pe.matmul(by4(1)[:, b, :], c_oT[:, b % 2, g, :], W("l3_WoP", g * 128, 128),
                                         start=False, stop=(b == GB - 1 and g == 3))
                    if b == GB - 1:
                        last.then_inc(y_ready, 1)

                pe.wait_ge(l3a_k, i * 4 + 4)
                pe.wait_ge(l3a_q, i * 4 + 4)
                pe.wait_ge(l3a_q_act, i * 4 + 4)
                scores(0)
                scores(1)
                bias_pe(pe, 2, W("l3_bv"))
                for b in range(GB):
                    last = pe.matmul(by4(2)[:, b, :], c_T[:, b, :], W("l3_WvT"), start=False, stop=(b == GB - 1))
                last.then_inc(l3a_v_psum, 1)
                begun(pe, L3A, i)
                bias_pe(pe, 1, W("l3_bo"))
                for m in range(NQ):
                    if m + 2 < NQ:
                        scores(m + 2)
                    turn_p(m)
                    if m:
                        weighted(m - 1)
                    if m % 4 == 3 and m > 4:
                        project(m // 4 - 1)
                weighted(NQ - 1)
                project(GB - 1)

        areas[0] = 0
        g_h = work(C3, T)
        g_tmp = work(FF3)
        g_sum = work(2, 4)
        l3f_sum, l3f_allsum, l3f_w, l3f_psum, l3f_by_act, l3f_by_dve = (
            sem(f"l3f_{n}") for n in "sum allsum w psum by_act by_dve".split())

        def l3f_pool(pool, ended):
            norm_pool(pool, L3F, 0)
            pool.wait_ge(l3f_sum, 1)
            for k in range(2):
                last = pool.partition_all_reduce(g_sum[:, k, 1:2], g_sum[:, k, 0:1], 128, bass.bass_isa.ReduceOp.add)
            last.then_inc(l3f_allsum, 1)
            with pool.Fori(1, NG) as i:
                norm_pool(pool, L3F, i)

        def l3f_act(act, ended):
            with act.Fori(0, NG) as i:
                ended.turn(i, 0)
                turned_act(act, L3F, i)
                for c in (0, 2):
                    act.wait_ge(l3f_psum, i * C3 + c + 1)
                    act.activation(g_h[:, c, :], bank[1 + c][:, :], ACT.Relu, bias=W("l3_b1", c, 1)).then_inc(l3f_by_act, 1)
            ended.loop_over(NG)

        def l3f_dve(dve, ended):
            for k, w in enumerate(("l3_W1T", "l3_W2T")):
                last = dve.tensor_reduce(g_sum[:, k, 0:1], W(w), AX_X, ALU.add, apply_absolute_value=True)
            last.then_inc(l3f_sum, 1)
            dve.wait_ge(l3f_allsum, 1)
            ended(dve.tensor_scalar(g_sum[:, :, 2], g_sum[:, :, 1], 1.0 / (D * FF3), LN_EPS, ALU.mult, ALU.add))
            ended(dve.reciprocal(g_sum[:, :, 3], g_sum[:, :, 2]))
            for k, w in enumerate(("l3_W1T", "l3_W2T")):
                ended(dve.tensor_scalar(g_tmp, W(w), g_sum[:, k, 3:4], ROUND, ALU.mult, ALU.add))
                ended(dve.tensor_scalar(g_tmp, g_tmp, ROUND, -1.0, ALU.subtract, ALU.max))
                dve.tensor_scalar(W(w), g_tmp, 1.0, None, ALU.min).then_inc(l3f_w, 1)
                dve.wait_ge(l3f_w, k + 1)
            ended.straight_over()

            def body(i, stats, apply):
                for c in (1, 3):
                    dve.wait_ge(l3f_psum, i * C3 + c + 1)
                    dve.tensor_scalar(g_h[:, c, :], bank[1 + c][:, :], W("l3_b1", c, 1), 0.0, ALU.add, ALU.max)\
                       .then_inc(l3f_by_dve, 1)
                stats()
                apply()
                update_dve(dve, L3F, i, 5)
            over_groups_dve(dve, ended, L3F, 3, body)

        def l3f_pe(pe):
            pe.wait_ge(l3f_w, 2)
            with pe.Fori(0, NG) as i:
                turn_pe(pe, L3F, i)
                pe.wait_ge(xnT_ready, turned(L3F) + i + 1)
                for c in range(C3):
                    pe.matmul(bank[1 + c][:, :], W("l3_W1T", c * 128, 128), xnT[:, :, :], start=True, stop=True)\
                      .then_inc(l3f_psum, 1)
                begun(pe, L3F, i)
                bias_pe(pe, 5, W("l3_b2"))
                pe.wait_ge(l3f_by_act, i * 2 + 2)
                pe.wait_ge(l3f_by_dve, i * 2 + 2)
                for b in range(GB):
                    for c in range(C3):
                        last = pe.matmul(by4(5)[:, b, :], g_h[:, c, b * S:(b + 1) * S], W("l3_W2T", c * 128, 128),
                                         start=False, stop=(b == GB - 1 and c == C3 - 1))
                last.then_inc(y_ready, 1)

        programs = {
            L0A: (l0a_act, l0a_dve, l0a_pe, l1a_ahead_pool), L0F: (l0f_act, l0f_dve, l0f_pe, l0f_pool),
            L1A: (None, l1a_dve, l1a_pe, l1a_pool), L1F: (l1f_act, l1f_dve, l1f_pe, lambda pool, ended: norms_pool(pool, L1F)),
            L2A: (l2a_act, l2a_dve, l2a_pe, lambda pool, ended: norms_pool(pool, L2A)), L2F: (l2f_act, l2f_dve, l2f_pe, lambda pool, ended: norms_pool(pool, L2F)),
            L3A: (l3a_act, l3a_dve, l3a_pe, lambda pool, ended: norms_pool(pool, L3A)), L3F: (l3f_act, l3f_dve, l3f_pe, l3f_pool),
        }

        block = stack.enter_context(nc.Block())

        @block.sync
        def _(sp):
            sp.dma_start(x_all[:, :], x_in).then_inc(x_updated, X0)
            first = 0
            for n, name in enumerate(PARTS):
                _, at, cols = WHERE[name]
                sp.dma_start(pack[:, first:at + cols], pack_in[:, first:at + cols]).then_inc(part_loaded[n], 16)
                first = at + cols
                if n == 0:
                    sp.dma_start(cell, cell_in).then_inc(masks_loaded, 16)
                    sp.dma_start(seqm, seq_in.partition_broadcast(128)).then_inc(masks_loaded, 16)
                    sp.dma_start(ctxT[:, :], ctxT_in).then_inc(ctx_loaded, 16)
                    sp.dma_start(ctx[:, :], ctx_in).then_inc(ctx_loaded, 16)
                    sp.dma_start(imask[:, :], imask_in).then_inc(imask_loaded, 16)
            sp.wait_ge(x_updated, X0 + NG * layers)
            sp.dma_start(out, x_all[:, :]).then_inc(stored, 16)
            sp.wait_ge(stored, 16)

        @block.gpsimd
        def _(pool):
            ended = Ended(pool, pool_ended)
            ended(pool.memset(minus_half[:, :], -0.5))
            ended.straight_over()
            for l in range(layers):
                if programs[l][3]:
                    programs[l][3](pool, ended)

        @block.scalar
        def _(act):
            ended = Ended(act, act_ended)
            weights(act, 0)
            act.activation(tg[:, :], W("gates"), ACT.Tanh).then_inc(gates_ready, 1)
            for l in range(layers):
                if programs[l][0]:
                    programs[l][0](act, ended)

        @block.vector
        def _(dve):
            ended = Ended(dve, dve_ended)
            weights(dve, 0)
            ended(dve.tensor_copy(identb[:, :], W("ident")))
            ended.straight_over()
            dve.wait_ge(gates_ready, 1)
            begun(dve, 0, 0)
            for l in range(layers):
                programs[l][1](dve, ended)

        @block.tensor
        def _(pe):
            weights(pe, 0)
            pe.wait_ge(dve_ended, 1)
            for l in range(layers):
                programs[l][2](pe)


def packed(a):
    put = {}

    def t(name):
        return np.asarray(a[name], np.float32).T

    def col(v):
        return np.asarray(v, np.float32).reshape(-1, 1)

    def tiles(w):
        w = np.asarray(w, np.float32)
        return w.reshape(-1, 128, w.shape[1]).transpose(1, 0, 2).reshape(128, -1)

    def spread(w):
        w = np.asarray(w, np.float32)
        out = np.zeros(w.shape[:-1] + (4, 4, PADH), np.float32)
        out[..., :DH8] = w.reshape(w.shape[:-1] + (4, 4, DH8)).swapaxes(-3, -2)
        return out.reshape(w.shape[:-1] + (4, 128))

    put["ident"] = np.eye(128)
    put["ones"] = np.ones((128, 128))
    gates = np.stack([np.asarray(a["g_xattn"]), np.asarray(a["g_ffn"])], 1).reshape(1, 8)
    put["gates"] = np.broadcast_to(gates, (128, 8))
    put["eye8"] = np.repeat(np.eye(8), 128, 1)
    put["l0_WkT"], put["l0_WoT"] = t("L0_xattn_W_k"), t("L0_xattn_W_o")
    put["l0_bk"], put["l0_bo"] = col(a["L0_xattn_b_k"]), np.asarray(a["L0_xattn_b_o"])[None]
    put["l0_gate"], put["l0_up"] = tiles(a["L0_ffn_w_gate"]), tiles(a["L0_ffn_w_up"])
    put["l0_down"] = np.asarray(a["L0_ffn_w_down"])

    pos = np.arange(S, dtype=np.float64)[:, None]
    pair = np.arange(DH8 // 2, dtype=np.float64)
    base = (2 * pair + 0.4 * DH8) / (1.4 * DH8)
    scale = base[None, :] ** (pos / 512.0)
    angle = pos / 10000.0 ** (pair / (DH8 // 2))[None, :]
    gamma = 1.0 - np.exp(np.linspace(math.log(1 / 32), math.log(1 / 512), H16))
    decay = gamma[None, :, None] ** pos[:, :, None]
    sign = np.tile([-1.0, 1.0], DH8 // 2)

    def table(f, scale, decay):
        one = np.repeat(f * scale, 2, axis=1)
        return (one[:, None, :] * decay).reshape(S, D)

    put["cosq"] = table(np.cos(angle), scale, decay)
    put["sinq"] = table(np.sin(angle), scale, decay) * np.tile(sign, H16)
    put["cosk"] = table(np.cos(angle), 1.0 / scale, 1.0 / decay)
    put["sink"] = table(np.sin(angle), 1.0 / scale, 1.0 / decay) * np.tile(sign, H16)
    key, query = np.arange(S)[:, None], np.arange(S)[None, :]
    put["causalT"] = (query >= key).astype(np.float32)
    put["futureT"] = np.where(query >= key, 0.0, -BIG)

    put["l1_dw"] = np.asarray(a["L1_ffn_dw_kernel"]).reshape(128, 3)
    put["l1_dwb"], put["l1_pwb"] = col(a["L1_ffn_dw_bias"]), col(a["L1_ffn_pw_b"])
    put["l1_pwT"], put["l1_routerT"] = t("L1_ffn_pw_w"), t("L1_ffn_router_w")
    put["l1_routerb"] = np.broadcast_to(np.asarray(a["L1_ffn_router_b"])[None], (128, E1))
    put["l1_expertT"] = np.asarray(a["L1_ffn_expert_w"]).transpose(2, 0, 1).reshape(128, -1)
    put["l1_expertb"] = t("L1_ffn_expert_b")
    put["l1_outT"], put["l1_outb"] = t("L1_ffn_out_w"), col(a["L1_ffn_out_b"])
    put["l1_norm"] = col(a["L1_ffn_norm_w"])
    put["l1_downT"], put["l1_downb"] = t("L1_ffn_ff_down_w"), col(a["L1_ffn_ff_down_b"])
    put["l1_upT"], put["l1_upb"] = t("L1_ffn_ff_up_w"), col(a["L1_ffn_ff_up_b"])
    e, j = np.arange(8)[:, None], np.arange(8)[None, :]
    put["before"] = np.broadcast_to((j < e).astype(np.float32).reshape(1, 64), (128, 64))

    def gate_w(w):
        return np.asarray(w).reshape(H4, 3, 128).transpose(2, 1, 0).reshape(128, -1)

    put["l2_igT"], put["l2_fgT"] = gate_w(a["L2_xattn_igate_w"]), gate_w(a["L2_xattn_fgate_w"])
    put["l2_igb"], put["l2_fgb"] = col(a["L2_xattn_igate_b"]), col(a["L2_xattn_fgate_b"])
    put["l2_outw"] = np.broadcast_to(np.asarray(a["L2_xattn_out_w"])[None], (128, 128))
    first = (np.arange(T) % S == 0)[None]
    put["keep"] = np.broadcast_to(np.where(first, 0.0, 1.0), (H4, T))
    put["restart"] = np.broadcast_to(np.where(first, -BIG, 0.0), (H4, T))
    kv = np.asarray(a["L2_ffn_Wkv"])
    put["l2_Wq"], put["l2_Wk"], put["l2_Wv"] = np.asarray(a["L2_ffn_Wq"]), kv[:, :512], kv[:, 512:]
    put["l2_Ws"], put["l2_bo"] = np.asarray(a["L2_ffn_Ws"]), np.asarray(a["L2_ffn_bo"])
    put["l2_Wo"] = tiles(np.asarray(a["L2_ffn_Wo"]).reshape(512, 128))

    put["l3_WqP"], put["l3_WkP"] = (spread(t(n)).reshape(128, -1) for n in ("L3_xattn_Wq", "L3_xattn_Wk"))
    put["l3_WvT"] = t("L3_xattn_Wv")
    put["l3_WoP"] = spread(np.asarray(a["L3_xattn_Wo"])).transpose(2, 1, 0).reshape(128, -1)
    for n in "qkv":
        put[f"l3_A{n}"] = np.asarray(a[f"L3_xattn_A{n}"])
    put["l3_BqP"], put["l3_BkP"] = (spread(t(n)).reshape(RANK, -1) for n in ("L3_xattn_Bq", "L3_xattn_Bk"))
    put["l3_BvT"] = t("L3_xattn_Bv")
    put["l3_bqP"], put["l3_bkP"] = spread(a["L3_xattn_bq"]).T, spread(a["L3_xattn_bk"]).T
    put["l3_bv"], put["l3_bo"] = np.asarray(a["L3_xattn_bv"])[None], np.asarray(a["L3_xattn_bo"])[None]
    put["l3_W1T"], put["l3_b1"] = t("L3_ffn_W1"), np.asarray(a["L3_ffn_b1"]).reshape(C3, 128).T
    put["l3_W2T"], put["l3_b2"] = tiles(t("L3_ffn_W2")), np.asarray(a["L3_ffn_b2"])[None]

    out = np.zeros((128, COLS), np.float32)
    for name, p, n in pieces():
        _, at, _ = WHERE[name]
        out[:p, at:at + n] = put[name]
    return out


def kernel(**inputs):
    import concourse.bacc as bacc
    from concourse.bass_utils import run_bass_kernel_spmd

    a = {k: np.asarray(v) for k, v in inputs.items()}

    def tokens(v):
        return np.ascontiguousarray(v.transpose(1, 0, 2).reshape(128, -1))

    imask = a["mask_1x1xSxS2_if1"].reshape(S, S)
    arrays = {
        "x": tokens(a["x"]), "ctx": tokens(a["ctx_1024"]),
        "ctxT": np.ascontiguousarray(a["ctx_1024"].transpose(2, 0, 1).reshape(128, -1)),
        "cell": tokens(a["mask_BxSxS2_ff1"]), "seq": np.ascontiguousarray(a["mask_BxS2_ff1"].reshape(-1)),
        "imask": np.ascontiguousarray(imask),
        "pack": packed(a),
    }
    nc = bacc.Bacc("TRN2", target_bir_lowering=False, num_devices=1)
    aps = [nc.dram_tensor(f"in_{n}", v.shape, mybir.dt.from_np(v.dtype), kind="ExternalInput").ap()
           for n, v in arrays.items()]
    out = nc.dram_tensor("out", (128, B * D), F32, kind="ExternalOutput").ap()
    build(nc, *aps, out)
    r = run_bass_kernel_spmd(nc, [{f"in_{n}": v for n, v in arrays.items()}], core_ids=[0])
    got = r.results[0]["out"]
    return got.reshape(S, B, D).transpose(1, 0, 2)
```

```python
from contextlib import ExitStack
import math

import numpy as np

import concourse.bass as bass
from concourse import mybir

ALU = mybir.AluOpType
ACT = mybir.ActivationFunctionType
F32 = mybir.dt.float32
BF16 = mybir.dt.bfloat16
I32 = mybir.dt.int32
AX_X = mybir.AxisListType.X

B, S, D = 16, 128, 128
GB = 4
NG = B // GB
T = GB * S
LAYERS = 8
L0A, L0F, L1A, L1F, L2A, L2F, L3A, L3F = range(LAYERS)
LN_EPS = 1e-5

FF0, BLOCK = 384, 32
C0 = FF0 // 128
QMAX16, QMAX4 = 32767.0, 7.0
ROUND = 1.5 * 2.0 ** 23

H16, DH8 = 16, 8
PADH = 32
NQ = GB * 4
E1, TOP1, HID1 = 8, 2, 32
RMS_EPS = 1e-6
H4, DH32 = 4, 32
MLSTM_EPS = 1e-8
H8, DH64, TOP2 = 8, 64, 3
C2 = H8 * DH64 // 128
RANK = 8
LORA_SCALE = 16.0 / 8.0
FF3 = 512
C3 = FF3 // 128
X0 = 16
BIG = 1e30


def pieces():
    return [
        ("ident", 128, 128), ("ones", 128, 128), ("gates", 128, 8),
        ("l0_WkT", 128, 128), ("l0_bk", 128, 1), ("l0_WoT", 128, 128), ("l0_bo", 1, 128),
        ("l0_gate", 128, C0 * 128), ("l0_up", 128, C0 * 128), ("l0_down", 128, FF0),
        ("cosq", 128, 128), ("sinq", 128, 128), ("cosk", 128, 128), ("sink", 128, 128),
        ("causalT", 128, 128),
        ("l1_dw", 128, 3), ("l1_dwb", 128, 1), ("l1_pwT", 128, 128), ("l1_pwb", 128, 1),
        ("l1_routerT", 128, E1), ("l1_routerb", 128, E1), ("l1_expertT", 128, E1 * 128),
        ("l1_expertb", 1, E1 * 128), ("l1_outT", 128, 128), ("l1_outb", 128, 1), ("l1_norm", 128, 1),
        ("l1_downT", 128, HID1), ("l1_downb", HID1, 1), ("l1_upT", HID1, 128), ("l1_upb", 128, 1),
        ("before", 128, 64),
        ("l2_gateT", 128, 3 * 2 * H4), ("l2_gateb", 128, 2 * H4), ("beforeT", 128, 128),
        ("l2_outw", 128, 128), ("futureT", 128, 128),
        ("l2_Wq", 128, 512), ("l2_Wk", 128, 512), ("l2_Wv", 128, 512), ("l2_Ws", 128, H8),
        ("l2_Wo", 128, C2 * 128), ("l2_bo", H8, 128),
        ("l3_WqT", 128, 128), ("l3_WkT", 128, 128), ("l3_WvT", 128, 128),
        ("l3_Aq", RANK, 128), ("l3_Ak", RANK, 128), ("l3_Av", RANK, 128),
        ("l3_BqT", RANK, 128), ("l3_BkT", RANK, 128), ("l3_BvT", RANK, 128),
        ("l3_bq", 128, 1), ("l3_bk", 128, 1), ("headrows", 128, H16), ("l3_bv", 1, 128), ("l3_WoP", 128, 512),
        ("l3_bo", 1, 128),
        ("l3_W1T", 128, FF3), ("l3_b1", 128, C3), ("l3_W2T", 128, C3 * 128), ("l3_b2", 1, 128),
    ]


def columns():
    at, where = 0, {}
    for name, p, n in pieces():
        where[name] = (p, at, n)
        at += n
    return where, at


WHERE, COLS = columns()
PARTS = ["l0_bo", "l0_down", "causalT", "before", "futureT", "l2_bo", "l3_b2"]


class Ended:

    def __init__(self, eng, sem):
        self.eng, self.sem, self.total, self.base, self.n = eng, sem, 0, 0, 0

    def __call__(self, ins):
        self.n += 1
        ins.then_inc(self.sem, 1)
        self.eng.wait_ge(self.sem, self.base + self.n)

    def turn(self, i, per):
        self.base, self.n, self.per = self.total + i * per, 0, per

    def loop_over(self, turns):
        assert self.n == self.per, f"{self.n} in one turn, not {self.per}"
        self.total += turns * self.per
        self.base, self.n = self.total, 0

    def straight_over(self):
        self.total += self.n
        self.base, self.n = self.total, 0


def build(nc, x_in, ctx_in, ctxT_in, cell_in, seq_in, imask_in, pack_in, out, layers=LAYERS):
    with ExitStack() as stack:
        def sb(name, shape, dt=F32):
            return stack.enter_context(nc.sbuf_tensor(name, shape, dt))

        def sem(name):
            return stack.enter_context(nc.semaphore(name))

        x_all = sb("x_all", [128, B * D])
        ctx = sb("ctx", [128, B * D])
        ctxT = sb("ctxT", [128, B * S])
        pack = sb("pack", [128, COLS])
        tg = sb("tg", [128, LAYERS])
        identb = sb("identb", [128, 128], BF16)
        onesb = sb("onesb", [128, 128], BF16)
        onehot = sb("onehot", [96, GB * H4, 128], BF16)
        imask = sb("imask", [128, S], I32)

        def W(name, a=0, n=None):
            p, at, cols = WHERE[name]
            return pack[0:p, at + a:at + (cols if n is None else a + n)]

        stats = sb("stats", [128, GB, 6])
        moment = sb("moment", [128, GB, 3])
        mean = sb("mean", [128, GB])
        var = sb("var", [128, GB])
        rstd = sb("rstd", [128, GB])
        minus_half = sb("minus_half", [128, GB])
        minus_one = sb("minus_one", [128, 2])
        f_mean = sb("f_mean", [128, GB])
        f_var = sb("f_var", [128, GB])
        f_rstd = sb("f_rstd", [128, GB])
        f_amax = sb("f_amax", [128, 5, NG])
        f_scale = sb("f_scale", [128, 5, 4])
        g_sum = sb("g_sum", [128, 2, 4])
        xn = sb("xn", [128, GB, D])
        xnT = sb("xnT", [128, GB, S])
        w_max = sb("w_max", [128, 3 * FF0 // BLOCK])
        w_inv = sb("w_inv", [128, 3 * FF0 // BLOCK])
        k_rot = sb("k_rot", [128, B * D])
        kr_t = sb("kr_t", [128, GB, D])
        kr_r = sb("kr_r", [128, GB, D])
        area = sb("area", [128, 24576])
        areas = [0]
        AHEAD3, AHEAD2 = 9216, 20480

        def work(*shape, p=128, dt=F32):
            n = int(np.prod(shape)) // (2 if dt == BF16 else 1)
            a = area[0:p, areas[0]:areas[0] + n]
            areas[0] += n
            assert areas[0] <= 24576
            if dt == BF16:
                a = a.bitcast(BF16)
            if len(shape) == 2:
                a = a.rearrange("p (a b) -> p a b", a=shape[0])
            if len(shape) == 3:
                a = a.rearrange("p (a b c) -> p a b c", a=shape[0], b=shape[1])
            return a

        bank = [stack.enter_context(nc.psum_tensor(f"bank{k}", [128, 512], F32)) for k in range(8)]

        def by4(k):
            return bank[k][:, :].rearrange("p (b s) -> p b s", b=GB)

        ctx_loaded = sem("ctx_loaded")
        ctxT_loaded = sem("ctxT_loaded")
        masks_loaded = sem("masks_loaded")
        imask_loaded = sem("imask_loaded")
        part_loaded = [sem(f"part{n}_loaded") for n in range(len(PARTS))]
        x_updated = sem("x_updated")
        ln_var = sem("ln_var")
        ln_rstd = sem("ln_rstd")
        xn_ready = sem("xn_ready")
        xnT_psum = sem("xnT_psum")
        xnT_ready = sem("xnT_ready")
        y_ready = sem("y_ready")
        gates_ready = sem("gates_ready")
        onehot_zeroed = sem("onehot_zeroed")
        onehot_ready = sem("onehot_ready")
        dve_ended = sem("dve_ended")
        act_ended = sem("act_ended")
        pool_ended = sem("pool_ended")
        stored = sem("stored")

        def weights(eng, layer_part):
            eng.wait_ge(part_loaded[layer_part], 16)

        def group(t, i, b=0, n=GB):
            return t[:, bass.ds(i * T + b * 128, n * 128)]

        def group4(t, i):
            return group(t, i).rearrange("p (b d) -> p b d", b=GB)

        def moments_dve(dve, ended, stats, moment, mean, var):
            even, odd = stats[:, :, 1:3], stats[:, :, 4:6]
            dve.tensor_tensor(moment[:, :, 0:2], even, odd, ALU.add)
            ended(dve.tensor_tensor(moment[:, :, 2], even[:, :, 0], odd[:, :, 0], ALU.subtract))
            dve.tensor_scalar(mean, moment[:, :, 0], 0.5, None, ALU.mult)
            dve.tensor_scalar(var, moment[:, :, 1], 1.0 / D, LN_EPS, ALU.mult, ALU.add)
            ended(dve.tensor_tensor(moment[:, :, 2], moment[:, :, 2], moment[:, :, 2], ALU.mult))
            return dve.scalar_tensor_tensor(var, moment[:, :, 2], 0.25, var, ALU.mult, ALU.add)

        def normed(l):
            return 4 * (l if l < L0F else l - 1)

        def norm_stats_dve(dve, ended, l, i):
            for b in range(GB):
                last = dve.bn_stats(stats[:, b, :], group(x_all, i, b, 1))
            ended(last)
            moments_dve(dve, ended, stats[:, :, :], moment[:, :, :], mean[:, :], var[:, :]).then_inc(ln_var, 1)

        def norm_apply_dve(dve, l, i):
            dve.wait_ge(ln_rstd, normed(l) + i + 1)
            for b in range(GB):
                last = dve.tensor_scalar(xn[:, b, :], group(x_all, i, b, 1), mean[:, b:b + 1],
                                         rstd[:, b:b + 1], ALU.subtract, ALU.mult)
            last.then_inc(xn_ready, 1)
            dve.wait_ge(xn_ready, normed(l) + i + 1)

        def first_norm_dve(dve, ended, l):
            norm_stats_dve(dve, ended, l, 0)
            norm_apply_dve(dve, l, 0)
            ended.straight_over()

        def nothing():
            pass

        def over_groups_dve(dve, ended, l, per, body):
            def norms(l, i):
                return (lambda: norm_stats_dve(dve, ended, l, i)), (lambda: norm_apply_dve(dve, l, i))

            with dve.Fori(0, NG - 1) as i:
                ended.turn(i, per)
                body(i, *norms(l, i + 1))
            ended.loop_over(NG - 1)
            body(NG - 1, *(norms(l + 1, 0) if l + 1 < layers else (nothing, nothing)))
            ended.straight_over()

        def norm_pool(pool, l, i):
            pool.wait_ge(ln_var, normed(l) + i + 1)
            pool.tensor_tensor(rstd[:, :], var[:, :], minus_half[:, :], ALU.pow).then_inc(ln_rstd, 1)

        def norms_pool(pool, l):
            with pool.Fori(0, NG) as i:
                norm_pool(pool, l, i)

        def turned(l):
            return 4 * (l if l < L1A else l - 1)

        def turn_pe(pe, l, i, src=xn, ready=xn_ready):
            pe.wait_ge(ready, (normed(l) if ready is xn_ready else 0) + i + 1)
            for b in range(GB):
                last = pe.transpose(by4(0)[:, b, :], src[:, b, :], W("ident"))
            last.then_inc(xnT_psum, 1)

        def turned_act(act, l, i, dst=None):
            act.wait_ge(xnT_psum, turned(l) + i + 1)
            act.activation(xnT[:, :, :] if dst is None else dst, by4(0), ACT.Copy).then_inc(xnT_ready, 1)

        def update_dve(dve, l, i, k=None, src=None):
            dve.wait_ge(y_ready, 4 * l + i + 1)
            xs = group(x_all, i)
            dve.scalar_tensor_tensor(xs, bank[k][:, :] if src is None else src, tg[:, l:l + 1], xs,
                                     ALU.mult, ALU.add).then_inc(x_updated, 1)
            dve.wait_ge(x_updated, X0 + 4 * l + i + 1)

        def bias_pe(pe, k, row):
            pe.matmul(bank[k][:, :], W("ones")[0:1, :],
                      row.unsqueeze(1).to_broadcast([1, GB, 128]), start=True, stop=False)

        def begun(eng, l, i):
            eng.wait_ge(x_updated, X0 + 4 * l + i)

        def bc(ap, *shape):
            for axis, n in enumerate(shape):
                if n < 0:
                    ap = ap.unsqueeze(axis + 1)
            return ap.to_broadcast([ap.shape[0], *map(abs, shape)])

        def rank_dve(dve, ended, logit, sel, wide, top, between):
            lj = logit.unsqueeze(2).to_broadcast([128, GB, 8, 8])
            le = logit.unsqueeze(3).to_broadcast([128, GB, 8, 8])
            before = W("before").rearrange("p (e j) -> p e j", e=8).unsqueeze(1).to_broadcast([128, GB, 8, 8])
            gt, ge = wide[0], wide[1]
            dve.tensor_tensor(gt, lj, le, ALU.is_gt)
            ended(dve.tensor_tensor(ge, lj, le, ALU.is_ge))
            between[0]()
            ended(dve.tensor_tensor(ge, ge, gt, ALU.subtract))
            ended(dve.tensor_tensor(ge, ge, before, ALU.mult))
            between[1]()
            ended(dve.tensor_tensor(gt, gt, ge, ALU.add))
            between[2]()
            ended(dve.tensor_reduce(sel, gt, AX_X, ALU.add))
            ended(dve.tensor_scalar(sel, sel, float(top), None, ALU.is_lt))

        areas[0] = 0
        f_xn = work(B * D)
        cell, seqm = work(B * S), work(B * S)
        a_kT, a_s, a_p, a_pT, a_o, a_oT = (work(GB, 128) for _ in range(6))
        a_nmax, a_sum, a_rsum = work(GB), work(GB), work(GB)
        l0a_logs, l0a_k_psum, l0a_k, l0a_s_psum, l0a_masked, l0a_p, l0a_pT_psum, l0a_pT, l0a_o_psum, l0a_o, \
            l0a_oT_psum, l0a_oT = (sem(f"l0a_{n}") for n in "logs k_psum k s_psum masked p pT_psum pT o_psum o "
                                   "oT_psum oT".split())

        def l0a_act(act, ended):
            act.wait_ge(masks_loaded, 32)
            act.activation(cell, cell, ACT.Ln)
            act.activation(seqm, seqm, ACT.Ln).then_inc(l0a_logs, 1)

            def exponentials(i):
                act.wait_ge(l0a_masked, i + 1)
                for b in range(GB):
                    last = act.activation(a_p[:, b, :], a_s[:, b, :], ACT.Exp, bias=a_nmax[:, b:b + 1],
                                          accum_out=a_sum[:, b:b + 1])
                last.then_inc(l0a_p, 1)

            def tail(i):
                act.wait_ge(l0a_oT_psum, i + 1)
                act.activation(a_oT, by4(5), ACT.Copy).then_inc(l0a_oT, 1)

            turned_act(act, L0A, 0)
            exponentials(0)
            with act.Fori(0, NG - 1) as i:
                turned_act(act, L0A, i + 1)
                tail(i)
                exponentials(i + 1)
            tail(NG - 1)

        def l0f_norm_stats_dve(dve, ended, i):
            for b in range(GB):
                last = dve.bn_stats(stats[:, b, :], group(x_all, i, b, 1))
            ended(last)
            moments_dve(dve, ended, stats[:, :, :], moment[:, :, :], f_mean[:, :], f_var[:, :]).then_inc(l0f_var, 1)

        def l0f_norm_apply_dve(dve, ended, i):
            dve.wait_ge(l0f_rstd, i + 1)
            for b in range(GB):
                last = dve.tensor_scalar(group(f_xn, i, b, 1), group(x_all, i, b, 1), f_mean[:, b:b + 1],
                                         f_rstd[:, b:b + 1], ALU.subtract, ALU.mult)
            ended(last)
            ended(dve.tensor_reduce(f_amax[:, 0, i:i + 1] if isinstance(i, int) else f_amax[:, 0, bass.ds(i, 1)],
                                    group(f_xn, i), AX_X, ALU.max, apply_absolute_value=True))

        def l0f_norm_pool(pool, i):
            pool.wait_ge(l0f_var, i + 1)
            pool.tensor_tensor(f_rstd[:, :], f_var[:, :], minus_half[:, :], ALU.pow).then_inc(l0f_rstd, 1)

        def l0f_weights_dve(dve, ended):
            n = 3 * FF0 // BLOCK
            at = WHERE["l0_gate"][1]
            w3 = pack[:, at:at + 3 * FF0].rearrange("p (n k) -> p n k", k=BLOCK)

            def scaled():
                weights(dve, 1)
                ended(dve.tensor_reduce(w_max[:, :], w3, AX_X, ALU.max, apply_absolute_value=True))
                ended(dve.tensor_scalar(w_max[:, :], w_max[:, :], 1.0 / QMAX4, 1e-12, ALU.mult, ALU.max))
                ended(dve.reciprocal(w_inv[:, :], w_max[:, :]))
                ended(dve.tensor_tensor(w3, w3, bc(w_inv[:, :], n, -BLOCK), ALU.mult))

            def rounded():
                ended(dve.tensor_scalar(w3, w3, ROUND, ROUND, ALU.add, ALU.subtract))
                ended(dve.tensor_scalar(w3, w3, -QMAX4 - 1.0, QMAX4, ALU.max, ALU.min))
                dve.tensor_tensor(w3, w3, bc(w_max[:, :], n, -BLOCK), ALU.mult).then_inc(l0f_w, 1)

            return scaled, rounded

        def l0a_dve(dve, ended):
            norm_stats_dve(dve, ended, L0A, 0)
            dve.wait_ge(l0a_logs, 1)
            ended(dve.tensor_tensor(cell, cell, seqm, ALU.add))
            norm_apply_dve(dve, L0A, 0)

            def keys(i):
                dve.wait_ge(l0a_k_psum, i + 1)
                dve.tensor_scalar(a_kT, by4(1), W("l0_bk"), None, ALU.add).then_inc(l0a_k, 1)

            def masked(i):
                dve.wait_ge(l0a_s_psum, i + 1)
                ended(dve.tensor_tensor(a_s, by4(2), group4(cell, i), ALU.add))
                dve.tensor_reduce(a_nmax, a_s, AX_X, ALU.max, negate=True).then_inc(l0a_masked, 1)

            keys(0)
            masked(0)
            ended.straight_over()

            def turn(i, first_turn, last_turn):
                if not last_turn:
                    norm_stats_dve(dve, ended, L0A, i + 1)
                if not first_turn:
                    l0f_norm_stats_dve(dve, ended, i - 1)
                if not last_turn:
                    keys(i + 1)
                dve.wait_ge(l0a_p, i + 1)
                ended(dve.reciprocal(a_rsum, a_sum))
                dve.wait_ge(l0a_pT_psum, i + 1)
                dve.tensor_copy(a_pT, by4(3)).then_inc(l0a_pT, 1)
                if last_turn:
                    scale_weights()
                else:
                    norm_apply_dve(dve, L0A, i + 1)
                dve.wait_ge(l0a_o_psum, i + 1)
                dve.tensor_tensor(a_o, by4(4), bc(a_rsum, GB, -128), ALU.mult).then_inc(l0a_o, 1)
                if last_turn:
                    round_weights()
                else:
                    masked(i + 1)
                if not first_turn:
                    l0f_norm_apply_dve(dve, ended, i - 1)
                update_dve(dve, L0A, i, 6)

            scale_weights, round_weights = l0f_weights_dve(dve, ended)
            turn(0, True, False)
            ended.straight_over()
            with dve.Fori(1, NG - 1) as i:
                ended.turn(i - 1, 10)
                turn(i, False, False)
            ended.loop_over(NG - 2)
            turn(NG - 1, False, True)
            ended.straight_over()
            l0f_norm_stats_dve(dve, ended, NG - 1)
            l0f_norm_apply_dve(dve, ended, NG - 1)
            ended.straight_over()

        def l0a_pe(pe):
            def keys(i):
                pe.matmul(bank[1][:, :], W("l0_WkT"), group(ctxT, i), start=True, stop=True).then_inc(l0a_k_psum, 1)

            def scores(i):
                pe.wait_ge(l0a_k, i + 1)
                pe.wait_ge(xnT_ready, turned(L0A) + i + 1)
                for b in range(GB):
                    last = pe.matmul(by4(2)[:, b, :], xnT[:, b, :], a_kT[:, b, :], start=True, stop=True)
                last.then_inc(l0a_s_psum, 1)

            def turn(i, last_turn):
                if not last_turn:
                    keys(i + 1)
                pe.wait_ge(l0a_p, i + 1)
                for b in range(GB):
                    last = pe.transpose(by4(3)[:, b, :], a_p[:, b, :], W("ident"))
                last.then_inc(l0a_pT_psum, 1)
                if not last_turn:
                    turn_pe(pe, L0A, i + 1)
                pe.wait_ge(l0a_pT, i + 1)
                for b in range(GB):
                    last = pe.matmul(by4(4)[:, b, :], a_pT[:, b, :], group(ctx, i, b, 1), start=True, stop=True)
                last.then_inc(l0a_o_psum, 1)
                if not last_turn:
                    scores(i + 1)
                pe.wait_ge(l0a_o, i + 1)
                for b in range(GB):
                    last = pe.transpose(by4(5)[:, b, :], a_o[:, b, :], W("ident"))
                last.then_inc(l0a_oT_psum, 1)
                begun(pe, L0A, i)
                bias_pe(pe, 6, W("l0_bo"))
                pe.wait_ge(l0a_oT, i + 1)
                for b in range(GB):
                    last = pe.matmul(by4(6)[:, b, :], a_oT[:, b, :], W("l0_WoT"), start=False, stop=(b == GB - 1))
                last.then_inc(y_ready, 1)

            pe.wait_ge(ctxT_loaded, 16)
            keys(0)
            turn_pe(pe, L0A, 0)
            scores(0)
            pe.wait_ge(ctx_loaded, 16)
            with pe.Fori(0, NG - 1) as i:
                turn(i, False)
            turn(NG - 1, True)

        GW = C0 * T
        areas[0] = B * D
        f_gate, f_up, f_sig = (work(NG * GW) for _ in range(3))
        f_t, f_q = work(T), work(C0, T)
        f_s = f_q.rearrange("p c t -> p (c t)")
        f_unit = work(1)
        f_q2 = f_sig[:, 0:GW].rearrange("p (c t) -> p c t", c=C0)
        f_xnT = f_sig[:, 0:B * D]
        f_wT = work(9, 128)
        l0f_var, l0f_rstd, l0f_w, l0f_wT_psum, l0f_wT, l0f_max, l0f_allmax, l0f_xq, l0f_psum, l0f_copied, \
            l0f_gq, l0f_sig, l0f_u, l0f_scaled, l0f_t2, l0f_t3, l0f_t4, l0f_oq = (
                sem(f"l0f_{n}") for n in "var rstd w wT_psum wT max allmax xq psum copied gq sig u "
                "scaled t2 t3 t4 oq".split())

        def l0f_scale_dve(dve, ended, k, n, unit=None):
            dve.tensor_reduce(f_scale[:, k, 0:1], f_amax[:, k, 0:n], AX_X, ALU.max).then_inc(l0f_max, 1)
            dve.wait_ge(l0f_allmax, k + 1)
            if unit is not None:
                ended(dve.tensor_tensor(f_scale[:, k, 1:2], f_scale[:, k, 1:2], unit, ALU.mult))
            ended(dve.tensor_scalar(f_scale[:, k, 2:3], f_scale[:, k, 1:2], 1.0 / QMAX16, 1e-12, ALU.mult, ALU.max))
            last = dve.reciprocal(f_scale[:, k, 3:4], f_scale[:, k, 2:3])
            if unit is not None:
                ended(last)
                last = dve.tensor_tensor(f_scale[:, k, 3:4], f_scale[:, k, 3:4], unit, ALU.mult)
            last.then_inc(l0f_scaled, 1)
            dve.wait_ge(l0f_scaled, k + 1)

        def l0f_round_dve(dve, ended, k, dst, src, tmp):
            ended(dve.tensor_scalar(tmp, src, f_scale[:, k, 3:4], ROUND, ALU.mult, ALU.add))
            return dve.tensor_scalar(dst, tmp, ROUND, f_scale[:, k, 2:3], ALU.subtract, ALU.mult)

        def l0f_group(t, i):
            return t[:, i * GW:(i + 1) * GW]

        def l0f_pool(pool, ended):
            for k in range(5):
                if k == 1:
                    l1a_ahead_pool(pool, ended)
                pool.wait_ge(l0f_max, k + 1)
                pool.partition_all_reduce(f_scale[:, k, 1:2], f_scale[:, k, 0:1], 128,
                                          bass.bass_isa.ReduceOp.max).then_inc(l0f_allmax, 1)

        def l0f_round_act(act, k, dst, src):
            return act.activation(dst, src, ACT.Identity, scale=f_scale[:, k, 3:4], bias=ROUND)

        def l0f_act(act, ended):
            act.preload_act_table_set("sigmoid_and_others")
            for k in range(3):
                act.wait_ge(l0f_wT_psum, k + 1)
                act.activation(f_wT[:, 3 * k:3 * k + 3, :], by4(1 + k)[:, 0:3, :], ACT.Copy).then_inc(l0f_wT, 1)
            turned_act(act, L0F, 0, group4(f_xnT, 0))

            def turn(i, last_turn):
                for c in range(2 * C0):
                    act.wait_ge(l0f_psum, i * 2 * C0 + c + 1)
                    act.activation((f_gate, f_up)[c // C0][:, bass.ds(i * GW + c % C0 * T, T)], bank[1 + c][:, :],
                                   ACT.Copy).then_inc(l0f_copied, 1)
                    if c == 2 and not last_turn:
                        turned_act(act, L0F, i + 1, group4(f_xnT, i + 1))
            with act.Fori(0, NG - 1) as i:
                turn(i, False)
            turn(NG - 1, True)
            for i in range(NG):
                act.wait_ge(l0f_gq, i + 1)
                ended(act.activation(f_s, l0f_group(f_gate, i), ACT.Sigmoid))
                act.activation(l0f_group(f_sig, i), f_s, ACT.Identity, scale=65536.0, bias=ROUND).then_inc(l0f_sig, 1)
                act.wait_ge(l0f_sig, i + 1)
                l0f_round_act(act, 2, l0f_group(f_up, i), l0f_group(f_up, i)).then_inc(l0f_t2, 1)
            ended.straight_over()
            act.wait_ge(l0f_t2, NG)
            for i in range(NG):
                act.activation(l0f_group(f_up, i), l0f_group(f_up, i), ACT.Identity, bias=-ROUND).then_inc(l0f_u, 1)
            for k, done in ((3, l0f_t3), (4, l0f_t4)):
                act.wait_ge(l0f_scaled, k + 1)
                for i in range(NG):
                    l0f_round_act(act, k, l0f_group(f_gate, i), l0f_group(f_gate, i)).then_inc(done, 1)

        def l0f_dve(dve, ended):
            l0f_scale_dve(dve, ended, 0, NG)
            l0f_round_dve(dve, ended, 0, xn[:, :, :].rearrange("p b d -> p (b d)"), f_xn[:, 0:T], f_t).then_inc(l0f_xq, 1)
            ended.straight_over()

            def rounded(i):
                dve.wait_ge(xnT_psum, turned(L0F) + i)
                l0f_round_dve(dve, ended, 0, xn[:, :, :].rearrange("p b d -> p (b d)"), group(f_xn, i), f_t)\
                    .then_inc(l0f_xq, 1)

            def maxima(i, k, t):
                dve.wait_ge(l0f_copied, (i * 2 + k) * C0)
                ended(dve.tensor_reduce(f_amax[:, k, bass.ds(i, 1)], t[:, bass.ds(i * GW, GW)], AX_X, ALU.max,
                                        apply_absolute_value=True))

            rounded(1)
            ended.straight_over()
            with dve.Fori(0, NG - 2) as i:
                ended.turn(i, 3)
                maxima(i, 1, f_gate)
                rounded(i + 2)
                maxima(i, 2, f_up)
            ended.loop_over(NG - 2)
            for i in (NG - 2, NG - 1):
                maxima(i, 1, f_gate)
                maxima(i, 2, f_up)
            l0f_scale_dve(dve, ended, 1, NG)
            l0f_scale_dve(dve, ended, 2, NG)
            for i in range(NG):
                g = l0f_group(f_gate, i)
                l0f_round_dve(dve, ended, 1, g, g, g).then_inc(l0f_gq, 1)
            for i in range(NG):
                g = l0f_group(f_gate, i)
                s = l0f_group(f_sig, i)
                dve.wait_ge(l0f_sig, i + 1)
                ended(dve.tensor_scalar(s, s, ROUND, 65535.0, ALU.subtract, ALU.min))
                ended(dve.scalar_tensor_tensor(g, s, 1.0 / 65536.0, g, ALU.mult, ALU.mult))
                ended(dve.tensor_reduce(f_amax[:, 3, i:i + 1], g, AX_X, ALU.max, apply_absolute_value=True))
            l0f_scale_dve(dve, ended, 3, NG)
            ended(dve.tensor_tensor(f_unit, f_scale[:, 3, 2:3], f_scale[:, 2, 2:3], ALU.mult))
            dve.wait_ge(l0f_u, NG)
            for i in range(NG):
                g = l0f_group(f_gate, i)
                dve.wait_ge(l0f_t3, i + 1)
                ended(dve.scalar_tensor_tensor(g, g, ROUND, l0f_group(f_up, i), ALU.subtract, ALU.mult))
                ended(dve.tensor_reduce(f_amax[:, 4, i:i + 1], g, AX_X, ALU.max, apply_absolute_value=True))
            l0f_scale_dve(dve, ended, 4, NG, unit=f_unit)
            ended.straight_over()
            with dve.Fori(0, NG // 2) as pair:
                for k, q in enumerate((f_q, f_q2)):
                    i = pair * 2 + k
                    dve.wait_ge(l0f_t4, i + 1)
                    dve.tensor_scalar(q.rearrange("p c t -> p (c t)"), f_gate[:, bass.ds(i * GW, GW)], ROUND,
                                      f_scale[:, 4, 2:3], ALU.subtract, ALU.mult).then_inc(l0f_oq, 1)
                for k in range(2):
                    update_dve(dve, L0F, pair * 2 + k, 1 + k)

        def l0f_pe(pe):
            pe.wait_ge(l0f_w, 1)
            w = pack[:, WHERE["l0_gate"][1]:][:, 0:3 * FF0].rearrange("p (n k) -> p n k", k=128)
            for k in range(3):
                for c in range(3):
                    last = pe.transpose(by4(1 + k)[:, c, :], w[:, 3 * k + c, :], W("ident"))
                last.then_inc(l0f_wT_psum, 1)
            pe.wait_ge(l0f_wT, 3)
            turn_pe(pe, L0F, 0, ready=l0f_xq)

            def turn(i, first_turn, last_turn):
                pe.wait_ge(xnT_ready, turned(L0F) + i + 1)
                for c in range(2 * C0):
                    if c == 2 and not last_turn:
                        turn_pe(pe, L0F, i + 1, ready=l0f_xq)
                    if not first_turn:
                        pe.wait_ge(l0f_copied, (i - 1) * 2 * C0 + c + 1)
                    pe.matmul(bank[1 + c][:, :], f_wT[:, c, :], group(f_xnT, i), start=True, stop=True)\
                      .then_inc(l0f_psum, 1)

            turn(0, True, False)
            with pe.Fori(1, NG - 1) as i:
                turn(i, False, False)
            turn(NG - 1, False, True)
            with pe.Fori(0, NG // 2) as pair:
                for k, q in enumerate((f_q, f_q2)):
                    pe.wait_ge(l0f_oq, pair * 2 + k + 1)
                    for b in range(GB):
                        for c in range(C0):
                            last = pe.matmul(by4(1 + k)[:, b, :], q[:, c, b * 128:b * 128 + 128], f_wT[:, 6 + c, :],
                                             start=(c == 0), stop=(c == C0 - 1))
                    last.then_inc(y_ready, 1)

        HALF = 512
        NK = 2 * GB
        areas[0] = 0
        r_kv = work(NK, HALF)
        r_t, r_r, r_q, r_o = (work(GB, D) for _ in range(4))
        r_m = work(2, HALF)
        l1a_q, l1a_kv, l1a_sum_psum, l1a_m, l1a_o = (
            sem(f"l1a_{n}") for n in "q kv sum_psum m o".split())

        def pairs(ap, k):
            return ap.rearrange("p b (h two) -> p b h two", two=2)[:, :, :, k]

        def pairs2(ap, k):
            return ap.rearrange("p (h two) -> p h two", two=2)[:, :, k].unsqueeze(1).to_broadcast([128, GB, 64])

        def l1a_rotate(eng, ended, src, cos, sin, t, r, dst):
            c = W(cos).unsqueeze(1).to_broadcast([128, GB, D])
            eng.tensor_tensor(t, src, c, ALU.mult)
            eng.tensor_tensor(pairs(r, 0), pairs(src, 1), pairs2(W(sin), 0), ALU.mult)
            ended(eng.tensor_tensor(pairs(r, 1), pairs(src, 0), pairs2(W(sin), 1), ALU.mult))
            return eng.tensor_tensor(dst, t, r, ALU.add)

        def l1a_half(ap, n, last):
            b, half = divmod(n, 2)
            a = ap[:, b * D + half * 64:b * D + half * 64 + 64].rearrange("p (h f) -> p h f", h=8)
            return a.unsqueeze(3 if last else 2).to_broadcast([128, 8, DH8, DH8])

        def l0a_pool(pool, ended):
            for i in range(2):
                norm_pool(pool, L0A, i)
            with pool.Fori(1, NG - 1) as i:
                norm_pool(pool, L0A, i + 1)
                l0f_norm_pool(pool, i - 1)
            for i in range(NG - 2, NG):
                l0f_norm_pool(pool, i)

        def l1a_ahead_pool(pool, ended):
            weights(pool, 2)
            pool.wait_ge(ctx_loaded, 16)
            with pool.Fori(0, NG) as i:
                ended.turn(i, 2)
                ended(l1a_rotate(pool, ended, group4(ctx, i), "cosk", "sink", kr_t[:, :, :], kr_r[:, :, :],
                                 group4(k_rot, i)))
            ended.loop_over(NG)

        def l1a_pool(pool, ended):
            pool.wait_ge(x_updated, X0 + 4 * L1A)

            def outer(i, first):
                norm_pool(pool, L1A, i)
                k, v = group(k_rot, i), group(ctx, i)
                for n in range(NK):
                    if not first:
                        pool.wait_ge(l1a_sum_psum, (i - 1) * NK + n + 1)
                    pool.tensor_tensor(r_kv[:, n, :].rearrange("p (h e d) -> p h e d", h=8, e=DH8),
                                       l1a_half(v, n, True), l1a_half(k, n, False), ALU.mult).then_inc(l1a_kv, 1)

            outer(0, True)
            with pool.Fori(1, NG) as i:
                outer(i, False)

        def l1a_dve(dve, ended):
            weights(dve, 2)
            first_norm_dve(dve, ended, L1A)

            def body(i, stats, apply):
                l1a_rotate(dve, ended, xn[:, :, :], "cosq", "sinq", r_t, r_r, r_q).then_inc(l1a_q, 1)
                dve.wait_ge(l1a_q, i + 1)
                q = r_q.rearrange("p b d -> p (b d)")

                def by_q(n):
                    dve.wait_ge(l1a_sum_psum, i * NK + n + 1)
                    dve.tensor_tensor(r_m[:, n % 2, :].rearrange("p (h e d) -> p h e d", h=8, e=DH8),
                                      bank[n][:, :].rearrange("p (h e d) -> p h e d", h=8, e=DH8),
                                      l1a_half(q, n, False), ALU.mult).then_inc(l1a_m, 1)

                by_q(0)
                for n in range(NK):
                    if n + 1 < NK:
                        if n:
                            dve.wait_ge(l1a_o, i * (NK - 1) + n)
                        by_q(n + 1)
                    dve.wait_ge(l1a_m, i * NK + n + 1)
                    b, half = divmod(n, 2)
                    last = dve.tensor_reduce(r_o[:, b, half * 64:half * 64 + 64],
                                             r_m[:, n % 2, :].rearrange("p (f d) -> p f d", d=DH8), AX_X, ALU.add)
                    last.then_inc(l1a_o if n < NK - 1 else y_ready, 1)
                    if n == 3:
                        stats()
                    if n == 5:
                        apply()
                update_dve(dve, L1A, i, src=r_o.rearrange("p b d -> p (b d)"))
            over_groups_dve(dve, ended, L1A, 4, body)

        def l1a_pe(pe):
            weights(pe, 2)
            begun(pe, L1A, 0)

            def sums(i, first):
                for n in range(NK):
                    pe.wait_ge(l1a_kv, i * NK + n + 1)
                    if not first:
                        pe.wait_ge(l1a_m, (i - 1) * NK + n + 1)
                    pe.matmul(bank[n][:, :], W("causalT"), r_kv[:, n, :], start=True, stop=True)\
                      .then_inc(l1a_sum_psum, 1)

            sums(0, True)
            with pe.Fori(1, NG) as i:
                sums(i, False)

        areas[0] = 0
        e_x = work(GB, S + 2)
        e_conv, e_silu, e_x1, e_y, e_sq, e_ms, e_rr, e_h, e_o = (work(GB, S) for _ in range(9))
        e_logit, e_shift, e_exp, e_sel, e_rw = (work(GB, E1) for _ in range(5))
        e_wide = work(2, GB, 64).rearrange("p k b (e j) -> p k b e j", e=8)
        e_max, e_sum, e_rsum = work(GB), work(GB), work(GB)
        e_gelu = work(GB, S, p=HID1)
        e_ye, e_ys = work(2, 4, D), work(2, 4, D)
        e_add = work(2, 4 * D)
        e_combT = work(GB, S)
        e_left, e_mid = work(E1 * D, p=1), work(E1 * D, p=1, dt=BF16)
        e_bias = work(E1 * D, p=96, dt=BF16)
        l1f_const, l1f_conv, l1f_pw_psum, l1f_silu, l1f_x1, l1f_logit_psum, l1f_shift, l1f_exp, \
            l1f_ye_psum, l1f_ye, l1f_ys, l1f_add, l1f_combT_psum, l1f_combT, l1f_out_psum, l1f_sq, \
            l1f_ms_psum, l1f_ms, l1f_rr, l1f_h, l1f_down_psum, l1f_gelu, l1f_up_psum, l1f_o = (
                sem(f"l1f_{n}") for n in "const conv pw_psum silu x1 logit_psum shift exp ye_psum ye ys add "
                "combT_psum combT out_psum sq ms_psum ms rr h down_psum gelu up_psum o".split())
        NE = 2 * GB

        def l1f_act(act, ended):
            def silu(i):
                act.wait_ge(l1f_pw_psum, i + 1)
                act.activation(e_silu, by4(1), ACT.Silu, bias=W("l1_pwb")).then_inc(l1f_silu, 1)

            def turn(i, last):
                for m in range(NE):
                    act.wait_ge(l1f_ye_psum, i * NE + m + 1)
                    if m >= 2:
                        act.wait_ge(l1f_ys, i * NE + m - 1)
                    act.activation(e_ye[:, m % 2, :, :], by4(4 + m % 2), ACT.Silu).then_inc(l1f_ye, 1)
                if not last:
                    turned_act(act, L1F, i + 1, e_x[:, :, 2:])
                act.wait_ge(l1f_combT_psum, (i + 1) * GB)
                act.activation(e_combT, by4(3), ACT.Copy).then_inc(l1f_combT, 1)
                if not last:
                    silu(i + 1)
                act.preload_act_table_set("natural_log_exp_and_others")
                act.wait_ge(l1f_ms_psum, i + 1)
                act.activation(e_ms, by4(6), ACT.Ln, scale=1.0 / D, bias=RMS_EPS).then_inc(l1f_ms, 1)
                act.wait_ge(l1f_ms, i + 1)
                act.activation(e_rr, e_ms, ACT.Exp, scale=-0.5).then_inc(l1f_rr, 1)
                if not last:
                    power(i + 1)
                act.preload_act_table_set("gelu_and_others")
                act.wait_ge(l1f_down_psum, i + 1)
                act.activation(e_gelu, by4(4)[0:HID1], ACT.Gelu, bias=W("l1_downb")).then_inc(l1f_gelu, 1)
                if not last:
                    act.preload_act_table_set("silu_and_others")

            def power(i):
                act.wait_ge(l1f_shift, i + 1)
                act.activation(e_exp, e_shift, ACT.Exp).then_inc(l1f_exp, 1)

            act.preload_act_table_set("silu_and_others")
            turned_act(act, L1F, 0, e_x[:, :, 2:])
            silu(0)
            act.preload_act_table_set("natural_log_exp_and_others")
            power(0)
            act.preload_act_table_set("silu_and_others")
            with act.Fori(0, NG - 1) as i:
                turn(i, False)
            turn(NG - 1, True)

        def l1f_pool(pool, ended):
            norm_pool(pool, L1F, 0)

            def turn(i, last):
                for b in range(GB):
                    if b == 1 and not (last and layers == L2A):
                        norm_pool(pool, *((L2A, 0) if last else (L1F, i + 1)))
                    pool.wait_ge(l1f_ys, i * NE + 2 * b + 2)
                    if b >= 2:
                        pool.wait_ge(l1f_combT_psum, i * GB + b - 1)
                    flat = e_ys.rearrange("p k e d -> p k (e d)")
                    pool.tensor_tensor(e_add[:, b % 2, :], flat[:, 0, :], flat[:, 1, :], ALU.add).then_inc(l1f_add, 1)

            with pool.Fori(0, NG - 1) as i:
                turn(i, False)
            turn(NG - 1, True)
            l3f_weights_pool(pool, ended)

        def l1f_dve(dve, ended):
            weights(dve, 3)
            weights(dve, 6)
            for k, w in enumerate(("l3_W1T", "l3_W2T")):
                last = dve.tensor_reduce(g_sum[:, k, 0:1], W(w), AX_X, ALU.add, apply_absolute_value=True)
            last.then_inc(l3f_sum, 1)
            dve.memset(e_x[:, :, 0:2], 0.0)
            ended(dve.memset(e_bias, 0.0))
            ended(dve.tensor_copy(e_bias[0:1, :], W("l1_expertb")))
            ended(dve.tensor_tensor(e_left, W("l1_expertb"), e_bias[0:1, :], ALU.subtract))
            ended(dve.tensor_copy(e_bias[32:33, :], e_left))
            ended(dve.tensor_copy(e_mid, e_left))
            ended(dve.tensor_tensor(e_left, e_left, e_mid, ALU.subtract))
            dve.tensor_copy(e_bias[64:65, :], e_left).then_inc(l1f_const, 1)
            dve.wait_ge(l1f_const, 1)

            def conv(i):
                dve.wait_ge(xnT_ready, turned(L1F) + i + 1)
                ended(dve.tensor_scalar(e_conv, e_x[:, :, 0:S], W("l1_dw", 0, 1), W("l1_dwb"), ALU.mult, ALU.add))
                ended(dve.scalar_tensor_tensor(e_conv, e_x[:, :, 1:S + 1], W("l1_dw", 1, 1), e_conv, ALU.mult, ALU.add))
                dve.scalar_tensor_tensor(e_conv, e_x[:, :, 2:], W("l1_dw", 2, 1), e_conv, ALU.mult, ALU.add)\
                   .then_inc(l1f_conv, 1)

            def x1(i):
                dve.wait_ge(l1f_silu, i + 1)
                dve.tensor_tensor(e_x1, e_x[:, :, 2:], e_silu, ALU.add).then_inc(l1f_x1, 1)

            def logits(i):
                dve.wait_ge(l1f_logit_psum, i + 1)
                ended(dve.tensor_tensor(e_logit, bank[2][:, 0:GB * E1].rearrange("p (b e) -> p b e", b=GB),
                                        W("l1_routerb").unsqueeze(1).to_broadcast([128, GB, E1]), ALU.add))
                ended(dve.tensor_reduce(e_max, e_logit, AX_X, ALU.max))
                dve.tensor_tensor(e_shift, e_logit, bc(e_max, GB, -E1), ALU.subtract).then_inc(l1f_shift, 1)

            def router(i):
                rank_dve(dve, ended, e_logit, e_sel, (e_wide[:, 0], e_wide[:, 1]), TOP1, 3 * (nothing,))
                dve.wait_ge(l1f_exp, i + 1)
                ended(dve.tensor_tensor(e_sel, e_exp, e_sel, ALU.mult))
                ended(dve.tensor_reduce(e_sum, e_sel, AX_X, ALU.add))
                ended(dve.reciprocal(e_rsum, e_sum))
                ended(dve.tensor_tensor(e_rw, e_sel, bc(e_rsum, GB, -E1), ALU.mult))

            def body(i, stats, apply):
                last = isinstance(i, int)
                for m in range(NE):
                    b, half = divmod(m, 2)
                    dve.wait_ge(l1f_ye, i * NE + m + 1)
                    if m >= 2:
                        dve.wait_ge(l1f_add, i * GB + b)
                    dve.tensor_tensor(e_ys[:, half, :, :], e_ye[:, half, :, :], bc(e_rw[:, b, 4 * half:4 * half + 4], 4, -D),
                                      ALU.mult).then_inc(l1f_ys, 1)
                    if m == 2:
                        stats()
                    if m == 5:
                        apply()
                if not last:
                    conv(i + 1)
                dve.wait_ge(l1f_out_psum, i + 1)
                ended(dve.scalar_tensor_tensor(e_y, by4(7), W("l1_outb"), e_x1, ALU.add, ALU.add))
                dve.tensor_tensor(e_sq, e_y, e_y, ALU.mult).then_inc(l1f_sq, 1)
                if not last:
                    x1(i + 1)
                    logits(i + 1)
                dve.wait_ge(l1f_rr, i + 1)
                dve.scalar_tensor_tensor(e_h, e_y, W("l1_norm"), e_rr, ALU.mult, ALU.mult).then_inc(l1f_h, 1)
                if not last:
                    router(i + 1)
                dve.wait_ge(l1f_up_psum, i + 1)
                dve.wait_ge(l1f_h, i + 1)
                dve.scalar_tensor_tensor(e_o, by4(5), W("l1_upb"), e_h, ALU.add, ALU.add).then_inc(l1f_o, 1)
                update_dve(dve, L1F, i, 3)

            conv(0)
            x1(0)
            logits(0)
            router(0)
            ended.straight_over()
            over_groups_dve(dve, ended, L1F, 18, body)

        def l1f_pe(pe):
            weights(pe, 3)
            pe.wait_ge(l1f_const, 1)

            def convolved(i):
                pe.wait_ge(l1f_conv, i + 1)
                pe.matmul(bank[1][:, :], W("l1_pwT"), e_conv, start=True, stop=True).then_inc(l1f_pw_psum, 1)

            def logits(i):
                pe.wait_ge(l1f_x1, i + 1)
                for b in range(GB):
                    last = pe.matmul(bank[2][:, b * E1:(b + 1) * E1], e_x1[:, b, :], W("l1_routerT"), start=True, stop=True)
                last.then_inc(l1f_logit_psum, 1)

            def expert(i, m):
                b, half = divmod(m, 2)
                if m >= 2:
                    pe.wait_ge(l1f_ye, i * NE + m - 1)
                pe.matmul(bank[4 + m % 2][:, :], onesb[0:96, :], e_bias[:, half * 512:(half + 1) * 512],
                          start=True, stop=False)
                pe.matmul(bank[4 + m % 2][:, :], e_x1[:, b, :], W("l1_expertT", half * 512, 512), start=False, stop=True)\
                  .then_inc(l1f_ye_psum, 1)

            def turn(i, last):
                def combined(b):
                    if b == 0:
                        begun(pe, L1F, i)
                    pe.wait_ge(l1f_add, i * GB + b + 1)
                    for e in range(4):
                        mm = pe.matmul(by4(3)[:, b, :], e_add[:, b % 2, e * D:(e + 1) * D], W("ident"),
                                       start=(e == 0), stop=(e == 3))
                    mm.then_inc(l1f_combT_psum, 1)

                for m in range(NE):
                    expert(i, m)
                    if m in (4, 6):
                        combined(m // 2 - 2)
                if not last:
                    turn_pe(pe, L1F, i + 1)
                combined(GB - 2)
                combined(GB - 1)
                pe.wait_ge(l1f_combT, i + 1)
                pe.matmul(bank[7][:, :], W("l1_outT"), e_combT, start=True, stop=True).then_inc(l1f_out_psum, 1)
                if not last:
                    convolved(i + 1)
                pe.wait_ge(l1f_sq, i + 1)
                pe.matmul(bank[6][:, :], W("ones"), e_sq, start=True, stop=True).then_inc(l1f_ms_psum, 1)
                if not last:
                    logits(i + 1)
                pe.wait_ge(l1f_h, i + 1)
                pe.matmul(bank[4][0:HID1, :], W("l1_downT"), e_h, start=True, stop=True).then_inc(l1f_down_psum, 1)
                pe.wait_ge(l1f_gelu, i + 1)
                pe.matmul(bank[5][:, :], W("l1_upT"), e_gelu, start=True, stop=True).then_inc(l1f_up_psum, 1)
                pe.wait_ge(l1f_o, i + 1)
                for b in range(GB):
                    mm = pe.transpose(by4(3)[:, b, :], e_o[:, b, :], W("ident"))
                mm.then_inc(y_ready, 1)

            turn_pe(pe, L1F, 0)
            begun(pe, L1F, 0)
            convolved(0)
            logits(0)
            with pe.Fori(0, NG - 1) as i:
                turn(i, False)
            turn(NG - 1, True)

        areas[0] = 0
        NB = GB * H4
        m_g = work(GB, 2 * H4)
        m_log, m_lf, m_a, m_end = (work(NB) for _ in range(4))
        m_M, m_left = work(S, p=NB), work(S, p=NB)
        m_mid = work(S, p=NB, dt=BF16)
        m_nM = work(S, p=96, dt=BF16)
        m_zero = work(S, p=NB)
        m_kT = work(GB, S)
        m_nextT, m_next_kT = work(GB, S), work(GB, S)
        m_v = work(NB, DH32 + 1)
        m_d, m_c = work(2, GB, S), work(2, T)
        m_den, m_abs, m_h, m_sq = work(NB), work(NB), work(NB, DH32), work(NB, DH32)
        m_mean, m_var, m_rstd = work(NB), work(NB), work(NB)
        m_scale = work(D)
        m_wkv = work(2 * H4)
        m_future = work(S, dt=BF16)
        l2a_const, l2a_kT, l2a_v, l2a_gates_psum, l2a_g, l2a_log, l2a_lf, l2a_cs_psum, l2a_a, l2a_aT_psum, l2a_M, \
            l2a_nM, l2a_MT_psum, l2a_end_in, l2a_end, l2a_bias_psum, l2a_qk_psum, l2a_d, l2a_c, l2a_hv, l2a_var, \
            l2a_rstd = (
                sem(f"l2a_{n}") for n in "const kT v gates_psum g log lf cs_psum a aT_psum M nM MT_psum end_in end "
                "bias_psum qk_psum d c hv var rstd".split())
        GATES, UPTO, BEFORE, AT, MT = 0, 2 * NB, 3 * NB, 4 * NB, 4 * NB + S

        def l1a_act(act, ended):
            act.wait_ge(onehot_zeroed, 1)
            for k in range(3):
                rows = slice(32 * k, 32 * k + NB)
                last = act.activation(onehot[rows, :, :], W("ident")[rows, rows].unsqueeze(2).to_broadcast([NB, NB, 128]),
                                      ACT.Copy)
            last.then_inc(onehot_ready, 1)

        def l2a_act(act, ended):
            def ahead(i):
                turned_act(act, L2A, i, m_nextT)
                act.wait_ge(l2a_g, i + 1)
                log = m_log.rearrange("p (b h) -> p b h", b=GB)
                ended(act.activation(log, m_g[:, :, H4:], ACT.Abs))
                ended(act.activation(m_log, m_log, ACT.Exp, scale=-1.0))
                act.activation(m_log, m_log, ACT.Ln, bias=1.0).then_inc(l2a_log, 1)

            def inputs(i):
                act.activation(xnT[:, :, :], by4(0), ACT.Copy)
                act.activation(m_kT, group4(ctxT, i), ACT.Copy)
                act.activation(m_v[:, :, 0:DH32], group(ctx, i).rearrange("p (n d) -> p n d", d=DH32), ACT.Copy)\
                   .then_inc(l2a_v, 1)

            def end(i):
                act.wait_ge(l2a_end_in, i + 1)
                act.activation(m_end, m_end, ACT.Exp, scale=-1.0).then_inc(l2a_end, 1)

            def keys_ahead(i):
                act.activation(m_next_kT, group4(ctxT, i), ACT.Copy).then_inc(l2a_kT, 1)

            def decay(i, h):
                act.wait_ge(l2a_bias_psum, i * H4 + h + 1)
                if h >= 2:
                    act.wait_ge(l2a_c, i * H4 + h - 1)
                for b in range(GB):
                    last = act.activation(m_d[:, h % 2, b, :], by4(4 + h % 2)[:, b, :], ACT.Exp,
                                          bias=m_a[:, b * H4 + h:b * H4 + h + 1])
                last.then_inc(l2a_d, 1)

            def tail(i):
                act.wait_ge(l2a_var, i + 1)
                ended(act.activation(m_rstd, m_var, ACT.Ln, scale=1.0 / DH32, bias=LN_EPS))
                act.activation(m_rstd, m_rstd, ACT.Exp, scale=-0.5).then_inc(l2a_rstd, 1)

            act.preload_act_table_set("natural_log_exp_and_others")
            act.wait_ge(l2a_const, 1)
            keys_ahead(0)
            ahead(0)
            inputs(0)
            decay(0, 0)
            decay(0, 1)
            end(0)
            ended.straight_over()
            with act.Fori(0, NG - 1) as i:
                ended.turn(i, 3)
                keys_ahead(i + 1)
                decay(i, 2)
                decay(i, 3)
                ahead(i + 1)
                act.wait_ge(y_ready, 4 * L2A + i + 1)
                inputs(i + 1)
                decay(i + 1, 0)
                tail(i)
                decay(i + 1, 1)
                end(i + 1)
            ended.loop_over(NG - 1)
            decay(NG - 1, 2)
            decay(NG - 1, 3)
            tail(NG - 1)
            ended.straight_over()

        def l2a_dve(dve, ended):
            weights(dve, 4)
            dve.memset(m_v[:, :, DH32:], 1.0)
            dve.memset(m_zero, 0.0)
            dve.memset(m_nM, 0.0)
            dve.tensor_tensor(m_wkv, W("l2_gateT", 2 * H4, 2 * H4), W("l2_gateT", 4 * H4, 2 * H4), ALU.add)
            dve.tensor_copy(m_future, W("futureT"))
            dve.tensor_scalar(m_scale, W("l2_outw"), 1.0, None, ALU.add).then_inc(l2a_const, 1)
            dve.wait_ge(l2a_const, 1)

            def gates(i):
                dve.wait_ge(l2a_gates_psum, i + 1)
                dve.tensor_tensor(m_g, bank[3][:, GATES:GATES + 2 * NB].rearrange("p (b g) -> p b g", b=GB),
                                  W("l2_gateb").unsqueeze(1).to_broadcast([128, GB, 2 * H4]), ALU.add).then_inc(l2a_g, 1)

            def forget(i):
                dve.wait_ge(l2a_log, i + 1)
                dve.scalar_tensor_tensor(m_lf.rearrange("p (b h) -> p b h", b=GB), m_g[:, :, H4:], 0.0,
                                         m_log.rearrange("p (b h) -> p b h", b=GB), ALU.min, ALU.subtract)\
                   .then_inc(l2a_lf, 1)

            def a(i):
                dve.wait_ge(l2a_cs_psum, i + 1)
                dve.tensor_tensor(m_a.rearrange("p (b h) -> p b h", b=GB), m_g[:, :, 0:H4],
                                  bank[3][:, BEFORE:BEFORE + NB].rearrange("p (b h) -> p b h", b=GB), ALU.subtract)\
                   .then_inc(l2a_a, 1)

            def running_max(i):
                dve.wait_ge(l2a_aT_psum, i + 1)
                dve.tensor_tensor_scan(m_M, m_zero, bank[3][0:NB, AT:AT + S], -BIG, ALU.add, ALU.max).then_inc(l2a_M, 1)
                dve.wait_ge(l2a_M, i + 1)
                ended(dve.tensor_scalar(m_nM[0:NB, :], m_M, -1.0, None, ALU.mult))
                ended(dve.scalar_tensor_tensor(m_left, m_M, -1.0, m_nM[0:NB, :], ALU.mult, ALU.subtract))
                dve.tensor_copy(m_nM[32:32 + NB, :], m_left)
                ended(dve.tensor_copy(m_mid, m_left))
                dve.tensor_tensor(m_nM[64:64 + NB, :], m_left, m_mid, ALU.subtract).then_inc(l2a_nM, 1)

            def end(i):
                dve.wait_ge(l2a_MT_psum, i + 1)
                ended(dve.tensor_copy(m_end, bank[3][:, MT:MT + NB]))
                dve.tensor_tensor(m_end, m_end, bank[3][:, UPTO:UPTO + NB], ALU.add).then_inc(l2a_end_in, 1)

            def scaled(i, h):
                dve.wait_ge(l2a_qk_psum, i * H4 + h + 1)
                dve.wait_ge(l2a_d, i * H4 + h + 1)
                if h >= 2:
                    dve.wait_ge(l2a_hv, i * (H4 - 1) + h - 1)
                dve.scalar_tensor_tensor(m_c[:, h % 2, :], bank[6 + h % 2][:, :], DH32 ** -0.5,
                                         m_d[:, h % 2, :, :].rearrange("p b s -> p (b s)"), ALU.mult, ALU.mult)\
                   .then_inc(l2a_c, 1)

            def body(i, stats, apply):
                last = isinstance(i, int)
                stats()
                scaled(i, 2)
                apply()
                scaled(i, 3)
                if not last:
                    gates(i + 1)
                    forget(i + 1)
                dve.wait_ge(l2a_end, i + 1)
                dve.wait_ge(y_ready, 4 * L2A + i + 1)
                n = NB // 2
                for half in range(2):
                    hv = bank[1 + half][:, 0:n * (DH32 + 1)].rearrange("p (n d) -> p n d", d=DH32 + 1)
                    mm = dve.tensor_copy(m_den[:, half * n:(half + 1) * n], hv[:, :, DH32])
                ended(mm)
                if not last:
                    a(i + 1)
                ended(dve.scalar_tensor_tensor(m_abs, m_den, -1.0, m_den, ALU.mult, ALU.max))
                ended(dve.tensor_tensor(m_abs, m_abs, m_end, ALU.max))
                ended(dve.tensor_scalar(m_abs, m_abs, MLSTM_EPS, None, ALU.add))
                ended(dve.reciprocal(m_den, m_abs))
                for half in range(2):
                    hv = bank[1 + half][:, 0:n * (DH32 + 1)].rearrange("p (n d) -> p n d", d=DH32 + 1)
                    mm = dve.tensor_tensor(m_h[:, half * n:(half + 1) * n, :], hv[:, :, 0:DH32],
                                           bc(m_den[:, half * n:(half + 1) * n], n, -DH32), ALU.mult)
                ended(mm)
                if not last:
                    running_max(i + 1)
                ended(dve.tensor_reduce(m_mean, m_h, AX_X, ALU.add))
                ended(dve.tensor_scalar(m_mean, m_mean, 1.0 / DH32, None, ALU.mult))
                ended(dve.tensor_tensor(m_h, m_h, bc(m_mean, NB, -DH32), ALU.subtract))
                ended(dve.tensor_tensor(m_sq, m_h, m_h, ALU.mult))
                dve.tensor_reduce(m_var, m_sq, AX_X, ALU.add).then_inc(l2a_var, 1)
                if not last:
                    scaled(i + 1, 0)
                dve.wait_ge(l2a_rstd, i + 1)
                ended(dve.tensor_tensor(m_h, m_h, bc(m_rstd, NB, -DH32), ALU.mult))
                h4 = m_h.rearrange("p (b h) d -> p b (h d)", b=GB)
                ended(dve.tensor_tensor(h4, h4, m_scale.unsqueeze(1).to_broadcast([128, GB, D]), ALU.mult))
                if not last:
                    scaled(i + 1, 1)
                    end(i + 1)
                update_dve(dve, L2A, i, src=m_h.rearrange("p n d -> p (n d)"))

            gates(0)
            forget(0)
            a(0)
            running_max(0)
            scaled(0, 0)
            scaled(0, 1)
            end(0)
            ended.straight_over()
            over_groups_dve(dve, ended, L2A, 19, body)

        def l2a_pe(pe):
            weights(pe, 4)
            pe.wait_ge(l2a_const, 1)
            pe.wait_ge(onehot_ready, 1)

            def ahead(i):
                turn_pe(pe, L2A, i)
                pe.wait_ge(l2a_kT, i + 1)
                pe.wait_ge(xnT_ready, turned(L2A) + i + 1)
                for b in range(GB):
                    out = bank[3][:, GATES + b * 2 * H4:GATES + (b + 1) * 2 * H4]
                    pe.matmul(out, m_nextT[:, b, :], W("l2_gateT", 0, 2 * H4), start=True, stop=False)
                    mm = pe.matmul(out, m_next_kT[:, b, :], m_wkv, start=False, stop=True)
                mm.then_inc(l2a_gates_psum, 1)

            def recurrence(i):
                pe.wait_ge(l2a_lf, i + 1)
                pe.matmul(bank[3][:, UPTO:UPTO + NB], W("causalT"), m_lf, start=True, stop=True)
                pe.matmul(bank[3][:, BEFORE:BEFORE + NB], W("beforeT"), m_lf, start=True, stop=True).then_inc(l2a_cs_psum, 1)
                pe.wait_ge(l2a_a, i + 1)
                pe.transpose(bank[3][0:NB, AT:AT + S], m_a, W("ident")).then_inc(l2a_aT_psum, 1)
                pe.wait_ge(l2a_M, i + 1)
                pe.matmul(bank[3][:, MT:MT + NB], m_M, W("ident")[0:NB, 0:NB], start=True, stop=True).then_inc(l2a_MT_psum, 1)

            def products(i, h):
                if h >= 2:
                    pe.wait_ge(l2a_c, i * H4 + h - 1)
                pe.matmul(by4(4 + h % 2), identb[:, :], m_future.unsqueeze(1).to_broadcast([128, GB, S]),
                          start=True, stop=False)
                for b in range(GB):
                    mm = pe.matmul(by4(4 + h % 2)[:, b, :], onehot[:, b * H4 + h, :], m_nM, start=False, stop=(b == GB - 1))
                mm.then_inc(l2a_bias_psum, 1)
                rows = slice(h * DH32, (h + 1) * DH32)
                for b in range(GB):
                    mm = pe.matmul(by4(6 + h % 2)[:, b, :], m_kT[rows, b, :], xnT[rows, b, :], start=True, stop=True)
                mm.then_inc(l2a_qk_psum, 1)

            def heads(i, last_turn):
                pe.wait_ge(l2a_nM, i + 1)
                pe.wait_ge(l2a_v, i + 1)
                products(i, 0)
                for h in range(H4):
                    if h + 1 < H4:
                        products(i, h + 1)
                    if h == 2 and not last_turn:
                        ahead(i + 1)
                    pe.wait_ge(l2a_c, i * H4 + h + 1)
                    for b in range(GB):
                        at = (b % 2 * H4 + h) * (DH32 + 1)
                        mm = pe.matmul(bank[1 + b // 2][:, at:at + DH32 + 1], m_c[:, h % 2, b * S:(b + 1) * S],
                                       m_v[:, b * H4 + h, :], start=True, stop=True)
                    mm.then_inc(l2a_hv if h < H4 - 1 else y_ready, 1)

            begun(pe, L2A, 0)
            ahead(0)
            recurrence(0)
            with pe.Fori(0, NG - 1) as i:
                heads(i, False)
                recurrence(i + 1)
            heads(NG - 1, True)

        areas[0] = AHEAD2
        t_q = work(2 * C2, T)
        areas[0] = 0
        t_k = work(C2, T)
        t_v = work(GB * H8, DH64)
        t_sig, t_sel, t_sc = work(GB, H8), work(GB, H8), work(GB, H8)
        t_wide = work(2, GB, 64).rearrange("p k b (e j) -> p k b e j", e=8)
        t_scT = work(GB, S, p=H8)
        t_nmax, t_sum, t_r = work(2, 4), work(2, 4), work(2, 4)
        t_p, t_pT = work(2, C2, S), work(2, C2, S)
        t_oT = work(2, C2, S)
        l2f_zeroed, l2f_gate_psum, l2f_e, l2f_sc, l2f_psum, l2f_by_act, l2f_by_dve, l2f_s_psum, l2f_max, l2f_scT_psum, l2f_scT, \
            l2f_exp, l2f_p, l2f_pT_psum, l2f_pT, l2f_oT_psum, l2f_oT = (
                sem(f"l2f_{n}") for n in "zeroed gate_psum e sc psum by_act by_dve s_psum max scT_psum scT "
                "exp p pT_psum pT oT_psum oT".split())
        NH = 2 * GB

        def l2f_out(n):
            if n < 2 * C2:
                return t_k[:, n // 2, :]
            return t_v[:, (n - 2 * C2) * H8:(n - 2 * C2 + 1) * H8, :]

        def l2f_in(n):
            a = bank[1 + n % 4][:, :]
            return a if n < 2 * C2 else a.rearrange("p (h d) -> p h d", d=DH64)

        def l2f_act(act, ended):
            def projected(i, n):
                act.wait_ge(l2f_psum, i * 12 + n + 1)
                if n < 2 * C2:
                    for half in range(2):
                        rows = slice(DH64 * half, DH64 * (half + 1))
                        last = act.activation(t_q[rows, n + half, :], l2f_in(n)[rows], ACT.Copy, scale=DH64 ** -0.5)
                else:
                    last = act.activation(l2f_out(n), l2f_in(n), ACT.Copy)
                last.then_inc(l2f_by_act, 1)

            def ahead(i):
                turned_act(act, L2F, i)
                act.wait_ge(l2f_gate_psum, i + 1)
                act.activation(t_sig, bank[0][:, 0:GB * H8].rearrange("p (b h) -> p b h", b=GB), ACT.Exp, scale=-1.0)\
                   .then_inc(l2f_e, 1)
                projected(i, 0)
                projected(i, 2)

            def turn(i, last_turn):
                for n in range(4, 2 * C2, 2):
                    projected(i, n)

                def turned_p(m):
                    act.wait_ge(l2f_pT_psum, i * NH + m + 1)
                    act.activation(t_pT[:, m % 2, :, :], by4(1 + m % 2), ACT.Copy).then_inc(l2f_pT, 1)

                for m in range(NH):
                    act.wait_ge(l2f_max, i * NH + m + 1)
                    for c in range(C2):
                        last = act.activation(t_p[:, m % 2, c, :], by4(6 + m % 2)[:, c, :], ACT.Exp,
                                              bias=t_nmax[:, m % 2, c:c + 1], accum_out=t_sum[:, m % 2, c:c + 1])
                    last.then_inc(l2f_exp, 1)
                    if m < 2:
                        projected(i, 2 * C2 + 2 * m)
                    if m:
                        turned_p(m - 1)
                turned_p(NH - 1)
                if not last_turn:
                    ahead(i + 1)

            act.wait_ge(l2f_zeroed, 1)
            ahead(0)
            with act.Fori(0, NG - 1) as i:
                turn(i, False)
            turn(NG - 1, True)

        def l2f_dve(dve, ended):
            weights(dve, 5)

            def projected(i, n):
                dve.wait_ge(l2f_psum, i * 12 + n + 1)
                dve.tensor_copy(l2f_out(n), l2f_in(n)).then_inc(l2f_by_dve, 1)

            def ahead(i):
                dve.wait_ge(l2f_e, i + 1)
                ended(dve.tensor_scalar(t_sig, t_sig, 1.0, None, ALU.add))
                ended(dve.reciprocal(t_sig, t_sig))
                rank_dve(dve, ended, t_sig, t_sel, (t_wide[:, 0], t_wide[:, 1]), TOP2,
                         (lambda: projected(i, 1), lambda: projected(i, 3), nothing))
                dve.tensor_tensor(t_sc, t_sig, t_sel, ALU.mult).then_inc(l2f_sc, 1)

            def body(i, stats, apply):
                last = isinstance(i, int)
                for n in range(5, 2 * C2, 2):
                    projected(i, n)
                stats()

                def normed(m):
                    b, half = divmod(m, 2)
                    dve.wait_ge(l2f_exp, i * NH + m + 1)
                    ended(dve.reciprocal(t_r[:, m % 2, :], t_sum[:, m % 2, :]))
                    ended(dve.tensor_tensor(t_r[:, m % 2, :], t_r[:, m % 2, :], t_sc[:, b, half::2], ALU.mult))
                    dve.tensor_tensor(t_p[:, m % 2, :, :], t_p[:, m % 2, :, :], bc(t_r[:, m % 2, :], C2, -S), ALU.mult)\
                       .then_inc(l2f_p, 1)

                for m in range(NH):
                    dve.wait_ge(l2f_s_psum, i * NH + m + 1)
                    dve.tensor_reduce(t_nmax[:, m % 2, :], by4(6 + m % 2), AX_X, ALU.max, negate=True)\
                       .then_inc(l2f_max, 1)
                    if m == 1:
                        projected(i, 2 * C2 + 1)
                        projected(i, 2 * C2 + 3)
                        dve.wait_ge(l2f_scT_psum, i + 1)
                        dve.tensor_copy(t_scT, by4(0)[0:H8]).then_inc(l2f_scT, 1)
                        dve.wait_ge(l2f_sc, i + 1)
                    if m:
                        normed(m - 1)
                    if m > 1 and m % 2 == 1:
                        l2f_out_dve(dve, i, m // 2 - 1)
                    if m == 6:
                        apply()
                normed(NH - 1)
                l2f_out_dve(dve, i, GB - 1)
                if not last:
                    ahead(i + 1)
                update_dve(dve, L2F, i, 5)

            ahead(0)
            ended.straight_over()
            over_groups_dve(dve, ended, L2F, 27, body)

        def l2f_out_dve(dve, i, b):
            dve.wait_ge(l2f_oT_psum, i * GB + b + 1)
            dve.tensor_copy(t_oT[:, b % 2, :, :], by4(3 + b % 2)).then_inc(l2f_oT, 1)

        def l2f_pe(pe):
            def projection(i, n):
                if n >= 4:
                    pe.wait_ge((l2f_by_act, l2f_by_dve)[n % 2], i * 6 + (n - 4) // 2 + 1)
                if n < 2 * C2:
                    w = W(("l2_Wq", "l2_Wk")[n % 2], n // 2 * 128, 128)
                    last = pe.matmul(bank[1 + n % 4][:, :], w, xnT[:, :, :], start=True, stop=True)
                else:
                    last = pe.matmul(bank[1 + n % 4][:, :], xnT[:, n - 2 * C2, :], W("l2_Wv"), start=True, stop=True)
                last.then_inc(l2f_psum, 1)

            def ahead(i):
                pe.wait_ge(xnT_ready, turned(L2F) + i + 1)
                for b in range(GB):
                    last = pe.matmul(bank[0][:, b * H8:(b + 1) * H8], xnT[:, b, :], W("l2_Ws"), start=True, stop=True)
                last.then_inc(l2f_gate_psum, 1)
                projection(i, 0)
                projection(i, 1)

            def turn(i, last_turn):
                def scores(m):
                    b, half = divmod(m, 2)
                    if m >= 2:
                        pe.wait_ge(l2f_exp, i * NH + m - 1)
                    for c in range(C2):
                        last = pe.matmul(by4(6 + m % 2)[:, c, :], t_q[:, 2 * c + half, b * S:(b + 1) * S],
                                         t_k[:, c, b * S:(b + 1) * S], start=True, stop=True)
                    last.then_inc(l2f_s_psum, 1)

                def turn_p(m):
                    pe.wait_ge(l2f_p, i * NH + m + 1)
                    if m >= 2:
                        pe.wait_ge(l2f_pT, i * NH + m - 1)
                    for c in range(C2):
                        last = pe.transpose(by4(1 + m % 2)[:, c, :], t_p[:, m % 2, c, :], W("ident"))
                    last.then_inc(l2f_pT_psum, 1)

                def weighted(m):
                    b, half = divmod(m, 2)
                    pe.wait_ge(l2f_pT, i * NH + m + 1)
                    if half == 0 and b >= 2:
                        pe.wait_ge(l2f_oT, i * GB + b - 1)
                    for c in range(C2):
                        last = pe.matmul(by4(3 + b % 2)[DH64 * half:DH64 * (half + 1), c, :],
                                         t_v[:, b * H8 + 2 * c + half, :], t_pT[:, m % 2, c, :], start=True, stop=True)
                    if half:
                        last.then_inc(l2f_oT_psum, 1)

                def project(b):
                    pe.wait_ge(l2f_oT, i * GB + b + 1)
                    if b == 0:
                        pe.wait_ge(l2f_scT, i + 1)
                        begun(pe, L2F, i)
                    pe.matmul(by4(5)[:, b, :], t_scT[:, b, :], W("l2_bo"), start=True, stop=False)
                    for c in range(C2):
                        last = pe.matmul(by4(5)[:, b, :], t_oT[:, b % 2, c, :], W("l2_Wo", c * 128, 128),
                                         start=False, stop=(c == C2 - 1))
                    if b == GB - 1:
                        last.then_inc(y_ready, 1)

                for n in range(4, 2 * C2):
                    projection(i, n)
                pe.wait_ge(l2f_by_act, i * 6 + C2)
                pe.wait_ge(l2f_by_dve, i * 6 + C2)
                scores(0)
                scores(1)
                for n in range(2 * C2, 12):
                    projection(i, n)
                pe.wait_ge(l2f_by_act, i * 6 + 6)
                pe.wait_ge(l2f_by_dve, i * 6 + 6)
                pe.wait_ge(l2f_sc, i + 1)
                for b in range(GB):
                    last = pe.transpose(by4(0)[0:H8, b, :], t_sc[:, b, :], W("ident"))
                last.then_inc(l2f_scT_psum, 1)
                for m in range(NH):
                    if m + 2 < NH:
                        scores(m + 2)
                    if m:
                        weighted(m - 1)
                    turn_p(m)
                    if m % 2 == 0 and m > 2:
                        project(m // 2 - 2)
                if not last_turn:
                    turn_pe(pe, L2F, i + 1)
                weighted(NH - 1)
                if not last_turn:
                    ahead(i + 1)
                project(GB - 2)
                if not last_turn:
                    projection(i + 1, 2)
                project(GB - 1)
                if not last_turn:
                    projection(i + 1, 3)

            weights(pe, 5)
            turn_pe(pe, L2F, 0)
            begun(pe, L2F, 0)
            ahead(0)
            projection(0, 2)
            projection(0, 3)
            with pe.Fori(0, NG - 1) as i:
                turn(i, False)
            turn(NG - 1, True)

        areas[0] = AHEAD3
        c_q = work(H16, T)
        c_v = work(GB * H16, PADH)
        assert areas[0] <= AHEAD2
        areas[0] = 0
        c_T, c_k = work(GB, S), work(T)
        c_sq, c_bq = work(H16), work(H16)
        c_nmax, c_sum, c_r = work(2, 4), work(2, 4), work(2, 4)
        c_p, c_pT = work(2, 4, S), work(2, 4, S)
        c_oT = work(2, 4, S)
        c_mask = work(S, dt=BF16)
        l3a_zeroed, l3a_q_act, l3a_w_psum, l3a_const, l3a_ctxT, l3a_q_psum, l3a_q2_psum, l3a_k_psum, l3a_q, l3a_k, l3a_v_psum, l3a_v, l3a_s_psum, \
            l3a_max, l3a_exp, l3a_p, l3a_pT_psum, l3a_pT, l3a_oT_psum, l3a_oT = (
                sem(f"l3a_{n}") for n in "zeroed q_act w_psum const ctxT q_psum q2_psum k_psum q k v_psum v s_psum "
                "max exp p pT_psum pT oT_psum oT".split())

        def l3a_act(act, ended):
            def heads_q(j):
                for h in range(4 * j + 2, 4 * j + 4):
                    last = act.activation(c_q[:, h, :], bank[0][:, :], ACT.Identity, bias=c_bq[:, h:h + 1],
                                          scale=c_sq[:, h:h + 1])
                last.then_inc(l3a_q_act, 1)

            def ctx_ahead(i):
                act.activation(c_T, group4(ctxT, i), ACT.Copy).then_inc(l3a_ctxT, 1)

            def keys(i):
                turned_act(act, L3A, i)
                act.wait_ge(l3a_k_psum, i + 1)
                act.activation(c_k, bank[4][:, :], ACT.Identity, bias=W("l3_bk")).then_inc(l3a_k, 1)

            def queries(i):
                act.wait_ge(l3a_q_psum, i + 1)
                heads_q(0)
                heads_q(1)

            def turn(i, last_turn):
                def turned_p(m):
                    act.wait_ge(l3a_pT_psum, i * NQ + m + 1)
                    act.activation(c_pT[:, m % 2, :, :], by4(6 + m % 2), ACT.Copy).then_inc(l3a_pT, 1)

                for m in range(NQ):
                    act.wait_ge(l3a_max, i * NQ + m + 1)
                    for g in range(4):
                        last = act.activation(c_p[:, m % 2, g, :], by4(4 + m % 2)[:, g, :], ACT.Exp,
                                              bias=c_nmax[:, m % 2, g:g + 1], accum_out=c_sum[:, m % 2, g:g + 1])
                    last.then_inc(l3a_exp, 1)
                    if m < 2:
                        heads_q(2 + m)
                    if m:
                        turned_p(m - 1)
                    if m == NQ - 3 and not last_turn:
                        ctx_ahead(i + 1)
                if not last_turn:
                    keys(i + 1)
                turned_p(NQ - 1)
                if not last_turn:
                    queries(i + 1)

            act.wait_ge(l3a_const, 1)
            ctx_ahead(0)
            keys(0)
            queries(0)
            with act.Fori(0, NG - 1) as i:
                turn(i, False)
            turn(NG - 1, True)

        def l3a_dve(dve, ended):
            weights(dve, 6)
            dve.wait_ge(l3a_w_psum, 1)
            for k, w in ((1, "l3_WqT"), (2, "l3_WkT"), (3, "l3_WvT")):
                n = WHERE[w][2]
                dve.scalar_tensor_tensor(W(w), bank[k][:, 0:n], LORA_SCALE, W(w), ALU.mult, ALU.add)
            dve.wait_ge(l3a_zeroed, 1)
            ended(dve.tensor_scalar(c_sq, W("headrows"), DH8 ** -0.5, None, ALU.mult))
            dve.tensor_scalar(c_bq, c_sq, W("l3_bq"), None, ALU.mult)
            ended.straight_over()
            dve.wait_ge(imask_loaded, 16)
            dve.tensor_scalar(c_mask, imask[:, :], 0.0, -BIG, ALU.is_equal, ALU.mult).then_inc(l3a_const, 1)
            dve.wait_ge(l3a_const, 1)

            def heads_q(j):
                for h in range(4 * j, 4 * j + 2):
                    last = dve.tensor_scalar(c_q[:, h, :], bank[7][:, :], W("l3_bq"), c_sq[:, h:h + 1],
                                             ALU.add, ALU.mult)
                last.then_inc(l3a_q, 1)

            def queries(i):
                dve.wait_ge(l3a_q2_psum, i + 1)
                heads_q(0)
                heads_q(1)

            def body(i, stats, apply):
                def normed(m):
                    dve.wait_ge(l3a_exp, i * NQ + m + 1)
                    ended(dve.reciprocal(c_r[:, m % 2, :], c_sum[:, m % 2, :]))
                    dve.tensor_tensor(c_p[:, m % 2, :, :], c_p[:, m % 2, :, :], bc(c_r[:, m % 2, :], 4, -S), ALU.mult)\
                       .then_inc(l3a_p, 1)

                for m in range(NQ):
                    b, j = divmod(m, 4)
                    dve.wait_ge(l3a_s_psum, i * NQ + m + 1)
                    dve.tensor_reduce(c_nmax[:, m % 2, :], by4(4 + m % 2), AX_X, ALU.max, negate=True)\
                       .then_inc(l3a_max, 1)
                    if m == 0:
                        heads_q(2)
                    if m == 1:
                        heads_q(3)
                        dve.wait_ge(l3a_v_psum, i + 1)
                        dve.tensor_copy(c_v[:, :, 0:DH8], bank[2][:, :].rearrange("p (n d) -> p n d", d=DH8))\
                           .then_inc(l3a_v, 1)
                    if m:
                        normed(m - 1)
                    if j == 2 and b:
                        l3a_out_dve(dve, i, b - 1)
                    if m == 8:
                        stats()
                    if m == 11:
                        apply()
                normed(NQ - 1)
                l3a_out_dve(dve, i, GB - 1)
                if not isinstance(i, int):
                    queries(i + 1)
                update_dve(dve, L3A, i, 1)

            queries(0)
            over_groups_dve(dve, ended, L3A, 19, body)

        def l3a_out_dve(dve, i, b):
            dve.wait_ge(l3a_oT_psum, i * GB + b + 1)
            dve.tensor_copy(c_oT[:, b % 2, :, :], by4(2 + b % 2)).then_inc(l3a_oT, 1)

        def l3a_pe(pe):
            weights(pe, 6)
            begun(pe, L3A, 0)
            pe.matmul(bank[1][:, 0:128], W("l3_Aq"), W("l3_BqT"), start=True, stop=True)
            pe.matmul(bank[2][:, 0:128], W("l3_Ak"), W("l3_BkT"), start=True, stop=True)
            pe.matmul(bank[3][:, 0:128], W("l3_Av"), W("l3_BvT"), start=True, stop=True).then_inc(l3a_w_psum, 1)
            pe.wait_ge(l3a_const, 1)

            def keys(i):
                turn_pe(pe, L3A, i)
                pe.wait_ge(l3a_ctxT, i + 1)
                pe.matmul(bank[4][:, :], W("l3_WkT"), c_T, start=True, stop=True).then_inc(l3a_k_psum, 1)

            def queries(i):
                pe.wait_ge(xnT_ready, turned(L3A) + i + 1)
                pe.matmul(bank[0][:, :], W("l3_WqT"), xnT[:, :, :], start=True, stop=True).then_inc(l3a_q_psum, 1)

            def queries_again(i):
                pe.matmul(bank[7][:, :], W("l3_WqT"), xnT[:, :, :], start=True, stop=True).then_inc(l3a_q2_psum, 1)

            def values(i):
                bias_pe(pe, 2, W("l3_bv"))
                for b in range(GB):
                    last = pe.matmul(by4(2)[:, b, :], c_T[:, b, :], W("l3_WvT"), start=False, stop=(b == GB - 1))
                last.then_inc(l3a_v_psum, 1)

            def turn(i, last_turn):
                def scores(m):
                    b, j = divmod(m, 4)
                    if m >= 2:
                        pe.wait_ge(l3a_exp, i * NQ + m - 1)
                    if b == 0:
                        pe.wait_ge(l3a_q, i * 4 + j + 1)
                        pe.wait_ge(l3a_q_act, i * 4 + j + 1)
                    k = 4 + m % 2
                    pe.matmul(by4(k), identb[:, :], c_mask.unsqueeze(1).to_broadcast([128, 4, S]),
                              start=True, stop=False)
                    for g in range(4):
                        last = pe.matmul(by4(k)[:, g, :], c_q[:, 4 * j + g, b * S:(b + 1) * S], c_k[:, b * S:(b + 1) * S],
                                         start=False, stop=(g == 3))
                    last.then_inc(l3a_s_psum, 1)

                def turn_p(m):
                    pe.wait_ge(l3a_p, i * NQ + m + 1)
                    if m >= 2:
                        pe.wait_ge(l3a_pT, i * NQ + m - 1)
                    for g in range(4):
                        last = pe.transpose(by4(6 + m % 2)[:, g, :], c_p[:, m % 2, g, :], W("ident"))
                    last.then_inc(l3a_pT_psum, 1)

                def weighted(m):
                    b, j = divmod(m, 4)
                    pe.wait_ge(l3a_pT, i * NQ + m + 1)
                    if m == 0:
                        pe.wait_ge(l3a_v, i + 1)
                    if j == 0 and b >= 2:
                        pe.wait_ge(l3a_oT, i * GB + b - 1)
                    for g in range(4):
                        last = pe.matmul(by4(2 + b % 2)[PADH * j:PADH * (j + 1), g, :], c_v[:, b * H16 + 4 * j + g, :],
                                         c_pT[:, m % 2, g, :], start=True, stop=True)
                    if j == 3:
                        last.then_inc(l3a_oT_psum, 1)

                def project(b):
                    pe.wait_ge(l3a_oT, i * GB + b + 1)
                    for g in range(4):
                        last = pe.matmul(by4(1)[:, b, :], c_oT[:, b % 2, g, :], W("l3_WoP", g * 128, 128),
                                         start=False, stop=(b == GB - 1 and g == 3))
                    if b == GB - 1:
                        last.then_inc(y_ready, 1)

                pe.wait_ge(l3a_k, i + 1)
                scores(0)
                scores(1)
                begun(pe, L3A, i)
                bias_pe(pe, 1, W("l3_bo"))
                for m in range(NQ):
                    if m + 2 < NQ:
                        scores(m + 2)
                    turn_p(m)
                    if m == NQ - 2 and not last_turn:
                        keys(i + 1)
                    if m:
                        weighted(m - 1)
                    if m == NQ - 1 and not last_turn:
                        queries(i + 1)
                    if m % 4 == 3 and m > 4:
                        project(m // 4 - 1)
                weighted(NQ - 1)
                if not last_turn:
                    queries_again(i + 1)
                    values(i + 1)
                project(GB - 1)

            keys(0)
            queries(0)
            queries_again(0)
            values(0)
            with pe.Fori(0, NG - 1) as i:
                turn(i, False)
            turn(NG - 1, True)

        areas[0] = 0
        g_h = work(C3, T)
        l3f_sum, l3f_w, l3f_psum, l3f_by_act, l3f_by_dve = (
            sem(f"l3f_{n}") for n in "sum w psum by_act by_dve".split())

        def l3f_weights_pool(pool, ended):
            pool.wait_ge(l3f_sum, 1)
            for k in range(2):
                last = pool.partition_all_reduce(g_sum[:, k, 1:2], g_sum[:, k, 0:1], 128, bass.bass_isa.ReduceOp.add)
            ended(last)
            ended(pool.tensor_scalar(g_sum[:, :, 2], g_sum[:, :, 1], 1.0 / (D * FF3), LN_EPS, ALU.mult, ALU.add))
            ended(pool.tensor_tensor(g_sum[:, :, 3], g_sum[:, :, 2], minus_one[:, :], ALU.pow))
            for k, w in enumerate(("l3_W1T", "l3_W2T")):
                ended(pool.tensor_scalar(W(w), W(w), g_sum[:, k, 3:4], ROUND, ALU.mult, ALU.add))
                ended(pool.tensor_scalar(W(w), W(w), ROUND, -1.0, ALU.subtract, ALU.max))
                pool.tensor_scalar(W(w), W(w), 1.0, None, ALU.min).then_inc(l3f_w, 1)
            ended.straight_over()

        def l2a_pool(pool, ended):
            with pool.Fori(1, NG) as i:
                norm_pool(pool, L2A, i)
            pool.memset(t_q[:, :, :], 0.0).then_inc(l2f_zeroed, 1)

        def l2f_pool(pool, ended):
            norms_pool(pool, L2F)
            pool.memset(c_v[:, :, :], 0.0)
            pool.memset(c_q[:, :, :], 0.0).then_inc(l3a_zeroed, 1)

        def l3f_act(act, ended):
            with act.Fori(0, NG) as i:
                turned_act(act, L3F, i)
                for c in (0, 2):
                    act.wait_ge(l3f_psum, i * C3 + c + 1)
                    act.activation(g_h[:, c, :], bank[1 + c][:, :], ACT.Relu, bias=W("l3_b1", c, 1)).then_inc(l3f_by_act, 1)

        def l3f_dve(dve, ended):
            def body(i, stats, apply):
                for c in (1, 3):
                    dve.wait_ge(l3f_psum, i * C3 + c + 1)
                    dve.tensor_scalar(g_h[:, c, :], bank[1 + c][:, :], W("l3_b1", c, 1), 0.0, ALU.add, ALU.max)\
                       .then_inc(l3f_by_dve, 1)
                stats()
                apply()
                update_dve(dve, L3F, i, 5)
            over_groups_dve(dve, ended, L3F, 3, body)

        def l3f_pe(pe):
            pe.wait_ge(l3f_w, 2)
            turn_pe(pe, L3F, 0)
            begun(pe, L3F, 0)

            def turn(i, last_turn):
                pe.wait_ge(xnT_ready, turned(L3F) + i + 1)
                for c in range(C3):
                    pe.matmul(bank[1 + c][:, :], W("l3_W1T", c * 128, 128), xnT[:, :, :], start=True, stop=True)\
                      .then_inc(l3f_psum, 1)
                begun(pe, L3F, i)
                bias_pe(pe, 5, W("l3_b2"))
                pe.wait_ge(l3f_by_act, i * 2 + 2)
                pe.wait_ge(l3f_by_dve, i * 2 + 2)
                for b in range(GB):
                    if b == GB - 1 and not last_turn:
                        turn_pe(pe, L3F, i + 1)
                    for c in range(C3):
                        last = pe.matmul(by4(5)[:, b, :], g_h[:, c, b * S:(b + 1) * S], W("l3_W2T", c * 128, 128),
                                         start=False, stop=(b == GB - 1 and c == C3 - 1))
                last.then_inc(y_ready, 1)

            with pe.Fori(0, NG - 1) as i:
                turn(i, False)
            turn(NG - 1, True)

        programs = {
            L0A: (l0a_act, l0a_dve, l0a_pe, l0a_pool), L0F: (l0f_act, l0f_dve, l0f_pe, l0f_pool),
            L1A: (l1a_act, l1a_dve, l1a_pe, l1a_pool), L1F: (l1f_act, l1f_dve, l1f_pe, l1f_pool),
            L2A: (l2a_act, l2a_dve, l2a_pe, l2a_pool), L2F: (l2f_act, l2f_dve, l2f_pe, l2f_pool),
            L3A: (l3a_act, l3a_dve, l3a_pe, lambda pool, ended: norms_pool(pool, L3A)),
            L3F: (l3f_act, l3f_dve, l3f_pe, lambda pool, ended: norms_pool(pool, L3F)),
        }

        block = stack.enter_context(nc.Block())

        @block.sync
        def _(sp):
            sp.dma_start(x_all[:, :], x_in).then_inc(x_updated, X0)
            first = 0
            for n, name in enumerate(PARTS):
                _, at, cols = WHERE[name]
                sp.dma_start(pack[:, first:at + cols], pack_in[:, first:at + cols]).then_inc(part_loaded[n], 16)
                first = at + cols
                if n == 0:
                    sp.dma_start(cell, cell_in).then_inc(masks_loaded, 16)
                    sp.dma_start(seqm, seq_in.partition_broadcast(128)).then_inc(masks_loaded, 16)
                    sp.dma_start(ctxT[:, :], ctxT_in).then_inc(ctxT_loaded, 16)
                    sp.dma_start(ctx[:, :], ctx_in).then_inc(ctx_loaded, 16)
                    sp.dma_start(imask[:, :], imask_in).then_inc(imask_loaded, 16)
            sp.wait_ge(x_updated, X0 + NG * layers)
            sp.dma_start(out, x_all[:, :]).then_inc(stored, 16)
            sp.wait_ge(stored, 16)

        @block.gpsimd
        def _(pool):
            ended = Ended(pool, pool_ended)
            pool.memset(minus_one[:, :], -1.0)
            pool.memset(onehot[:, :, :], 0.0).then_inc(onehot_zeroed, 1)
            ended(pool.memset(minus_half[:, :], -0.5))
            ended.straight_over()
            for l in range(layers):
                programs[l][3](pool, ended)

        @block.scalar
        def _(act):
            ended = Ended(act, act_ended)
            weights(act, 0)
            act.activation(tg[:, :], W("gates"), ACT.Tanh).then_inc(gates_ready, 1)
            act.preload_act_table_set("natural_log_exp_and_others")
            for l in range(layers):
                programs[l][0](act, ended)

        @block.vector
        def _(dve):
            ended = Ended(dve, dve_ended)
            weights(dve, 0)
            dve.memset(onesb[:, :], 1.0)
            ended(dve.tensor_copy(identb[:, :], W("ident")))
            ended.straight_over()
            dve.wait_ge(gates_ready, 1)
            begun(dve, 0, 0)
            for l in range(layers):
                programs[l][1](dve, ended)

        @block.tensor
        def _(pe):
            weights(pe, 0)
            pe.wait_ge(dve_ended, 1)
            for l in range(layers):
                programs[l][2](pe)


def packed(a):
    put = {}

    def t(name):
        return np.asarray(a[name], np.float32).T

    def col(v):
        return np.asarray(v, np.float32).reshape(-1, 1)

    def tiles(w):
        w = np.asarray(w, np.float32)
        return w.reshape(-1, 128, w.shape[1]).transpose(1, 0, 2).reshape(128, -1)

    def spread(w):
        w = np.asarray(w, np.float32)
        out = np.zeros(w.shape[:-1] + (4, 4, PADH), np.float32)
        out[..., :DH8] = w.reshape(w.shape[:-1] + (4, 4, DH8)).swapaxes(-3, -2)
        return out.reshape(w.shape[:-1] + (4, 128))

    put["ident"] = np.eye(128)
    put["ones"] = np.ones((128, 128))
    gates = np.stack([np.asarray(a["g_xattn"]), np.asarray(a["g_ffn"])], 1).reshape(1, 8)
    put["gates"] = np.broadcast_to(gates, (128, 8))
    put["l0_WkT"], put["l0_WoT"] = t("L0_xattn_W_k"), t("L0_xattn_W_o")
    put["l0_bk"], put["l0_bo"] = col(a["L0_xattn_b_k"]), np.asarray(a["L0_xattn_b_o"])[None]
    put["l0_gate"], put["l0_up"] = tiles(a["L0_ffn_w_gate"]), tiles(a["L0_ffn_w_up"])
    put["l0_down"] = np.asarray(a["L0_ffn_w_down"])

    pos = np.arange(S, dtype=np.float64)[:, None]
    pair = np.arange(DH8 // 2, dtype=np.float64)
    base = (2 * pair + 0.4 * DH8) / (1.4 * DH8)
    scale = base[None, :] ** (pos / 512.0)
    angle = pos / 10000.0 ** (pair / (DH8 // 2))[None, :]
    gamma = 1.0 - np.exp(np.linspace(math.log(1 / 32), math.log(1 / 512), H16))
    decay = gamma[None, :, None] ** pos[:, :, None]
    sign = np.tile([-1.0, 1.0], DH8 // 2)

    def table(f, scale, decay):
        one = np.repeat(f * scale, 2, axis=1)
        return (one[:, None, :] * decay).reshape(S, D)

    put["cosq"] = table(np.cos(angle), scale, decay)
    put["sinq"] = table(np.sin(angle), scale, decay) * np.tile(sign, H16)
    put["cosk"] = table(np.cos(angle), 1.0 / scale, 1.0 / decay)
    put["sink"] = table(np.sin(angle), 1.0 / scale, 1.0 / decay) * np.tile(sign, H16)
    key, query = np.arange(S)[:, None], np.arange(S)[None, :]
    put["causalT"] = (query >= key).astype(np.float32)
    put["futureT"] = np.where(query >= key, 0.0, -BIG)

    put["l1_dw"] = np.asarray(a["L1_ffn_dw_kernel"]).reshape(128, 3)
    put["l1_dwb"], put["l1_pwb"] = col(a["L1_ffn_dw_bias"]), col(a["L1_ffn_pw_b"])
    put["l1_pwT"], put["l1_routerT"] = t("L1_ffn_pw_w"), t("L1_ffn_router_w")
    put["l1_routerb"] = np.broadcast_to(np.asarray(a["L1_ffn_router_b"])[None], (128, E1))
    put["l1_expertT"] = np.asarray(a["L1_ffn_expert_w"]).transpose(2, 0, 1).reshape(128, -1)
    put["l1_expertb"] = np.asarray(a["L1_ffn_expert_b"]).reshape(1, -1)
    put["l1_outT"], put["l1_outb"] = t("L1_ffn_out_w"), col(a["L1_ffn_out_b"])
    put["l1_norm"] = col(a["L1_ffn_norm_w"])
    put["l1_downT"], put["l1_downb"] = t("L1_ffn_ff_down_w"), col(a["L1_ffn_ff_down_b"])
    put["l1_upT"], put["l1_upb"] = t("L1_ffn_ff_up_w"), col(a["L1_ffn_ff_up_b"])
    e, j = np.arange(8)[:, None], np.arange(8)[None, :]
    put["before"] = np.broadcast_to((j < e).astype(np.float32).reshape(1, 64), (128, 64))

    gate_w = np.stack([np.asarray(a["L2_xattn_igate_w"]), np.asarray(a["L2_xattn_fgate_w"])])
    put["l2_gateT"] = gate_w.reshape(2 * H4, 3, 128).transpose(2, 1, 0).reshape(128, -1)
    gate_b = np.concatenate([np.asarray(a["L2_xattn_igate_b"]), np.asarray(a["L2_xattn_fgate_b"])])
    put["l2_gateb"] = np.broadcast_to(gate_b[None], (128, 2 * H4))
    put["beforeT"] = (query > key).astype(np.float32)
    put["l2_outw"] = np.broadcast_to(np.asarray(a["L2_xattn_out_w"])[None], (128, 128))
    kv = np.asarray(a["L2_ffn_Wkv"])
    put["l2_Wq"], put["l2_Wk"], put["l2_Wv"] = np.asarray(a["L2_ffn_Wq"]), kv[:, :512], kv[:, 512:]
    put["l2_Ws"], put["l2_bo"] = np.asarray(a["L2_ffn_Ws"]), np.asarray(a["L2_ffn_bo"])
    put["l2_Wo"] = tiles(np.asarray(a["L2_ffn_Wo"]).reshape(512, 128))

    put["l3_WqT"], put["l3_WkT"] = t("L3_xattn_Wq"), t("L3_xattn_Wk")
    put["headrows"] = np.repeat(np.eye(H16), DH8, 0)
    put["l3_WvT"] = t("L3_xattn_Wv")
    put["l3_WoP"] = spread(np.asarray(a["L3_xattn_Wo"])).transpose(2, 1, 0).reshape(128, -1)
    for n in "qkv":
        put[f"l3_A{n}"] = np.asarray(a[f"L3_xattn_A{n}"])
    put["l3_BqT"], put["l3_BkT"] = t("L3_xattn_Bq"), t("L3_xattn_Bk")
    put["l3_BvT"] = t("L3_xattn_Bv")
    put["l3_bq"], put["l3_bk"] = col(a["L3_xattn_bq"]), col(a["L3_xattn_bk"])
    put["l3_bv"], put["l3_bo"] = np.asarray(a["L3_xattn_bv"])[None], np.asarray(a["L3_xattn_bo"])[None]
    put["l3_W1T"], put["l3_b1"] = t("L3_ffn_W1"), np.asarray(a["L3_ffn_b1"]).reshape(C3, 128).T
    put["l3_W2T"], put["l3_b2"] = tiles(t("L3_ffn_W2")), np.asarray(a["L3_ffn_b2"])[None]

    out = np.zeros((128, COLS), np.float32)
    for name, p, n in pieces():
        _, at, _ = WHERE[name]
        out[:p, at:at + n] = put[name]
    return out


def kernel(**inputs):
    import concourse.bacc as bacc
    from concourse.bass_utils import run_bass_kernel_spmd

    a = {k: np.asarray(v) for k, v in inputs.items()}

    def tokens(v):
        return np.ascontiguousarray(v.transpose(1, 0, 2).reshape(128, -1))

    imask = a["mask_1x1xSxS2_if1"].reshape(S, S)
    arrays = {
        "x": tokens(a["x"]), "ctx": tokens(a["ctx_1024"]),
        "ctxT": np.ascontiguousarray(a["ctx_1024"].transpose(2, 0, 1).reshape(128, -1)),
        "cell": tokens(a["mask_BxSxS2_ff1"]), "seq": np.ascontiguousarray(a["mask_BxS2_ff1"].reshape(-1)),
        "imask": np.ascontiguousarray(imask),
        "pack": packed(a),
    }
    nc = bacc.Bacc("TRN2", target_bir_lowering=False, num_devices=1)
    aps = [nc.dram_tensor(f"in_{n}", v.shape, mybir.dt.from_np(v.dtype), kind="ExternalInput").ap()
           for n, v in arrays.items()]
    out = nc.dram_tensor("out", (128, B * D), F32, kind="ExternalOutput").ap()
    build(nc, *aps, out)
    r = run_bass_kernel_spmd(nc, [{f"in_{n}": v for n, v in arrays.items()}], core_ids=[0])
    got = r.results[0]["out"]
    return got.reshape(S, B, D).transpose(1, 0, 2)
```
